# Optimizing a Trainium2 kernel written in Bass

```python
import numpy as np
import jax
import jax.numpy as jnp

def _softmax(x, axis=-1):
    return jax.nn.softmax(x, axis=axis)

def _gelu(x):
    return jax.nn.gelu(x, approximate=True)

def _silu(x):
    return jax.nn.silu(x)

def _sigmoid(x):
    return jax.nn.sigmoid(x)

def _layernorm(x, axis=-1, eps=1e-05):
    m = jnp.mean(x, axis=axis, keepdims=True)
    v = jnp.var(x, axis=axis, keepdims=True)
    return (x - m) / jnp.sqrt(v + eps)

def _scatter_add(tgt, idx, src, axis=0):
    return tgt.at[idx].add(src)

def _segment_sum(src, seg, n):
    return jax.ops.segment_sum(src, seg, n)
kernel_name = 'mk_seq_preln_d1_jaxref_r4_40e712'

def setup_inputs(seed: int=0):
    np.random.seed(seed)
    _w = jnp.asarray

    def _L0_attn_setup():
        import jax, jax.numpy as jnp
        import numpy as np
        B, N, D, F = (4, 1024, 256, 64)
        LN_EPS = 1e-05
        ATTN_EPS = 1e-06

        def _layer_norm(x, w, b):
            mu = jnp.mean(x, axis=-1, keepdims=True)
            var = jnp.var(x, axis=-1, keepdims=True)
            return (x - mu) * jax.lax.rsqrt(var + LN_EPS) * w + b

        def _linear(x, w, b):
            return jnp.einsum('bnd,fd->bnf', x, w) + b

        def _causal_linear_attn(Q, K, V, eps=ATTN_EPS):
            b, n, f = K.shape
            d = V.shape[-1]
            Qt = jnp.swapaxes(Q, 0, 1)
            Kt = jnp.swapaxes(K, 0, 1)
            Vt = jnp.swapaxes(V, 0, 1)

            def step(carry, qkv):
                KV, Ks = carry
                q, k, v = qkv
                KV = KV + k[:, :, None] * v[:, None, :]
                Ks = Ks + k
                num = jnp.einsum('bf,bfd->bd', q, KV)
                den = jnp.sum(q * Ks, axis=-1, keepdims=True) + eps
                return ((KV, Ks), num / den)
            init = (jnp.zeros((b, f, d), Q.dtype), jnp.zeros((b, f), Q.dtype))
            _, out = jax.lax.scan(step, init, (Qt, Kt, Vt))
            return jnp.swapaxes(out, 0, 1)
        key = jax.random.key(seed)
        ks = jax.random.split(key, 9)
        s = 0.02
        return {'x': jax.random.normal(ks[0], (B, N, D), dtype=jnp.float32), 'ln1_w': jnp.ones((D,), jnp.float32), 'ln1_b': jnp.zeros((D,), jnp.float32), 'q_w': jax.random.normal(ks[1], (F, D), jnp.float32) * s, 'q_b': jnp.zeros((F,), jnp.float32), 'k_w': jax.random.normal(ks[2], (F, D), jnp.float32) * s, 'k_b': jnp.zeros((F,), jnp.float32), 'v_w': jax.random.normal(ks[3], (D, D), jnp.float32) * s, 'v_b': jnp.zeros((D,), jnp.float32), 'o_w': jax.random.normal(ks[4], (D, D), jnp.float32) * s, 'o_b': jnp.zeros((D,), jnp.float32), 'ln2_w': jnp.ones((D,), jnp.float32), 'ln2_b': jnp.zeros((D,), jnp.float32), 'f1_w': jax.random.normal(ks[5], (4 * D, D), jnp.float32) * s, 'f1_b': jnp.zeros((4 * D,), jnp.float32), 'f2_w': jax.random.normal(ks[6], (D, 4 * D), jnp.float32) * s, 'f2_b': jnp.zeros((D,), jnp.float32)}
    _L0_attn_in = _L0_attn_setup()

    def _L0_ffn_setup():
        import jax, jax.numpy as jnp
        import numpy as np
        EPS = 1e-06
        LN_EPS = 1e-05

        def _absmean_core(W):
            gamma = jnp.mean(jnp.abs(W)) + EPS
            Ws = W / gamma
            Wq = jnp.sign(Ws) * jnp.minimum(jnp.round(jnp.abs(Ws)), 1.0)
            return (Wq, gamma)

        @jax.custom_vjp
        def absmean(W):
            return _absmean_core(W)[0]

        def _absmean_fwd(W):
            Wq, gamma = _absmean_core(W)
            return (Wq, gamma)

        def _absmean_bwd(gamma, g):
            return (g / gamma,)
        absmean.defvjp(_absmean_fwd, _absmean_bwd)

        def layernorm(x, w, b, eps=LN_EPS):
            mu = jnp.mean(x, axis=-1, keepdims=True)
            var = jnp.mean((x - mu) ** 2, axis=-1, keepdims=True)
            return (x - mu) * jax.lax.rsqrt(var + eps) * w + b
        key = jax.random.key(seed)
        k1, k2, k3 = jax.random.split(key, 3)
        d, h = (256, 1024)
        B, T = (8, 512)
        return {'x': jax.random.normal(k1, (B, T, d), jnp.float32), 'W_fc': jax.random.normal(k2, (h, d), jnp.float32), 'ln_w': jnp.ones((h,), jnp.float32), 'ln_b': jnp.zeros((h,), jnp.float32), 'W_proj': jax.random.normal(k3, (d, h), jnp.float32)}
    _L0_ffn_in = _L0_ffn_setup()
    _d = {'L0_attn_x': _L0_attn_in['x'], 'L0_attn_ln1_w': _L0_attn_in['ln1_w'], 'L0_attn_ln1_b': _L0_attn_in['ln1_b'], 'L0_attn_q_w': _L0_attn_in['q_w'], 'L0_attn_q_b': _L0_attn_in['q_b'], 'L0_attn_k_w': _L0_attn_in['k_w'], 'L0_attn_k_b': _L0_attn_in['k_b'], 'L0_attn_v_w': _L0_attn_in['v_w'], 'L0_attn_v_b': _L0_attn_in['v_b'], 'L0_attn_o_w': _L0_attn_in['o_w'], 'L0_attn_o_b': _L0_attn_in['o_b'], 'L0_attn_ln2_w': _L0_attn_in['ln2_w'], 'L0_attn_ln2_b': _L0_attn_in['ln2_b'], 'L0_attn_f1_w': _L0_attn_in['f1_w'], 'L0_attn_f1_b': _L0_attn_in['f1_b'], 'L0_attn_f2_w': _L0_attn_in['f2_w'], 'L0_attn_f2_b': _L0_attn_in['f2_b'], 'L0_ffn_W_fc': _L0_ffn_in['W_fc'], 'L0_ffn_ln_w': _L0_ffn_in['ln_w'], 'L0_ffn_ln_b': _L0_ffn_in['ln_b'], 'L0_ffn_W_proj': _L0_ffn_in['W_proj']}
    _x0 = _d['L0_attn_x']
    _d['L0_attn_x'] = jax.random.normal(jax.random.fold_in(jax.random.key(seed), 1), (8, 512, 256), dtype=_x0.dtype)
    del _x0
    return _d

def reference(L0_attn_x, L0_attn_ln1_w, L0_attn_ln1_b, L0_attn_q_w, L0_attn_q_b, L0_attn_k_w, L0_attn_k_b, L0_attn_v_w, L0_attn_v_b, L0_attn_o_w, L0_attn_o_b, L0_attn_ln2_w, L0_attn_ln2_b, L0_attn_f1_w, L0_attn_f1_b, L0_attn_f2_w, L0_attn_f2_b, L0_ffn_W_fc, L0_ffn_ln_w, L0_ffn_ln_b, L0_ffn_W_proj):

    def _L0_attn_ref(x, ln1_w, ln1_b, q_w, q_b, k_w, k_b, v_w, v_b, o_w, o_b, ln2_w, ln2_b, f1_w, f1_b, f2_w, f2_b):
        import jax, jax.numpy as jnp
        import numpy as np
        B, N, D, F = (4, 1024, 256, 64)
        LN_EPS = 1e-05
        ATTN_EPS = 1e-06

        def _layer_norm(x, w, b):
            mu = jnp.mean(x, axis=-1, keepdims=True)
            var = jnp.var(x, axis=-1, keepdims=True)
            return (x - mu) * jax.lax.rsqrt(var + LN_EPS) * w + b

        def _linear(x, w, b):
            return jnp.einsum('bnd,fd->bnf', x, w) + b

        def _causal_linear_attn(Q, K, V, eps=ATTN_EPS):
            b, n, f = K.shape
            d = V.shape[-1]
            Qt = jnp.swapaxes(Q, 0, 1)
            Kt = jnp.swapaxes(K, 0, 1)
            Vt = jnp.swapaxes(V, 0, 1)

            def step(carry, qkv):
                KV, Ks = carry
                q, k, v = qkv
                KV = KV + k[:, :, None] * v[:, None, :]
                Ks = Ks + k
                num = jnp.einsum('bf,bfd->bd', q, KV)
                den = jnp.sum(q * Ks, axis=-1, keepdims=True) + eps
                return ((KV, Ks), num / den)
            init = (jnp.zeros((b, f, d), Q.dtype), jnp.zeros((b, f), Q.dtype))
            _, out = jax.lax.scan(step, init, (Qt, Kt, Vt))
            return jnp.swapaxes(out, 0, 1)
        x_norm = _layer_norm(x, ln1_w, ln1_b)
        Q = jax.nn.elu(_linear(x_norm, q_w, q_b)) + 1.0
        K = jax.nn.elu(_linear(x_norm, k_w, k_b)) + 1.0
        V = _linear(x_norm, v_w, v_b)
        attn = _causal_linear_attn(Q, K, V)
        attn = _linear(attn, o_w, o_b)
        x = x + attn
        h = _layer_norm(x, ln2_w, ln2_b)
        h = jax.nn.gelu(_linear(h, f1_w, f1_b), approximate=False)
        x = x + _linear(h, f2_w, f2_b)
        return x

    def _L0_ffn_ref(x, W_fc, ln_w, ln_b, W_proj):
        import jax, jax.numpy as jnp
        import numpy as np
        EPS = 1e-06
        LN_EPS = 1e-05

        def _absmean_core(W):
            gamma = jnp.mean(jnp.abs(W)) + EPS
            Ws = W / gamma
            Wq = jnp.sign(Ws) * jnp.minimum(jnp.round(jnp.abs(Ws)), 1.0)
            return (Wq, gamma)

        @jax.custom_vjp
        def absmean(W):
            return _absmean_core(W)[0]

        def _absmean_fwd(W):
            Wq, gamma = _absmean_core(W)
            return (Wq, gamma)

        def _absmean_bwd(gamma, g):
            return (g / gamma,)
        absmean.defvjp(_absmean_fwd, _absmean_bwd)

        def layernorm(x, w, b, eps=LN_EPS):
            mu = jnp.mean(x, axis=-1, keepdims=True)
            var = jnp.mean((x - mu) ** 2, axis=-1, keepdims=True)
            return (x - mu) * jax.lax.rsqrt(var + eps) * w + b
        h = jnp.einsum('btd,hd->bth', x, absmean(W_fc))
        h = jax.nn.gelu(h, approximate=False)
        h = layernorm(h, ln_w, ln_b)
        return jnp.einsum('bth,dh->btd', h, absmean(W_proj))
    x = L0_attn_x
    x = x + _L0_attn_ref(_layernorm(x, axis=-1), L0_attn_ln1_w, L0_attn_ln1_b, L0_attn_q_w, L0_attn_q_b, L0_attn_k_w, L0_attn_k_b, L0_attn_v_w, L0_attn_v_b, L0_attn_o_w, L0_attn_o_b, L0_attn_ln2_w, L0_attn_ln2_b, L0_attn_f1_w, L0_attn_f1_b, L0_attn_f2_w, L0_attn_f2_b)
    x = x + _L0_ffn_ref(_layernorm(x, axis=-1), L0_ffn_W_fc, L0_ffn_ln_w, L0_ffn_ln_b, L0_ffn_W_proj)
    return x

_drawn_inputs = setup_inputs


def setup_inputs(seed=0):
    import zlib

    import numpy as np

    out = dict(_drawn_inputs(seed))
    spreads = {'L0_attn_ln1_w': (1.0, 0.6),
     'L0_attn_ln1_b': (0.0, 0.8),
     'L0_attn_q_b': (0.0, 0.8),
     'L0_attn_k_b': (0.0, 0.8),
     'L0_attn_v_b': (0.0, 0.478),
     'L0_attn_o_b': (0.0, 0.1),
     'L0_attn_ln2_w': (1.0, 0.6),
     'L0_attn_ln2_b': (0.0, 0.8),
     'L0_attn_f1_b': (0.0, 0.382),
     'L0_attn_f2_b': (0.0, 0.1),
     'L0_ffn_ln_w': (1.0, 0.2),
     'L0_ffn_ln_b': (0.0, 0.1)}
    factors = {'L0_attn_q_w': 8.0, 'L0_attn_k_w': 8.0, 'L0_attn_v_w': 6.111, 'L0_attn_o_w': 3.217}
    for name, (base, spread) in spreads.items():
        noise = np.random.default_rng([zlib.crc32(name.encode()), seed]).standard_normal(out[name].shape)
        drawn = base * np.exp(spread * noise) if base else spread * noise
        out[name] = jnp.asarray(drawn.astype(out[name].dtype))
    for name, factor in factors.items():
        out[name] = (out[name] * factor).astype(out[name].dtype)
    return out
```

```python
from contextlib import ExitStack

import concourse.bass as bass
from concourse import mybir

F32 = mybir.dt.float32
F32R = mybir.dt.float32r
ALU = mybir.AluOpType
ACT = mybir.ActivationFunctionType
AXX = mybir.AxisListType.X

P = 128
LN_EPS = 1e-5
ATTN_EPS = 1e-6
ABSMEAN_EPS = 1e-6


def later(g, n):
    return not isinstance(g, int) or g >= n


def build(nc, x, ln1_w, ln1_b, q_w, q_b, k_w, k_b, v_w, v_b, o_w, o_b, ln2_w, ln2_b, f1_w, f1_b,
          f2_w, f2_b, fc_w, ln3_w, ln3_b, pj_w, out):
    G, N, D = x.shape
    FQ = q_w.shape[0]
    H = f1_w.shape[0]
    T = N // P
    KD = D // P
    KH = H // P
    VW = D + 2
    assert (T, KD, KH, 2 * FQ) == (4, 2, 8, P) and H == fc_w.shape[0]

    x_flat = x.rearrange("g n d -> (g n d)")
    out_flat = out.rearrange("g n d -> (g n d)")

    def group_rows(flat, offset):
        return flat[bass.ds(offset, N * D)].rearrange("(t p d) -> p t d", t=T, p=P)

    with ExitStack() as ctx:
        def sb(name, shape, dt=F32):
            return ctx.enter_context(nc.sbuf_tensor(name, shape, dt))

        def sem(name):
            return ctx.enter_context(nc.semaphore(name))

        bank = {n: ctx.enter_context(nc.psum_tensor("bank_" + n, [P, 512], F32))
                for n in ("f0", "f1", "y0", "y1", "p0", "p1", "x", "c")}

        wqk = [sb("wqk_hi", [P, KD, P], F32R), sb("wqk_lo", [P, KD, P], F32R)]
        wvo = [sb("wvo_hi", [P, KD, D], F32R), sb("wvo_lo", [P, KD, D], F32R)]
        wf1 = [sb("wf1_hi", [P, KD, H], F32R), sb("wf1_lo", [P, KD, H], F32R)]
        wf2 = [sb("wf2_hi", [P, KH, D], F32R), sb("wf2_lo", [P, KH, D], F32R)]
        wfc = sb("wfc_t", [P, KD, H], F32R)
        wpj = sb("wpj_t", [P, KH, D], F32R)

        ident = sb("ident", [P, P])
        mean_w = sb("mean_w", [P, P])
        mask = sb("mask", [P, P])
        neg_half = sb("neg_half", [P, 8])
        vec = sb("vec", [P, 31])
        f1b_c, ln3w_c, ln3b_c = vec[:, 0:8], vec[:, 8:16], vec[:, 16:24]
        ln1w_c, ln2w_c, vb_c, qkb_c = vec[:, 24:26], vec[:, 26:28], vec[:, 28:30], vec[:, 30:31]
        dots = sb("dots", [P, 11])
        f1_bias = sb("f1_bias", [P, KH])
        vb_full = sb("vb_full", [P, KD])
        qk_bias = sb("qk_bias", [P, 1])
        abs_sum = sb("abs_sum", [P, 8])
        abs_tot = sb("abs_tot", [P, 2])
        theta = sb("theta", [P, 4])
        bvo_b = sb("bvo_b", [P, D])
        ob_b = sb("ob_b", [P, D])
        f2b_b = sb("f2b_b", [P, D])
        cpj_b = sb("cpj_b", [P, D])

        x_sb = sb("x_sb", [P, T, D])
        u = sb("u", [P, T, D])
        xa = sb("xa", [P, T, D])
        xpb = sb("xpb", [P, T, D])
        xs = sb("xs", [P, T, D])
        z = sb("z", [P, T, D])
        y_yc = sb("y_yc", [P, 2, T, D])
        y, yc = y_yc[:, 0], y_yc[:, 1]
        uT = [sb("uT_hi", [P, KD, N], F32R), sb("uT_lo", [P, KD, N], F32R)]
        z2T = [sb("z2T_hi", [P, KD, N], F32R), sb("z2T_lo", [P, KD, N], F32R)]
        z3T = [sb("z3T_hi", [P, KD, N], F32R), sb("z3T_lo", [P, KD, N], F32R)]
        qk_exp = sb("qk_exp", [P, N])
        qk = sb("qk", [P, N])
        qkh = [sb("qk_hi", [P, N], F32R), sb("qk_lo", [P, N], F32R)]
        kk = [sb("kk_hi", [FQ, N], F32R), sb("kk_lo", [FQ, N], F32R)]
        v32 = sb("v32", [P, 2, D])
        v = [sb("v_hi", [P, T, VW], F32R), sb("v_lo", [P, T, VW], F32R)]
        a = [sb("a_hi", [P, T, N], F32R), sb("a_lo", [P, T, N], F32R)]
        hring = sb("hring", [P, 3, N])
        hr = [sb("h_hi", [P, 3, N], F32R), sb("h_lo", [P, 3, N], F32R)]
        h3 = sb("h3", [P, KH, N])
        sums = sb("sums", [P, 4, N])
        sq, hsum, sqsum = sums[:, 0:2], sums[:, 2], sums[:, 3]
        gr = [sb("g_hi", [P, 2, N], F32R), sb("g_lo", [P, 2, N], F32R)]
        mu = sb("mu", [P, N])
        bn = [sb(f"bn{n}", [P, T, 6]) for n in range(3)]
        mv = [sb(f"mv{n}", [P, T, 2]) for n in range(3)]
        ve = [sb(f"ve{n}", [P, 2, T]) for n in range(4)]
        rs = [sb(f"rs{n}", [P, 2, T]) for n in range(4)]
        fence = sb("fence", [P, 1])
        den = sb("den", [P, T])
        rden = sb("rden", [P, T])

        qk_raw = hring[:, 0, 0:D]
        wv_raw = hring[:, 1, :].rearrange("p (k d) -> p k d", k=KD)
        wo_raw = hring[:, 2, :].rearrange("p (k d) -> p k d", k=KD)
        woT = v32
        vec_rows = z[0:31, 0, 0:P]
        f1_raw = y_yc[:, :].rearrange("p a t d -> p (a t) d")
        f2_raw = sums[:, :].rearrange("p a n -> p (a n)").rearrange("p (k h) -> p k h", k=KD)
        fc_raw = h3[:, 0:4, :].rearrange("p a n -> p (a n)").rearrange("p (m d) -> p m d", m=KH)
        pj_raw = h3[:, 4:8, :].rearrange("p a n -> p (a n)").rearrange("p (k h) -> p k h", k=KD)
        tern_low = y_yc[:].rearrange("p a t d -> p (a t d)")
        ln1b_b, ln2b_b, dot_out = xs[:, 0, :], xs[:, 1, :], xs[:, 2, :]
        vb_wide = xs[:, 3, :].rearrange("p (k m) -> p k m", k=KD)
        ln3b_wide = mu[:, 0:P]
        abs_out = mu

        names = """x_loaded rows_loaded bcast_loaded qk_raw_loaded v_raw_loaded f1_raw_loaded f2_raw_loaded
            fc_raw_loaded pj_raw_loaded consts_memset consts_ready vec_t vec_ready
            dots_done bias_done vb_wide_ready qkT_done wqk_hi_ready wqk_ready woT_done woT_ready wvo_done
            wvo_hi_ready wvo_ready bvo_done bvo_ready f1T_done wf1_hi_ready wf1_ready f2T_done wf2_hi_ready
            wf2_ready abs_summed abs_tot_done theta_ready fc_low fc_tern pj_low pj_tern fcT_done wfc_ready pjT_done
            wpj_ready lnb_wide_ready cpj_done cpj_ready v_ones_ready
            ln1_bn ln1_mv ln1_ve ln1_rs u_ready tu_done u_hi u_lo qk_done qk_minmax qk_exp_ready qk_ready
            qk_hi_ready qk_lo_ready kk_ready v_done v_ready v_hi_ready v_lo_ready s_done a_hi_diag a_hi_off
            a_lo_ready a_lo_masked av_done den_ready rden_ready n1_ready n1o_ready xa_ready
            ln2_bn ln2_mv ln2_ve ln2_rs z2_ready tz2_done z2_hi z2_lo xpb_ready xs_ready
            f1_done h_gelu h_hi_ready h_lo_ready f2_step y_ready
            ln3_bn ln3_mv ln3_ve ln3_rs z3_ready tz3_done z3_hi z3_lo
            fc_done h3_gelu hsum_step mu_done mu_ready d_ready sq_ready sqsum_step g_hi_ready g_lo_ready
            pj_step var_done var_ready rs3_ready yc_ready out_ready out_stored fence_done""".split()
        s = {n: sem(n) for n in names}

        block = ctx.enter_context(nc.Block())

        def steps(engine, body):
            for i in range(-1, 3):
                body(i)
            with engine.Fori(3, G - 2) as i:
                body(i)
            for i in range(G - 2, G + 2):
                body(i)

        def groups(i):
            g = [i + 1, i, i - 1, i - 2]
            if not isinstance(i, int):
                return g
            return [n if 0 <= n < G else None for n in g]

        def has_next(i):
            return not isinstance(i, int) or i + 2 < G

        @block.sync
        def _(sp):
            sp.dma_start(x_sb[:], group_rows(x_flat, 0)).then_inc(s["x_loaded"], 16)
            sp.dma_start(qk_raw[0:FQ, :], q_w).then_inc(s["qk_raw_loaded"], 16)
            sp.dma_start(qk_raw[FQ:P, :], k_w).then_inc(s["qk_raw_loaded"], 16)
            rows = [(f1_b, 0), (ln3_w, 8), (ln3_b, 16), (ln1_w, 24), (ln2_w, 26), (v_b, 28)]
            for src, r in rows:
                n = src.shape[0] // P
                sp.dma_start(vec_rows[r:r + n, :], src.rearrange("(r p) -> r p", p=P)).then_inc(s["rows_loaded"], 16)
            sp.dma_start(vec_rows[30:31, 0:FQ], q_b.rearrange("(r p) -> r p", r=1)).then_inc(s["rows_loaded"], 16)
            sp.dma_start(vec_rows[30:31, FQ:P], k_b.rearrange("(r p) -> r p", r=1)).then_inc(s["rows_loaded"], 16)
            sp.dma_start(wv_raw, v_w.rearrange("(k p) d -> p k d", p=P)).then_inc(s["v_raw_loaded"], 16)
            sp.dma_start(wo_raw, o_w.rearrange("(k p) d -> p k d", p=P)).then_inc(s["v_raw_loaded"], 16)
            for dst, src in ((ln1b_b, ln1_b), (ln2b_b, ln2_b), (ob_b[:], o_b), (f2b_b[:], f2_b)):
                sp.dma_start(dst, src.rearrange("(r d) -> r d", r=1).to_broadcast([P, D])).then_inc(s["bcast_loaded"], 16)
            sp.dma_start(f1_raw, f1_w.rearrange("(m p) d -> p m d", p=P)).then_inc(s["f1_raw_loaded"], 16)
            sp.dma_start(f2_raw, f2_w.rearrange("(k p) h -> p k h", p=P)).then_inc(s["f2_raw_loaded"], 16)
            sp.dma_start(fc_raw, fc_w.rearrange("(m p) d -> p m d", p=P)).then_inc(s["fc_raw_loaded"], 16)
            sp.dma_start(pj_raw, pj_w.rearrange("(k p) h -> p k h", p=P)).then_inc(s["pj_raw_loaded"], 16)

            def load_x(g):
                offset = sp.snap(g * (N * D)) if not isinstance(g, int) else g * N * D
                if not isinstance(g, int):
                    n1_count, xpb_count = sp.snap(4 * g), sp.snap(g + 0)
                sp.wait_ge(s["n1_ready"], 4 * g if isinstance(g, int) else n1_count)
                sp.wait_ge(s["xpb_ready"], g if isinstance(g, int) else xpb_count)
                sp.dma_start(x_sb[:], group_rows(x_flat, offset)).then_inc(s["x_loaded"], 16)

            def store(g):
                offset = sp.snap(g * (N * D)) if not isinstance(g, int) else g * N * D
                sp.wait_ge(s["out_ready"], 4 * g + 4)
                sp.dma_start(group_rows(out_flat, offset), yc).then_inc(s["out_stored"], 16)

            def body(i):
                at, ml, fc, pj = groups(i)
                if has_next(i):
                    load_x(i + 2)
                if pj is not None:
                    store(pj)

            steps(sp, body)
            sp.wait_ge(s["out_stored"], 16 * G)

        @block.tensor
        def _(pe):
            def split3(ps, w, r, start, stop, skip=False):
                pe.matmul(ps, w[0], r[0], start=start, stop=False, skip_group_check=skip)
                pe.matmul(ps, w[0], r[1], start=False, stop=False, skip_group_check=skip)
                return pe.matmul(ps, w[1], r[0], start=False, stop=stop, skip_group_check=skip)

            def flip(src, banks, k):
                for t in range(T):
                    mm = pe.transpose(banks[:, t * P:(t + 1) * P], src[:, t, k * P:(k + 1) * P], ident[:])
                return mm

            def prep_small():
                pe.wait_ge(s["consts_ready"], 3)
                pe.wait_ge(s["rows_loaded"], 16 * 8)
                pe.transpose(bank["p0"][:, 0:31], vec_rows, ident[0:31, 0:31]).then_inc(s["vec_t"], 1)
                pe.wait_ge(s["qk_raw_loaded"], 32)
                for k in range(KD):
                    mm = pe.transpose(bank["p1"][:, k * P:(k + 1) * P], qk_raw[:, k * P:(k + 1) * P], ident[:])
                mm.then_inc(s["qkT_done"], 1)
                pe.wait_ge(s["v_raw_loaded"], 32)
                for k in range(KD):
                    for e in range(KD):
                        mm = pe.transpose(bank["y0"][:, k * D + e * P:k * D + (e + 1) * P],
                                          wo_raw[:, e, k * P:(k + 1) * P], ident[:])
                mm.then_inc(s["woT_done"], 1)

            def prep_vo():
                pe.wait_ge(s["woT_ready"], 1)
                for c in range(KD):
                    for k in range(KD):
                        mm = pe.matmul(bank["y1"][:, c * D:(c + 1) * D], wv_raw[:, k, c * P:(c + 1) * P],
                                       woT[:, k, :], start=(k == 0), stop=(k == KD - 1))
                mm.then_inc(s["wvo_done"], 1)
                pe.wait_ge(s["vb_wide_ready"], KD)
                pe.wait_ge(s["vec_ready"], 1)
                for k in range(KD):
                    mm = pe.matmul(bank["p0"][:, 0:D], vb_wide[:, k, :], woT[:, k, :],
                                   start=(k == 0), stop=(k == KD - 1))
                mm.then_inc(s["bvo_done"], 1)

            def prep_f1():
                pe.wait_ge(s["f1_raw_loaded"], 16)
                for n in range(4):
                    k, half = n // 2, n % 2
                    b = bank[("f0", "f1")[half]]
                    if n >= 2:
                        pe.wait_ge(s["wf1_ready"], n - 1)
                    for m in range(4):
                        mm = pe.transpose(b[:, m * P:(m + 1) * P], f1_raw[:, 4 * half + m, k * P:(k + 1) * P], ident[:])
                    mm.then_inc(s["f1T_done"], 1)

            def prep_f2():
                pe.wait_ge(s["f2_raw_loaded"], 16)
                for n in range(4):
                    b = bank[("y0", "y1")[n % 2]]
                    if n == 0:
                        pe.wait_ge(s["woT_ready"], 1)
                    if n == 1:
                        pe.wait_ge(s["wvo_ready"], 1)
                    if n >= 2:
                        pe.wait_ge(s["wf2_ready"], n - 1)
                    for q in range(4):
                        k, e = 2 * n + q // 2, q % 2
                        mm = pe.transpose(b[:, q * P:(q + 1) * P], f2_raw[:, e, k * P:(k + 1) * P], ident[:])
                    mm.then_inc(s["f2T_done"], 1)

            def prep_theta():
                pe.wait_ge(s["abs_summed"], 8)
                pe.wait_ge(s["wqk_ready"], 1)
                pe.matmul(bank["p1"][:, 0:8], mean_w[:], abs_sum[:], start=True, stop=True).then_inc(s["abs_tot_done"], 1)

            def prep_fc():
                for n in range(4):
                    k, half = n // 2, n % 2
                    b = bank[("f0", "f1")[half]]
                    if n == 0:
                        pe.wait_ge(s["fc_tern"], 1)
                        pe.wait_ge(s["wf1_ready"], 4)
                    if n >= 2:
                        pe.wait_ge(s["wfc_ready"], n - 1)
                    for m in range(4):
                        mm = pe.transpose(b[:, m * P:(m + 1) * P], fc_raw[:, 4 * half + m, k * P:(k + 1) * P], ident[:])
                    mm.then_inc(s["fcT_done"], 1)

            def prep_pj():
                for n in range(4):
                    b = bank[("y0", "y1")[n % 2]]
                    if n == 0:
                        pe.wait_ge(s["pj_tern"], 1)
                        pe.wait_ge(s["wf2_ready"], 4)
                    if n >= 2:
                        pe.wait_ge(s["wpj_ready"], n - 1)
                    for q in range(4):
                        k, e = 2 * n + q // 2, q % 2
                        mm = pe.transpose(b[:, q * P:(q + 1) * P], pj_raw[:, e, k * P:(k + 1) * P], ident[:])
                    mm.then_inc(s["pjT_done"], 1)

            def prep_cpj():
                pe.wait_ge(s["wpj_ready"], 4)
                for k in range(KH):
                    pe.wait_ge(s["lnb_wide_ready"], k + 1)
                    pe.matmul(bank["y0"][:, 0:D], ln3b_wide, wpj[:, k, :].bitcast(F32),
                              start=(k == 0), stop=(k == KH - 1)).then_inc(s["cpj_done"], 1)

            def tu(g, prev_pj):
                pe.wait_ge(s["u_ready"], 4 * g + 4)
                for k, b in ((0, "x"), (1, "c")):
                    if k == 0 and later(g, 1):
                        pe.wait_ge(s["z2_lo"], 2 * (g - 1) + 1)
                    if k == 1 and prev_pj is not None:
                        pe.wait_ge(s["mu_ready"], prev_pj + 1)
                    elif k == 1 and later(g, 1):
                        pe.wait_ge(s["u_lo"], 2 * (g - 1) + 2)
                    flip(u, bank[b], k).then_inc(s["tu_done"], 1)

            def qk_proj(g, fc):
                if later(g, 1) and fc is not None:
                    pe.wait_ge(s["z3_lo"], 2 * fc + 1)
                pe.wait_ge(s["u_lo"], 2 * g + 2)
                pe.wait_ge(s["u_hi"], 2 * g + 2)
                if isinstance(g, int) and g == 0:
                    pe.wait_ge(s["wqk_ready"], 1)
                for k in range(KD):
                    mm = split3(bank["x"][:], [w[:, k, :] for w in wqk], [r[:, k, :] for r in uT],
                                k == 0, k == KD - 1)
                mm.then_inc(s["qk_done"], 1)

            def v_proj(g, half):
                if half == 0:
                    pe.wait_ge(s["qk_minmax"], 2 * g + 2)
                    if isinstance(g, int) and g == 0:
                        pe.wait_ge(s["wvo_ready"], 1)
                else:
                    pe.wait_ge(s["v_ready"], 2 * g + 1)
                for j in range(2):
                    t = 2 * half + j
                    for k in range(KD):
                        mm = split3(bank["x"][:, j * D:(j + 1) * D], [r[:, k, t * P:(t + 1) * P] for r in uT],
                                    [w[:, k, :] for w in wvo], k == 0, k == KD - 1)
                mm.then_inc(s["v_done"], 1)

            def scores(g, pj):
                pe.wait_ge(s["kk_ready"], 2 * g + 2)
                pe.wait_ge(s["qk_lo_ready"], g + 1)
                pe.wait_ge(s["qk_hi_ready"], g + 1)
                q = [r[0:FQ, :] for r in qkh]
                for j, b, c0, q0 in ((0, "p0", 0, 0), (1, "p1", 0, P), (2, "x", 0, 2 * P), (3, "x", 2 * P, 2 * P)):
                    if j < 2 and pj is not None:
                        pe.wait_ge(s["out_ready"], 4 * pj + 2 * j + 2)
                    elif j == 0 and later(g, 1):
                        pe.wait_ge(s["xa_ready"], 4 * (g - 1) + 4)
                    elif j == 1 and later(g, 1):
                        pe.wait_ge(s["z2_lo"], 2 * (g - 1) + 2)
                    elif j == 0:
                        pe.wait_ge(s["bvo_ready"], 1)
                    elif j == 1:
                        pe.wait_ge(s["theta_ready"], 1)
                    if j == 2:
                        pe.wait_ge(s["v_ready"], 2 * g + 2)
                    mm = split3(bank[b][:, c0:c0 + N - q0], [w[:, j * P:(j + 1) * P] for w in kk],
                                [r[:, q0:] for r in q], True, True)
                    if j != 2:
                        mm.then_inc(s["s_done"], 1)

            def attend(g):
                pe.wait_ge(s["v_lo_ready"], 2 * g + 2)
                pe.wait_ge(s["v_hi_ready"], 2 * g + 2)
                pe.wait_ge(s["a_hi_diag"], 4 * g + 4)
                pe.wait_ge(s["a_hi_off"], 3 * g + 3)
                pe.wait_ge(s["a_lo_ready"], 4 * g + 4)
                pe.wait_ge(s["a_lo_masked"], g + 1)
                if isinstance(g, int) and g == 0:
                    pe.wait_ge(s["v_ones_ready"], 3)
                for t, b in enumerate(("p0", "p1", "x", "p0")):
                    if t == 3:
                        pe.wait_ge(s["xa_ready"], 4 * g + 1)
                    for j in range(t + 1):
                        mm = split3(bank[b][:, 0:VW], [w[:, j, (t - j) * P:(t - j + 1) * P] for w in a],
                                    [r[:, j, :] for r in v], j == 0, j == t)
                    mm.then_inc(s["av_done"], 1)

            def tz2(g):
                pe.wait_ge(s["z2_ready"], 4 * g + 4)
                for k, b in ((0, "x"), (1, "p1")):
                    pe.wait_ge(s["xa_ready"], 4 * g + (3 if k == 0 else 2))
                    flip(z, bank[b], k).then_inc(s["tz2_done"], 1)

            def f1(g, m):
                if m == 0:
                    pe.wait_ge(s["z2_lo"], 2 * g + 2)
                    pe.wait_ge(s["z2_hi"], 2 * g + 2)
                    if isinstance(g, int) and g == 0:
                        pe.wait_ge(s["wfc_ready"], 4)
                if later(g, 1) or m >= 2:
                    pe.wait_ge(s["h_gelu"], 8 * g + m - 1)
                for k in range(KD):
                    mm = split3(bank[("f0", "f1")[m % 2]][:], [w[:, k, m * P:(m + 1) * P] for w in wf1],
                                [r[:, k, :] for r in z2T], k == 0, k == KD - 1)
                mm.then_inc(s["f1_done"], 1)

            def f2(g, k):
                if k == 0:
                    if later(g, 1):
                        pe.wait_ge(s["y_ready"], 2 * (g - 1) + 2)
                    if isinstance(g, int) and g == 0:
                        pe.wait_ge(s["cpj_ready"], 1)
                        pe.wait_ge(s["wpj_ready"], 4)
                pe.wait_ge(s["h_lo_ready"], 8 * g + k + 1)
                pe.wait_ge(s["h_hi_ready"], 8 * g + k + 1)
                for t in range(T):
                    ps = bank[("y0", "y1")[t // 2]][:, (t % 2) * D:(t % 2 + 1) * D]
                    mm = split3(ps, [r[:, k % 3, t * P:(t + 1) * P] for r in hr], [w[:, k, :] for w in wf2],
                                k == 0 and t % 2 == 0, k == KH - 1, skip=True)
                mm.then_inc(s["f2_step"], 1)

            def tz3(g, at, prev_pj):
                pe.wait_ge(s["z3_ready"], 4 * g + 4)
                for k, b in ((0, "x"), (1, "c")):
                    if at is not None:
                        pe.wait_ge(s["u_lo"], 2 * at + k + 1)
                    else:
                        if k == 0 and later(g, G - 1):
                            pe.wait_ge(s["z3_lo"], 2 * (g - 1) + 1)
                        elif k == 0:
                            pe.wait_ge(s["z2_lo"], 2 * (g + 1) + 1)
                        else:
                            pe.wait_ge(s["mu_ready"], prev_pj + 1)
                    flip(z, bank[b], k).then_inc(s["tz3_done"], 1)

            def fc_up(g, m, pj):
                if m == 0:
                    pe.wait_ge(s["z3_lo"], 2 * g + 2)
                    pe.wait_ge(s["z3_hi"], 2 * g + 2)
                    if pj is not None:
                        pe.wait_ge(s["var_ready"], pj + 1)
                if m >= 1:
                    pe.wait_ge(s["h3_gelu"], 8 * g + m)
                for k in range(KD):
                    for part in range(2):
                        mm = pe.matmul(bank["c"][:], wfc[:, k, m * P:(m + 1) * P], z3T[part][:, k, :],
                                       start=(k == 0 and part == 0), stop=(k == KD - 1 and part == 1))
                mm.then_inc(s["fc_done"], 1)

            def mean(g):
                pe.wait_ge(s["h3_gelu"], 8 * g + 8)
                pe.wait_ge(s["hsum_step"], 7 * g + 7)
                pe.matmul(bank["c"][:], mean_w[:], hsum, start=True, stop=True).then_inc(s["mu_done"], 1)

            def proj(g, k, prev_at):
                if k == 0:
                    if prev_at is not None:
                        pe.wait_ge(s["xa_ready"], 4 * prev_at + 4)
                        pe.wait_ge(s["z2_lo"], 2 * prev_at + 2)
                    else:
                        pe.wait_ge(s["out_ready"], 4 * (g - 1) + 4)
                pe.wait_ge(s["g_lo_ready"], 8 * g + k + 1)
                pe.wait_ge(s["g_hi_ready"], 8 * g + k + 1)
                for t in range(T):
                    ps = bank[("p0", "p1")[t // 2]][:, (t % 2) * D:(t % 2 + 1) * D]
                    for part in range(2):
                        mm = pe.matmul(ps, gr[part][:, k % 2, t * P:(t + 1) * P], wpj[:, k, :],
                                       start=(k == 0 and t % 2 == 0 and part == 0), stop=(k == KH - 1 and part == 1),
                                       skip_group_check=True)
                mm.then_inc(s["pj_step"], 1)

            def var(g, fc):
                pe.wait_ge(s["sqsum_step"], 7 * g + 7)
                if fc is not None:
                    pe.wait_ge(s["z3_lo"], 2 * fc + 2)
                else:
                    pe.wait_ge(s["mu_ready"], g + 1)
                for t in range(T):
                    mm = pe.matmul(bank["c"][:, t:t + 1], sqsum[:, t * P:(t + 1) * P], mean_w[:, 0:1],
                                   start=True, stop=True)
                mm.then_inc(s["var_done"], 1)

            def body(i):
                at, ml, fc, pj = groups(i)
                first = isinstance(i, int) and i == -1
                if first:
                    prep_small()
                    prep_vo()
                if at is not None:
                    tu(at, pj)
                if first:
                    qk_proj(at, fc)
                    prep_f1()
                    v_proj(at, 0)
                    prep_f2()
                    v_proj(at, 1)
                    prep_theta()
                    scores(at, pj)
                    prep_fc()
                    prep_pj()
                    attend(at)
                    prep_cpj()
                    tz2(at)
                    return
                for m in range(KH):
                    if ml is not None:
                        f1(ml, m)
                    if m == 1 and fc is not None:
                        tz3(fc, at, pj)
                    if m == 2 and at is not None:
                        qk_proj(at, fc)
                    if m == 3 and at is not None:
                        v_proj(at, 0)
                    if m == 5 and at is not None:
                        scores(at, pj)
                    if m >= 4 and fc is not None:
                        fc_up(fc, 2 * (m - 4), pj)
                    if m < 4 and pj is not None:
                        proj(pj, 2 * m, ml)
                    if ml is not None and m >= 1:
                        f2(ml, m - 1)
                    if m == 6 and at is not None:
                        attend(at)
                    if m == 3 and at is not None:
                        v_proj(at, 1)
                    if m < 4 and pj is not None:
                        proj(pj, 2 * m + 1, ml)
                    if m == 3 and pj is not None:
                        var(pj, fc)
                    if m >= 4 and fc is not None:
                        fc_up(fc, 2 * (m - 4) + 1, pj)
                if ml is not None:
                    f2(ml, KH - 1)
                if fc is not None:
                    mean(fc)
                if at is not None:
                    tz2(at)

            steps(pe, body)

        @block.scalar
        def _(act):
            def prep():
                act.wait_ge(s["woT_done"], 1)
                act.activation(woT[:].rearrange("p k d -> p (k d)"), bank["y0"][:], ACT.Copy).then_inc(s["woT_ready"], 1)
                act.wait_ge(s["qkT_done"], 1)
                act.wait_ge(s["vec_ready"], 1)
                for k in range(KD):
                    act.activation(wqk[0][:, k, :], bank["p1"][:, k * P:(k + 1) * P], ACT.Copy,
                                   scale=ln1w_c[:, k:k + 1]).then_inc(s["wqk_hi_ready"], 1)
                act.wait_ge(s["wvo_done"], 1)
                for k in range(KD):
                    act.activation(wvo[0][:, k, :], bank["y1"][:, k * D:(k + 1) * D], ACT.Copy,
                                   scale=ln1w_c[:, k:k + 1]).then_inc(s["wvo_hi_ready"], 1)
                act.wait_ge(s["bvo_done"], 1)
                act.activation(bvo_b[:], bank["p0"][:, 0:D], ACT.Copy).then_inc(s["bvo_ready"], 1)

            def prep_f1():
                for n in range(4):
                    k, half = n // 2, n % 2
                    act.wait_ge(s["f1T_done"], n + 1)
                    act.activation(wf1[0][:, k, half * 512:(half + 1) * 512], bank[("f0", "f1")[half]][:], ACT.Copy,
                                   scale=ln2w_c[:, k:k + 1]).then_inc(s["wf1_hi_ready"], 1)

            def prep_f2():
                for n in range(4):
                    act.wait_ge(s["f2T_done"], n + 1)
                    act.activation(wf2[0][:, 2 * n:2 * n + 2, :].rearrange("p k d -> p (k d)"),
                                   bank[("y0", "y1")[n % 2]][:], ACT.Copy).then_inc(s["wf2_hi_ready"], 1)

            def prep_abs():
                act.wait_ge(s["fc_raw_loaded"], 16)
                act.wait_ge(s["pj_raw_loaded"], 16)
                for n in range(8):
                    if n:
                        act.wait_ge(s["abs_summed"], n)
                    act.activation(abs_out[:], h3[:, n, :], ACT.Abs,
                                   accum_out=abs_sum[:, n:n + 1]).then_inc(s["abs_summed"], 1)

            def prep_tern():
                for n in range(4):
                    k, half = n // 2, n % 2
                    act.wait_ge(s["fcT_done"], n + 1)
                    act.activation(wfc[:, k, half * 512:(half + 1) * 512], bank[("f0", "f1")[half]][:],
                                   ACT.Copy).then_inc(s["wfc_ready"], 1)
                for n in range(4):
                    act.wait_ge(s["pjT_done"], n + 1)
                    act.activation(wpj[:, 2 * n:2 * n + 2, :].rearrange("p k d -> p (k d)"),
                                   bank[("y0", "y1")[n % 2]][:], ACT.Copy).then_inc(s["wpj_ready"], 1)

            def u_hi(g):
                if later(g, 1):
                    act.wait_ge(s["v_done"], 2 * (g - 1) + 2)
                for k, b in ((0, "x"), (1, "c")):
                    act.wait_ge(s["tu_done"], 2 * g + k + 1)
                    act.activation(uT[0][:, k, :], bank[b][:], ACT.Copy).then_inc(s["u_hi"], 1)

            def qk_e(g):
                act.wait_ge(s["qk_minmax"], 2 * g + 2)
                act.activation(qk_exp[:], qk_exp[:], ACT.Exp).then_inc(s["qk_exp_ready"], 1)

            def qk_h(g):
                act.wait_ge(s["qk_ready"], g + 1)
                if later(g, 1):
                    act.wait_ge(s["s_done"], 3 * (g - 1) + 3)
                    act.wait_ge(s["kk_ready"], 2 * (g - 1) + 2)
                act.activation(qkh[0][:], qk[:], ACT.Copy).then_inc(s["qk_hi_ready"], 1)

            def v_h(g, half):
                act.wait_ge(s["v_ready"], 2 * g + half + 1)
                if half == 0 and later(g, 1):
                    act.wait_ge(s["av_done"], 4 * (g - 1) + 4)
                act.activation(v[0][:, 2 * half:2 * half + 2, 0:D], v32[:], ACT.Copy).then_inc(s["v_hi_ready"], 1)

            def a_off(g):
                if later(g, 1):
                    act.wait_ge(s["av_done"], 4 * (g - 1) + 4)
                for j, b, n in ((0, "p0", 1), (1, "p1", 2), (2, "x", 3)):
                    w = N - (j + 1) * P
                    act.wait_ge(s["a_hi_diag"], 4 * g + (n if n < 3 else 4))
                    act.wait_ge(s["s_done"], 3 * g + n)
                    act.activation(a[0][:, j, P:P + w], bank[b][:, P:P + w], ACT.Copy).then_inc(s["a_hi_off"], 1)

            def z2_hi(g):
                if later(g, 1):
                    act.wait_ge(s["f1_done"], 8 * (g - 1) + 8)
                for k, b in ((0, "x"), (1, "p1")):
                    act.wait_ge(s["tz2_done"], 2 * g + k + 1)
                    act.activation(z2T[0][:, k, :], bank[b][:], ACT.Copy).then_inc(s["z2_hi"], 1)

            def gelu(g, m):
                act.wait_ge(s["f1_done"], 8 * g + m + 1)
                if later(g, 1) or m >= 3:
                    act.wait_ge(s["h_lo_ready"], 8 * g + (m - 2 if m >= 3 else 0))
                act.activation(hring[:, m % 3, :], bank[("f0", "f1")[m % 2]][:], ACT.Gelu,
                               bias=f1_bias[:, m:m + 1]).then_inc(s["h_gelu"], 1)

            def z3_hi(g):
                if later(g, 1):
                    act.wait_ge(s["fc_done"], 8 * (g - 1) + 8)
                for k, b in ((0, "x"), (1, "c")):
                    act.wait_ge(s["tz3_done"], 2 * g + k + 1)
                    act.activation(z3T[0][:, k, :], bank[b][:], ACT.Copy).then_inc(s["z3_hi"], 1)

            def gelu3(g, m):
                act.wait_ge(s["fc_done"], 8 * g + m + 1)
                if m == 0 and later(g, 1):
                    act.wait_ge(s["g_lo_ready"], 8 * (g - 1) + 8)
                    act.wait_ge(s["g_hi_ready"], 8 * (g - 1) + 8)
                    act.wait_ge(s["sq_ready"], 8 * (g - 1) + 8)
                act.activation(h3[:, m, :], bank["c"][:], ACT.Gelu).then_inc(s["h3_gelu"], 1)

            def mu_copy(g):
                act.wait_ge(s["mu_done"], g + 1)
                if later(g, 1):
                    act.wait_ge(s["d_ready"], 8 * (g - 1) + 8)
                act.activation(mu[:], bank["c"][:], ACT.Copy).then_inc(s["mu_ready"], 1)

            def g_hi(g, m):
                act.wait_ge(s["d_ready"], 8 * g + m + 1)
                if later(g, 1) or m >= 2:
                    act.wait_ge(s["pj_step"], 8 * g + (m - 1 if m >= 2 else 0))
                act.activation(gr[0][:, m % 2, :], h3[:, m, :], ACT.Copy,
                               scale=ln3w_c[:, m:m + 1]).then_inc(s["g_hi_ready"], 1)

            def square(g, m):
                act.wait_ge(s["d_ready"], 8 * g + m + 1)
                if later(g, 1) or m >= 2:
                    act.wait_ge(s["sqsum_step"], 7 * g + (max(m - 2, 1) if m >= 2 else 0))
                act.activation(sq[:, m % 2, :], h3[:, m, :], ACT.Square).then_inc(s["sq_ready"], 1)

            def body(i):
                at, ml, fc, pj = groups(i)
                if isinstance(i, int) and i == -1:
                    prep()
                    u_hi(at)
                    prep_f1()
                    qk_e(at)
                    prep_f2()
                    v_h(at, 0)
                    qk_h(at)
                    v_h(at, 1)
                    prep_abs()
                    a_off(at)
                    prep_tern()
                    act.wait_ge(s["cpj_done"], KH)
                    act.activation(cpj_b[:], bank["y0"][:, 0:D], ACT.Copy).then_inc(s["cpj_ready"], 1)
                    z2_hi(at)
                    return
                if at is not None:
                    u_hi(at)
                for m in range(KH):
                    if m < 4 and pj is not None:
                        g_hi(pj, 2 * m)
                    if ml is not None:
                        gelu(ml, m)
                    if m == 1 and fc is not None:
                        z3_hi(fc)
                    if m < 4 and pj is not None:
                        g_hi(pj, 2 * m + 1)
                    if m == 2 and at is not None:
                        qk_e(at)
                    if m < 4 and pj is not None:
                        square(pj, 2 * m)
                        square(pj, 2 * m + 1)
                    if m == 3 and at is not None:
                        qk_h(at)
                        v_h(at, 0)
                        v_h(at, 1)
                    if m == 5 and at is not None:
                        a_off(at)
                    if m >= 4 and fc is not None:
                        gelu3(fc, 2 * (m - 4))
                        gelu3(fc, 2 * (m - 4) + 1)
                if fc is not None:
                    mu_copy(fc)
                if at is not None:
                    z2_hi(at)

            steps(act, body)

        @block.vector
        def _(dve):
            def consts():
                dve.memset(mean_w[:], 1.0 / H).then_inc(s["consts_ready"], 1)
                dve.memset(neg_half[:], -0.5)
                dve.memset(v[0][:, :, D:D + 1].bitcast(F32), 1.0).then_inc(s["v_ones_ready"], 1)
                dve.memset(v[0][:, :, D + 1:VW].bitcast(F32), 0.0).then_inc(s["v_ones_ready"], 1)
                dve.memset(v[1][:, :, D:VW].bitcast(F32), 0.0).then_inc(s["v_ones_ready"], 1)

            def prep_vec():
                dve.wait_ge(s["vec_t"], 1)
                dve.tensor_copy(vec[:], bank["p0"][:, 0:31]).then_inc(s["vec_ready"], 1)
                dve.wait_ge(s["vec_ready"], 1)
                dve.wait_ge(s["bcast_loaded"], 64)
                dve.wait_ge(s["qk_raw_loaded"], 32)
                dve.wait_ge(s["v_raw_loaded"], 32)

                n = 0
                for src, col in ((wv_raw[:, 0, :], 8), (wv_raw[:, 1, :], 9), (qk_raw, 10)):
                    if n:
                        dve.wait_ge(s["dots_done"], n)
                    dve.tensor_tensor_reduce(dot_out, src, ln1b_b, 1.0, 0.0, ALU.mult, ALU.add,
                                             dots[:, col:col + 1]).then_inc(s["dots_done"], 1)
                    n += 1
                dve.wait_ge(s["dots_done"], 3)
                dve.tensor_tensor(vb_full[:], dots[:, 8:10], vb_c, ALU.add).then_inc(s["bias_done"], 1)
                dve.tensor_tensor(qk_bias[:], dots[:, 10:11], qkb_c, ALU.add).then_inc(s["bias_done"], 1)
                dve.wait_ge(s["bias_done"], 2)
                for k in range(KD):
                    dve.tensor_scalar(vb_wide[:, k, :], mean_w[:], 0.0, vb_full[:, k:k + 1],
                                      ALU.mult, ALU.add).then_inc(s["vb_wide_ready"], 1)
                dve.wait_ge(s["wqk_hi_ready"], 2)
                for k in range(KD):
                    mm = dve.scalar_tensor_tensor(wqk[1][:, k, :], bank["p1"][:, k * P:(k + 1) * P],
                                                  ln1w_c[:, k:k + 1], wqk[0][:, k, :].bitcast(F32),
                                                  ALU.mult, ALU.subtract)
                mm.then_inc(s["wqk_ready"], 1)
                dve.wait_ge(s["wvo_hi_ready"], 2)
                for k in range(KD):
                    mm = dve.scalar_tensor_tensor(wvo[1][:, k, :], bank["y1"][:, k * D:(k + 1) * D],
                                                  ln1w_c[:, k:k + 1], wvo[0][:, k, :].bitcast(F32),
                                                  ALU.mult, ALU.subtract)
                mm.then_inc(s["wvo_ready"], 1)

            def prep_f1():
                for n in range(4):
                    k, half = n // 2, n % 2
                    dve.wait_ge(s["wf1_hi_ready"], n + 1)
                    dve.scalar_tensor_tensor(wf1[1][:, k, half * 512:(half + 1) * 512],
                                             bank[("f0", "f1")[half]][:], ln2w_c[:, k:k + 1],
                                             wf1[0][:, k, half * 512:(half + 1) * 512].bitcast(F32),
                                             ALU.mult, ALU.subtract).then_inc(s["wf1_ready"], 1)
                dve.wait_ge(s["f1_raw_loaded"], 16)
                for m in range(KH):
                    dve.wait_ge(s["dots_done"], 3 + m)
                    dve.tensor_tensor_reduce(dot_out, f1_raw[:, m, :], ln2b_b, 1.0, 0.0, ALU.mult, ALU.add,
                                             dots[:, m:m + 1]).then_inc(s["dots_done"], 1)
                dve.wait_ge(s["dots_done"], 3 + KH)
                dve.tensor_tensor(f1_bias[:], dots[:, 0:KH], f1b_c, ALU.add).then_inc(s["bias_done"], 1)

            def prep_f2():
                for n in range(4):
                    dve.wait_ge(s["wf2_hi_ready"], n + 1)
                    dve.tensor_tensor(wf2[1][:, 2 * n:2 * n + 2, :].rearrange("p k d -> p (k d)"),
                                      bank[("y0", "y1")[n % 2]][:],
                                      wf2[0][:, 2 * n:2 * n + 2, :].rearrange("p k d -> p (k d)").bitcast(F32),
                                      ALU.subtract).then_inc(s["wf2_ready"], 1)

            def prep_tern():
                dve.wait_ge(s["abs_tot_done"], 1)
                dve.tensor_reduce(abs_tot[:], bank["p1"][:, 0:8].rearrange("p (w n) -> p w n", w=2),
                                  AXX, ALU.add).then_inc(s["theta_ready"], 1)
                dve.wait_ge(s["theta_ready"], 1)
                dve.tensor_scalar(theta[:, 0:2], abs_tot[:], 0.5 * H / (H * D), 0.5 * ABSMEAN_EPS,
                                  ALU.mult, ALU.add).then_inc(s["theta_ready"], 1)
                dve.wait_ge(s["theta_ready"], 2)
                dve.tensor_scalar(theta[:, 2:4], theta[:, 0:2], -1.0, None, ALU.mult).then_inc(s["theta_ready"], 1)
                dve.wait_ge(s["theta_ready"], 3)
                for w, (low, tern) in enumerate((("fc_low", "fc_tern"), ("pj_low", "pj_tern"))):
                    raw = h3[:, 4 * w:4 * w + 4, :].rearrange("p a n -> p (a n)")
                    if w:
                        dve.wait_ge(s["fc_tern"], 1)
                    dve.tensor_scalar(tern_low, raw, theta[:, 2 + w:3 + w], None, ALU.is_lt).then_inc(s[low], 1)
                    dve.wait_ge(s[low], 1)
                    dve.scalar_tensor_tensor(raw, raw, theta[:, w:w + 1], tern_low,
                                             ALU.is_gt, ALU.subtract).then_inc(s[tern], 1)

            def prep_lnb():
                for k in range(KH):
                    if k:
                        dve.wait_ge(s["cpj_done"], k)
                    dve.tensor_scalar(ln3b_wide, mean_w[:], 0.0, ln3b_c[:, k:k + 1],
                                      ALU.mult, ALU.add).then_inc(s["lnb_wide_ready"], 1)

            def stats(n, src, t, ready):
                dve.bn_stats(bn[n][:, t, :], src[:, t, :]).then_inc(s[f"ln{n + 1}_bn"], 1)

            def aggregate(n, g):
                if later(g, 1):
                    dve.wait_ge(s[f"ln{n + 1}_rs"], (g - 1) + 1)
                dve.wait_ge(s[f"ln{n + 1}_bn"], 4 * g + 4)
                dve.tensor_scalar(fence[:], mean_w[:, 0:1], 1.0, None, ALU.mult)
                for t in range(T):
                    dve.bn_aggr(mv[n][:, t, :], bn[n][:, t, :]).then_inc(s[f"ln{n + 1}_mv"], 1)
                dve.wait_ge(s[f"ln{n + 1}_mv"], 4 * g + 4)
                dve.tensor_scalar(ve[n][:, 0, :], mv[n][:, :, 1], 1.0, LN_EPS, ALU.mult, ALU.add).then_inc(s[f"ln{n + 1}_ve"], 1)
                if n == 0:
                    dve.tensor_scalar(ve[n][:, 1, :], mv[n][:, :, 1], 1.0 + LN_EPS, LN_EPS * LN_EPS,
                                      ALU.mult, ALU.add).then_inc(s["ln1_ve"], 1)

            def normalise(dst, src, n, t, row, ready):
                dve.tensor_scalar(dst[:, t, :], src[:, t, :], mv[n][:, t, 0:1], rs[n][:, row, t:t + 1],
                                  ALU.subtract, ALU.mult).then_inc(s[ready], 1)

            def ln1_stats(g):
                dve.wait_ge(s["x_loaded"], 16 * g + 16)
                for t in range(T):
                    stats(0, x_sb, t, None)
                if later(g, 1):
                    dve.wait_ge(s["n1_ready"], 4 * (g - 1) + 4)
                aggregate(0, g)

            def ln1_u(g):
                dve.wait_ge(s["ln1_rs"], g + 1)
                if later(g, 1):
                    dve.wait_ge(s["tu_done"], 2 * (g - 1) + 2)
                for t in range(T):
                    normalise(u, x_sb, 0, t, 1, "u_ready")

            def n1(g):
                if later(g, 1):
                    dve.wait_ge(s["xs_ready"], (g - 1) + 1)
                for t in range(T):
                    normalise(xa, x_sb, 0, t, 0, "n1_ready")

            def lo_part(dst, b, hi, ready):
                dve.tensor_tensor(dst, b, hi.bitcast(F32), ALU.subtract).then_inc(s[ready], 1)

            def u_lo(g):
                for k, b in ((0, "x"), (1, "c")):
                    dve.wait_ge(s["u_hi"], 2 * g + k + 1)
                    lo_part(uT[1][:, k, :], bank[b][:], uT[0][:, k, :], "u_lo")

            def qk_mm(g):
                dve.wait_ge(s["qk_done"], g + 1)
                if later(g, 1):
                    dve.wait_ge(s["qk_lo_ready"], (g - 1) + 1)
                    dve.wait_ge(s["qk_hi_ready"], (g - 1) + 1)
                dve.tensor_scalar(qk_exp[:], bank["x"][:], qk_bias[:], 0.0, ALU.add, ALU.min).then_inc(s["qk_minmax"], 1)
                dve.tensor_scalar(qk[:], bank["x"][:], qk_bias[:], 0.0, ALU.add, ALU.max).then_inc(s["qk_minmax"], 1)

            def qk_l(g):
                dve.wait_ge(s["qk_hi_ready"], g + 1)
                dve.tensor_tensor(qkh[1][:], qk[:], qkh[0][:].bitcast(F32), ALU.subtract).then_inc(s["qk_lo_ready"], 1)
                dve.tensor_copy(kk[0][:], qkh[0][FQ:P, :]).then_inc(s["kk_ready"], 1)
                dve.wait_ge(s["qk_lo_ready"], g + 1)
                dve.tensor_copy(kk[1][:], qkh[1][FQ:P, :]).then_inc(s["kk_ready"], 1)

            def v_sum(g, half):
                dve.wait_ge(s["v_done"], 2 * g + half + 1)
                if half == 0 and isinstance(g, int) and g == 0:
                    dve.wait_ge(s["bvo_ready"], 1)
                    dve.wait_ge(s["bvo_done"], 1)
                if half or later(g, 1):
                    dve.wait_ge(s["v_hi_ready"], 2 * g + half)
                    dve.wait_ge(s["v_lo_ready"], 2 * g + half)
                for j in range(2):
                    mm = dve.tensor_tensor(v32[:, j, :], bank["x"][:, j * D:(j + 1) * D], bvo_b[:], ALU.add)
                mm.then_inc(s["v_ready"], 1)

            def a_split(g):
                for j, b, c0, n in ((0, "p0", 0, 1), (1, "p1", 0, 2), (2, "x", 0, 3), (3, "x", 3 * P, 3)):
                    dve.wait_ge(s["s_done"], 3 * g + n)
                    if j == 0 and later(g, 1):
                        dve.wait_ge(s["av_done"], 4 * (g - 1) + 4)
                    dve.tensor_tensor(a[0][:, j, 0:P], bank[b][:, c0:c0 + P], mask[:],
                                      ALU.mult).then_inc(s["a_hi_diag"], 1)
                for j, b, c0 in ((0, "p0", 0), (1, "p1", 0), (2, "x", 0), (3, "x", 3 * P)):
                    w = N - j * P
                    dve.wait_ge(s["a_hi_diag"], 4 * g + j + 1)
                    if j < 3:
                        dve.wait_ge(s["a_hi_off"], 3 * g + j + 1)
                    lo_part(a[1][:, j, 0:w], bank[b][:, c0:c0 + w], a[0][:, j, 0:w], "a_lo_ready")

            def attn_out(g, t, b):
                dve.wait_ge(s["av_done"], 4 * g + t + 1)
                dve.tensor_scalar(den[:, t:t + 1], bank[b][:, D:D + 1], ATTN_EPS, None, ALU.add).then_inc(s["den_ready"], 1)
                dve.wait_ge(s["den_ready"], 4 * g + t + 1)
                dve.reciprocal(rden[:, t:t + 1], den[:, t:t + 1]).then_inc(s["rden_ready"], 1)
                dve.wait_ge(s["rden_ready"], 4 * g + t + 1)
                if t == 0:
                    dve.wait_ge(s["n1o_ready"], g + 1)
                dve.scalar_tensor_tensor(xa[:, t, :], bank[b][:, 0:D], rden[:, t:t + 1], xa[:, t, :],
                                         ALU.mult, ALU.add).then_inc(s["xa_ready"], 1)

            def attn_end(g):
                for t, b in enumerate(("p0", "p1", "x", "p0")):
                    attn_out(g, t, b)
                    dve.wait_ge(s["xa_ready"], 4 * g + t + 1)
                    stats(1, xa, t, None)
                if later(g, 1):
                    dve.wait_ge(s["z2_ready"], 4 * (g - 1) + 4)
                aggregate(1, g)

            def z2(g, fc):
                dve.wait_ge(s["ln2_rs"], g + 1)
                if fc is not None:
                    dve.wait_ge(s["tz3_done"], 2 * fc + 2)
                elif later(g, 1):
                    dve.wait_ge(s["tz2_done"], 2 * (g - 1) + 2)
                for t in range(T):
                    normalise(z, xa, 1, t, 0, "z2_ready")

            def z2_lo(g):
                for k, b in ((0, "x"), (1, "p1")):
                    dve.wait_ge(s["z2_hi"], 2 * g + k + 1)
                    lo_part(z2T[1][:, k, :], bank[b][:], z2T[0][:, k, :], "z2_lo")

            def h_hi(g, m):
                dve.wait_ge(s["h_gelu"], 8 * g + m + 1)
                if later(g, 1) or m >= 3:
                    dve.wait_ge(s["f2_step"], 8 * g + (m - 2 if m >= 3 else 0))
                dve.tensor_copy(hr[0][:, m % 3, :], hring[:, m % 3, :]).then_inc(s["h_hi_ready"], 1)

            def y_sum(g):
                dve.wait_ge(s["f2_step"], 8 * g + 8)
                dve.wait_ge(s["xs_ready"], g + 1)
                if later(g, 1):
                    dve.wait_ge(s["yc_ready"], (g - 1) + 1)
                for h in range(2):
                    dve.tensor_tensor(y[:, 2 * h:2 * h + 2, :].rearrange("p t d -> p (t d)"), bank[("y0", "y1")[h]][:],
                                      xs[:, 2 * h:2 * h + 2, :].rearrange("p t d -> p (t d)"), ALU.add).then_inc(s["y_ready"], 1)

            def ln3_stats(g):
                dve.wait_ge(s["y_ready"], 2 * g + 2)
                for t in range(T):
                    stats(2, y, t, None)
                if later(g, 1):
                    dve.wait_ge(s["z3_ready"], 4 * (g - 1) + 4)
                aggregate(2, g)

            def z3(g):
                dve.wait_ge(s["ln3_rs"], g + 1)
                dve.wait_ge(s["tz2_done"], 2 * min(g + 1, G - 1) + 2 if isinstance(g, int) else 2 * (g + 1) + 2)
                if isinstance(g, int) and g == G - 1:
                    dve.wait_ge(s["tz3_done"], 2 * (g - 1) + 2)
                for t in range(T):
                    normalise(z, y, 2, t, 0, "z3_ready")

            def z3_lo(g):
                for k, b in ((0, "x"), (1, "c")):
                    dve.wait_ge(s["z3_hi"], 2 * g + k + 1)
                    lo_part(z3T[1][:, k, :], bank[b][:], z3T[0][:, k, :], "z3_lo")

            def centre(g, m):
                if m == 0:
                    dve.wait_ge(s["mu_ready"], g + 1)
                    dve.wait_ge(s["hsum_step"], 7 * g + 7)
                dve.tensor_tensor(h3[:, m, :], h3[:, m, :], mu[:], ALU.subtract).then_inc(s["d_ready"], 1)

            def g_lo(g, m):
                dve.wait_ge(s["g_hi_ready"], 8 * g + m + 1)
                if later(g, 1) or m >= 2:
                    dve.wait_ge(s["pj_step"], 8 * g + (m - 1 if m >= 2 else 0))
                dve.wait_ge(s["d_ready"], 8 * g + m + 1)
                dve.scalar_tensor_tensor(gr[1][:, m % 2, :], h3[:, m, :], ln3w_c[:, m:m + 1],
                                         gr[0][:, m % 2, :].bitcast(F32), ALU.mult, ALU.subtract).then_inc(s["g_lo_ready"], 1)

            def var_eps(g):
                dve.wait_ge(s["var_done"], g + 1)
                if later(g, 1):
                    dve.wait_ge(s["rs3_ready"], (g - 1) + 1)
                dve.tensor_scalar(ve[3][:, 0, :], bank["c"][:, 0:T], LN_EPS, None, ALU.add).then_inc(s["var_ready"], 1)

            def output(g):
                dve.wait_ge(s["pj_step"], 8 * g + 8)
                dve.wait_ge(s["rs3_ready"], g + 1)
                dve.wait_ge(s["yc_ready"], g + 1)
                for t in range(T):
                    dve.scalar_tensor_tensor(yc[:, t, :], bank[("p0", "p1")[t // 2]][:, (t % 2) * D:(t % 2 + 1) * D],
                                             rs[3][:, 0, t:t + 1], yc[:, t, :], ALU.mult, ALU.add).then_inc(s["out_ready"], 1)

            def body(i):
                at, ml, fc, pj = groups(i)
                if isinstance(i, int) and i == -1:
                    consts()
                    ln1_stats(0)
                    prep_vec()
                    ln1_u(0)
                    n1(0)
                    u_lo(0)
                    prep_f1()
                    qk_mm(0)
                    prep_f2()
                    v_sum(0, 0)
                    qk_l(0)
                    v_sum(0, 1)
                    prep_tern()
                    a_split(0)
                    ln1_stats(1)
                    attn_end(0)
                    prep_lnb()
                    ln1_u(1)
                    z2(0, None)
                    z2_lo(0)
                    return
                if fc is not None:
                    y_sum(fc)
                if at is not None:
                    u_lo(at)
                if pj is not None:
                    centre(pj, 0)
                    centre(pj, 1)
                if fc is not None:
                    ln3_stats(fc)
                if at is not None:
                    n1(at)
                for m in range(KH):
                    if m < 4 and pj is not None:
                        g_lo(pj, 2 * m)
                    if ml is not None:
                        h_hi(ml, m)
                    if m == 0 and fc is not None:
                        z3(fc)
                    if m < 4 and pj is not None:
                        g_lo(pj, 2 * m + 1)
                    if m < 3 and pj is not None:
                        centre(pj, 2 * m + 2)
                        centre(pj, 2 * m + 3)
                    if m == 1 and fc is not None:
                        z3_lo(fc)
                    if m == 2 and at is not None:
                        qk_mm(at)
                    if m == 3 and at is not None:
                        v_sum(at, 0)
                        qk_l(at)
                        v_sum(at, 1)
                    if m == 3 and pj is not None:
                        var_eps(pj)
                    if m == 4:
                        if pj is not None:
                            output(pj)
                        if has_next(i):
                            ln1_stats(i + 2)
                    if m == 5 and at is not None:
                        a_split(at)
                    if m == 5 and has_next(i):
                        ln1_u(i + 2)
                    if m == 6 and at is not None:
                        attn_end(at)
                    if m == 7 and at is not None:
                        z2(at, fc)
                if at is not None:
                    z2_lo(at)

            steps(dve, body)

        @block.gpsimd
        def _(pool):
            def consts():
                pool.memset(ident[:], 0.0).then_inc(s["consts_memset"], 1)
                pool.memset(mask[:], 1.0).then_inc(s["consts_memset"], 1)
                pool.wait_ge(s["consts_memset"], 2)
                pool.affine_select(out=ident[:], in_=ident[:], compare_op=ALU.not_equal, fill=1.0, base=0,
                                   pattern=[[-1, P]], channel_multiplier=1).then_inc(s["consts_ready"], 1)
                pool.affine_select(out=mask[:], in_=mask[:], compare_op=ALU.is_ge, fill=0.0, base=0,
                                   pattern=[[1, P]], channel_multiplier=-1).then_inc(s["consts_ready"], 1)

            def rstd(n, g, two):
                ve_s, rs_s = s[f"ln{n + 1}_ve"], s[f"ln{n + 1}_rs"]
                c = 2 if two else 1
                if later(g, 1):
                    pool.wait_ge(s[("u_ready", "z2_ready", "z3_ready")[n]], 4 * (g - 1) + 4)
                    if two:
                        pool.wait_ge(s["n1_ready"], 4 * (g - 1) + 4)
                pool.wait_ge(ve_s, c * g + c)
                pool.tensor_tensor(rs[n][:, 0:c, :].rearrange("p c t -> p (c t)"),
                                   ve[n][:, 0:c, :].rearrange("p c t -> p (c t)"),
                                   neg_half[:, 0:c * T], ALU.pow).then_inc(rs_s, 1)

            def n1o(g):
                pool.wait_ge(s["n1_ready"], 4 * g + 4)
                if isinstance(g, int) and g == 0:
                    pool.wait_ge(s["bcast_loaded"], 64)
                pool.tensor_tensor(xa[:], xa[:], ob_b[:].unsqueeze(1).to_broadcast([P, T, D]),
                                   ALU.add).then_inc(s["n1o_ready"], 1)

            def xpb_(g):
                if isinstance(g, int) and g == 0:
                    pool.wait_ge(s["x_loaded"], 16)
                    pool.wait_ge(s["bcast_loaded"], 64)
                if later(g, 1):
                    pool.wait_ge(s["xs_ready"], (g - 1) + 1)
                pool.tensor_tensor(xpb[:], x_sb[:], f2b_b[:].unsqueeze(1).to_broadcast([P, T, D]),
                                   ALU.add).then_inc(s["xpb_ready"], 1)

            def xs_(g):
                pool.wait_ge(s["xa_ready"], 4 * g + 4)
                pool.wait_ge(s["xpb_ready"], g + 1)
                if later(g, 1):
                    pool.wait_ge(s["y_ready"], 2 * (g - 1) + 2)
                else:
                    pool.wait_ge(s["bias_done"], 3)
                    pool.wait_ge(s["bvo_done"], 1)
                pool.tensor_tensor(xs[:], xpb[:], xa[:], ALU.add).then_inc(s["xs_ready"], 1)

            def qk_sum(g):
                pool.wait_ge(s["qk_exp_ready"], g + 1)
                pool.wait_ge(s["qk_minmax"], 2 * g + 2)
                pool.tensor_tensor(qk[:], qk_exp[:], qk[:], ALU.add).then_inc(s["qk_ready"], 1)

            def v_lo(g, half):
                pool.wait_ge(s["v_hi_ready"], 2 * g + half + 1)
                pool.wait_ge(s["v_ready"], 2 * g + half + 1)
                if half == 0 and later(g, 1):
                    pool.wait_ge(s["av_done"], 4 * (g - 1) + 4)
                pool.tensor_tensor(v[1][:, 2 * half:2 * half + 2, 0:D], v32[:],
                                   v[0][:, 2 * half:2 * half + 2, 0:D].bitcast(F32), ALU.subtract).then_inc(s["v_lo_ready"], 1)

            def a_mask(g):
                pool.wait_ge(s["a_lo_ready"], 4 * g + 4)
                pool.tensor_tensor(a[1][:, :, 0:P], a[1][:, :, 0:P].bitcast(F32), mask[:].unsqueeze(1).to_broadcast([P, T, P]),
                                   ALU.mult).then_inc(s["a_lo_masked"], 1)

            def h_lo(g, m):
                pool.wait_ge(s["h_hi_ready"], 8 * g + m + 1)
                if later(g, 1) or m >= 3:
                    pool.wait_ge(s["f2_step"], 8 * g + (m - 2 if m >= 3 else 0))
                pool.tensor_tensor(hr[1][:, m % 3, :], hring[:, m % 3, :], hr[0][:, m % 3, :].bitcast(F32),
                                   ALU.subtract).then_inc(s["h_lo_ready"], 1)

            def hsum_step(g, m):
                pool.wait_ge(s["h3_gelu"], 8 * g + m + 1)
                if m == 1:
                    if later(g, 1):
                        pool.wait_ge(s["mu_done"], (g - 1) + 1)
                    pool.tensor_tensor(hsum, h3[:, 0, :], h3[:, 1, :], ALU.add).then_inc(s["hsum_step"], 1)
                else:
                    pool.wait_ge(s["hsum_step"], 7 * g + m - 1)
                    pool.tensor_tensor(hsum, hsum, h3[:, m, :], ALU.add).then_inc(s["hsum_step"], 1)

            def sqsum_step(g, m):
                pool.wait_ge(s["sq_ready"], 8 * g + m + 1)
                if m == 1:
                    if later(g, 1):
                        pool.wait_ge(s["var_done"], (g - 1) + 1)
                    pool.tensor_tensor(sqsum, sq[:, 0, :], sq[:, 1, :], ALU.add).then_inc(s["sqsum_step"], 1)
                else:
                    pool.wait_ge(s["sqsum_step"], 7 * g + m - 1)
                    pool.tensor_tensor(sqsum, sqsum, sq[:, m % 2, :], ALU.add).then_inc(s["sqsum_step"], 1)

            def rstd3(g):
                pool.wait_ge(s["var_ready"], g + 1)
                if later(g, 1):
                    pool.wait_ge(s["out_ready"], 4 * (g - 1) + 4)
                pool.tensor_tensor(rs[3][:, 0, :], ve[3][:, 0, :], neg_half[:, 0:T], ALU.pow).then_inc(s["rs3_ready"], 1)

            def yc_(g):
                pool.wait_ge(s["y_ready"], 2 * g + 2)
                if later(g, 1):
                    pool.wait_ge(s["out_stored"], 16 * (g - 1) + 16)
                pool.tensor_tensor(yc, y, cpj_b[:].unsqueeze(1).to_broadcast([P, T, D]),
                                   ALU.add).then_inc(s["yc_ready"], 1)

            def body(i):
                at, ml, fc, pj = groups(i)
                if isinstance(i, int) and i == -1:
                    consts()
                    rstd(0, 0, True)
                    xpb_(0)
                    n1o(0)
                    qk_sum(0)
                    v_lo(0, 0)
                    v_lo(0, 1)
                    a_mask(0)
                    rstd(0, 1, True)
                    rstd(1, 0, False)
                    return
                if ml is not None:
                    xs_(ml)
                if fc is not None:
                    rstd(2, fc, False)
                if at is not None:
                    n1o(at)
                for m in range(KH):
                    if ml is not None:
                        h_lo(ml, m)
                    if m < 4 and pj is not None:
                        if m:
                            sqsum_step(pj, 2 * m)
                        sqsum_step(pj, 2 * m + 1)
                    if m == 1 and at is not None:
                        xpb_(at)
                    if m == 2 and at is not None:
                        qk_sum(at)
                    if m == 3 and at is not None:
                        v_lo(at, 0)
                        v_lo(at, 1)
                    if m == 4:
                        if pj is not None:
                            rstd3(pj)
                        if has_next(i):
                            rstd(0, i + 2, True)
                    if m == 5 and at is not None:
                        a_mask(at)
                    if m >= 4 and fc is not None:
                        if m > 4:
                            hsum_step(fc, 2 * (m - 4))
                        hsum_step(fc, 2 * (m - 4) + 1)
                    if m == 6 and fc is not None:
                        yc_(fc)
                    if m == 6 and at is not None:
                        rstd(1, at, False)

            steps(pool, body)


_INS = ["L0_attn_x", "L0_attn_ln1_w", "L0_attn_ln1_b", "L0_attn_q_w", "L0_attn_q_b", "L0_attn_k_w", "L0_attn_k_b",
        "L0_attn_v_w", "L0_attn_v_b", "L0_attn_o_w", "L0_attn_o_b", "L0_attn_ln2_w", "L0_attn_ln2_b", "L0_attn_f1_w",
        "L0_attn_f1_b", "L0_attn_f2_w", "L0_attn_f2_b", "L0_ffn_W_fc", "L0_ffn_ln_w", "L0_ffn_ln_b", "L0_ffn_W_proj"]


def kernel(**inputs):
    import numpy as _np
    import concourse.bacc as _bacc
    from concourse import mybir as _mybir
    from concourse.bass_utils import run_bass_kernel_spmd as _run

    nc = _bacc.Bacc("TRN2", target_bir_lowering=False, num_devices=1)
    arrays, args = {}, []
    for name in _INS:
        a = _np.ascontiguousarray(inputs[name])
        arrays[f"in_{name}"] = a
        args.append(nc.dram_tensor(f"in_{name}", a.shape, _mybir.dt.from_np(a.dtype), kind="ExternalInput").ap())
    args.append(nc.dram_tensor("out", inputs["L0_attn_x"].shape, _mybir.dt.float32, kind="ExternalOutput").ap())
    build(nc, *args)
    r = _run(nc, [arrays], core_ids=[0])
    return r.results[0]["out"]
```

```python
from contextlib import ExitStack

import concourse.bass as bass
from concourse import mybir

F32 = mybir.dt.float32
F32R = mybir.dt.float32r
ALU = mybir.AluOpType
ACT = mybir.ActivationFunctionType
AXX = mybir.AxisListType.X

P = 128
LN_EPS = 1e-5
ATTN_EPS = 1e-6
ABSMEAN_EPS = 1e-6


def later(g, n):
    return not isinstance(g, int) or g >= n


def build(nc, x, ln1_w, ln1_b, q_w, q_b, k_w, k_b, v_w, v_b, o_w, o_b, ln2_w, ln2_b, f1_w, f1_b,
          f2_w, f2_b, fc_w, ln3_w, ln3_b, pj_w, out):
    G, N, D = x.shape
    FQ = q_w.shape[0]
    H = f1_w.shape[0]
    T = N // P
    KD = D // P
    KH = H // P
    VW = D + 2
    assert (T, KD, KH, 2 * FQ) == (4, 2, 8, P) and H == fc_w.shape[0]

    x_flat = x.rearrange("g n d -> (g n d)")
    out_flat = out.rearrange("g n d -> (g n d)")

    def group_rows(flat, offset):
        return flat[bass.ds(offset, N * D)].rearrange("(t p d) -> p t d", t=T, p=P)

    with ExitStack() as ctx:
        def sb(name, shape, dt=F32):
            return ctx.enter_context(nc.sbuf_tensor(name, shape, dt))

        def sem(name):
            return ctx.enter_context(nc.semaphore(name))

        bank = {n: ctx.enter_context(nc.psum_tensor("bank_" + n, [P, 512], F32))
                for n in ("f0", "f1", "y0", "y1", "p0", "p1", "x", "c")}

        wqk = [sb("wqk_hi", [P, KD, P], F32R), sb("wqk_lo", [P, KD, P], F32R)]
        wvo = [sb("wvo_hi", [P, KD, D], F32R), sb("wvo_lo", [P, KD, D], F32R)]
        wf1 = [sb("wf1_hi", [P, KD, H], F32R), sb("wf1_lo", [P, KD, H], F32R)]
        wf2 = [sb("wf2_hi", [P, KH, D], F32R), sb("wf2_lo", [P, KH, D], F32R)]
        wfc = sb("wfc_t", [P, KD, H], F32R)
        wpj = sb("wpj_t", [P, KH, D], F32R)

        ident = sb("ident", [P, P])
        mean_w = sb("mean_w", [P, P])
        mask = sb("mask", [P, P])
        neg_half = sb("neg_half", [P, 8])
        vec = sb("vec", [P, 31])
        ln1w_c, vb_c, qkb_c = vec[:, 0:2], vec[:, 2:4], vec[:, 4:5]
        ln2w_c, f1b_c, ln3w_c, ln3b_c = vec[:, 5:7], vec[:, 7:15], vec[:, 15:23], vec[:, 23:31]
        dots = sb("dots", [P, 11])
        f1_bias = sb("f1_bias", [P, KH])
        vb_full = sb("vb_full", [P, KD])
        qk_bias = sb("qk_bias", [P, 1])
        abs_sum = sb("abs_sum", [P, 8])
        abs_tot = sb("abs_tot", [P, 2])
        theta = sb("theta", [P, 4])
        bvo_b = sb("bvo_b", [P, D])
        ob_b = sb("ob_b", [P, D])
        f2b_b = sb("f2b_b", [P, D])
        pj_rows_b = sb("pj_rows_b", [P, 2, D])
        csum_b, cpj_b = pj_rows_b[:, 0, :], pj_rows_b[:, 1, :]

        x_sb = sb("x_sb", [P, T, D])
        u = sb("u", [P, T, D])
        xa = sb("xa", [P, T, D])
        xpb = sb("xpb", [P, T, D])
        xs = sb("xs", [P, T, D])
        z = sb("z", [P, T, D])
        y_yc = sb("y_yc", [P, 2, T, D])
        y, yc = y_yc[:, 0], y_yc[:, 1]
        uT = [sb("uT_hi", [P, KD, N], F32R), sb("uT_lo", [P, KD, N], F32R)]
        z2T = [sb("z2T_hi", [P, KD, N], F32R), sb("z2T_lo", [P, KD, N], F32R)]
        z3T = [sb("z3T_hi", [P, KD, N], F32R), sb("z3T_lo", [P, KD, N], F32R)]
        qk_out = sb("qk_out", [P, 2, N])
        qk_exp, qk = qk_out[:, 0, :], qk_out[:, 1, :]
        out_sb = qk_out[:].rearrange("p a n -> p (a n)").rearrange("p (t d) -> p t d", t=T)
        q_stack = sb("q_stack", [P, N], F32R)
        k_stack = sb("k_stack", [P, N], F32R)
        k_lo = sb("k_lo", [FQ, N], F32R)
        v32 = sb("v32", [P, 2, D])
        v = [sb("v_hi", [P, T, VW], F32R), sb("v_lo", [P, T, VW], F32R)]
        a = [sb("a_hi", [P, T, N], F32R), sb("a_lo", [P, T, N], F32R)]
        hring = sb("hring", [P, 3, N])
        hr = [sb("h_hi", [P, 3, N], F32R), sb("h_lo", [P, 3, N], F32R)]
        h3 = sb("h3", [P, KH, N])
        sums = sb("sums", [P, 5, N])
        sq, hsum, sqsum = sums[:, 0:2], sums[:, 2], sums[:, 3]
        gr = [sb("g_hi", [P, 2, N], F32R), sb("g_lo", [P, 2, N], F32R)]
        bn = [sb(f"bn{n}", [P, T, 6]) for n in range(3)]
        mv = [sb(f"mv{n}", [P, T, 2]) for n in range(3)]
        ve = [sb(f"ve{n}", [P, 2, T]) for n in range(4)]
        rs = [sb(f"rs{n}", [P, 2, T]) for n in range(4)]
        fence = sb("fence", [P, 1])
        den = sb("den", [P, T])
        rden = sb("rden", [P, T])
        neg_mu, mu_sq, var_raw, neg_mu_rs = [sb(n, [P, T]) for n in ("neg_mu", "mu_sq", "var_raw", "neg_mu_rs")]

        qk_raw = hring[:, 0, 0:D]
        wv_raw = hring[:, 1, :].rearrange("p (k d) -> p k d", k=KD)
        wo_raw = hring[:, 2, :].rearrange("p (k d) -> p k d", k=KD)
        woT = v32
        vec_rows, late_rows = z[0:5, 0, 0:P], z[0:26, 1, 0:P]
        f1_raw = y_yc[:, :].rearrange("p a t d -> p (a t) d")
        f2_raw = sums[:, 0:4].rearrange("p a n -> p (a n)").rearrange("p (k h) -> p k h", k=KD)
        fc_raw = h3[:, 0:4, :].rearrange("p a n -> p (a n)").rearrange("p (m d) -> p m d", m=KH)
        pj_raw = h3[:, 4:8, :].rearrange("p a n -> p (a n)").rearrange("p (k h) -> p k h", k=KD)
        tern_low = y_yc[:].rearrange("p a t d -> p (a t d)")
        ln1b_b, ln2b_b, dot_out = xs[:, 0, :], xs[:, 1, :], xs[:, 2, :]
        vb_wide = xs[:, 3, :].rearrange("p (k m) -> p k m", k=KD)
        abs_out = sums[:, 4, :]
        pj_rows = sums[0:2, 4, 0:D]
        row_select = sums[0:2, 4, D:D + 2 * P].rearrange("p (r m) -> p r m", r=2)

        names = """x_loaded rows_loaded late_rows_loaded ln1b_loaded ln2b_loaded ob_loaded qk_raw_loaded v_raw_loaded f1_raw_loaded f2_raw_loaded
            fc_raw_loaded pj_raw_loaded consts_memset consts_ready vec_t vec_ready late_vec_t late_vec_ready
            dots_done bias_done vb_wide_ready qkT_done wqk_hi_ready wqk_ready woT_done woT_ready wvo_done
            wvo_hi_ready wvo_ready bvo_done bvo_ready f1T_done wf1_hi_ready wf1_ready f2T_done wf2_hi_ready
            wf2_ready abs_summed abs_tot_done theta_ready fc_low fc_tern pj_low pj_tern fcT_done wfc_ready pjT_done
            wpj_ready cpj_done rows_ready select_ready rows_spread cpj_ready v_ones_ready
            ln1_bn ln1_mv ln1_ve ln1_rs u_ready tu_done u_hi u_lo qk_done qk_minmax qk_exp_ready qk_ready
            qk_hi_ready qk_lo_ready v_done v_ready v_hi_ready v_lo_ready s_done a_hi_diag a_hi_off
            a_lo_ready a_lo_masked av_done den_ready rden_ready n1_ready n1o_ready xa_ready
            ln2_bn ln2_mv ln2_ve ln2_rs z2_ready tz2_done z2_hi z2_lo xpb_ready xs_ready
            f1_done h_gelu h_hi_ready h_lo_even h_lo_odd f2_step y_ready
            ln3_bn ln3_mv ln3_ve ln3_rs z3_ready tz3_done z3_hi z3_lo
            fc_done h3_gelu hsum_step hsum_last sq_ready sqsum_step g_hi_ready g_lo_ready
            pj_step var_done moments var_ready scale_ready corrected rs3_ready yc_ready out_ready out_stored fence_done""".split()
        s = {n: sem(n) for n in names}

        block = ctx.enter_context(nc.Block())

        def steps(engine, body):
            for i in range(-1, 3):
                body(i)
            with engine.Fori(3, G - 2) as i:
                body(i)
            for i in range(G - 2, G + 1):
                body(i)

        def groups(i):
            g = [i + 1, i, i - 1, i - 2]
            if not isinstance(i, int):
                return g
            return [n if 0 <= n < G else None for n in g]

        def is_step(i, n):
            return isinstance(i, int) and i == n

        def fc_bank(g, m):
            return bank[("c", "f0", "f1")[m % 3] if is_step(g, G - 1) else "c"]

        def moment_bank(g):
            return bank["x" if is_step(g, G - 1) or is_step(g, G - 2) else "c"]

        def following(i):
            return i + 2 if not isinstance(i, int) or i + 2 < G else None

        @block.sync
        def _(sp):
            def load_rows(rows, column, done):
                for src, c in rows:
                    n = src.shape[0] // P
                    sp.dma_start(column[c:c + n, :], src.rearrange("(r p) -> r p", p=P)).then_inc(s[done], 16)

            def load_wide(dst, src, done):
                sp.dma_start(dst, src.rearrange("(r d) -> r d", r=1).to_broadcast([P, D])).then_inc(s[done], 16)

            sp.dma_start(x_sb[:], group_rows(x_flat, 0)).then_inc(s["x_loaded"], 16)
            load_rows([(ln1_w, 0), (v_b, 2)], vec_rows, "rows_loaded")
            sp.dma_start(vec_rows[4:5, 0:FQ], q_b.rearrange("(r p) -> r p", r=1)).then_inc(s["rows_loaded"], 16)
            sp.dma_start(vec_rows[4:5, FQ:P], k_b.rearrange("(r p) -> r p", r=1)).then_inc(s["rows_loaded"], 16)
            sp.dma_start(qk_raw[0:FQ, :], q_w).then_inc(s["qk_raw_loaded"], 16)
            sp.dma_start(qk_raw[FQ:P, :], k_w).then_inc(s["qk_raw_loaded"], 16)
            load_wide(ln1b_b, ln1_b, "ln1b_loaded")
            sp.dma_start(wo_raw, o_w.rearrange("(k p) d -> p k d", p=P)).then_inc(s["v_raw_loaded"], 16)
            sp.dma_start(wv_raw, v_w.rearrange("(k p) d -> p k d", p=P)).then_inc(s["v_raw_loaded"], 16)
            load_rows([(ln2_w, 0), (f1_b, 2), (ln3_w, 10), (ln3_b, 18)], late_rows, "late_rows_loaded")
            sp.dma_start(f1_raw, f1_w.rearrange("(m p) d -> p m d", p=P)).then_inc(s["f1_raw_loaded"], 16)
            load_wide(ob_b[:], o_b, "ob_loaded")
            load_wide(f2b_b[:], f2_b, "ob_loaded")
            load_wide(ln2b_b, ln2_b, "ln2b_loaded")
            sp.dma_start(f2_raw, f2_w.rearrange("(k p) h -> p k h", p=P)).then_inc(s["f2_raw_loaded"], 16)
            sp.dma_start(fc_raw, fc_w.rearrange("(m p) d -> p m d", p=P)).then_inc(s["fc_raw_loaded"], 16)
            sp.dma_start(pj_raw, pj_w.rearrange("(k p) h -> p k h", p=P)).then_inc(s["pj_raw_loaded"], 16)

            def load_x(g):
                offset = sp.snap(g * (N * D)) if not isinstance(g, int) else g * N * D
                if not isinstance(g, int):
                    n1_count, xpb_count = sp.snap(4 * g), sp.snap(g + 0)
                sp.wait_ge(s["n1_ready"], 4 * g if isinstance(g, int) else n1_count)
                sp.wait_ge(s["xpb_ready"], g if isinstance(g, int) else xpb_count)
                sp.dma_start(x_sb[:], group_rows(x_flat, offset)).then_inc(s["x_loaded"], 16)

            def store(g):
                offset = sp.snap(g * (N * D)) if not isinstance(g, int) else g * N * D
                sp.wait_ge(s["out_ready"], 4 * g + 4)
                sp.dma_start(group_rows(out_flat, offset), out_sb).then_inc(s["out_stored"], 16)

            def body(i):
                at, ml, fc, pj = groups(i)
                if following(i) is not None:
                    load_x(i + 2)
                if pj is not None:
                    store(pj)

            steps(sp, body)
            store(G - 1)
            sp.wait_ge(s["out_stored"], 16 * G)

        @block.tensor
        def _(pe):
            def split3(ps, w, r, start, stop, skip=False):
                pe.matmul(ps, w[0], r[0], start=start, stop=False, skip_group_check=skip)
                pe.matmul(ps, w[0], r[1], start=False, stop=False, skip_group_check=skip)
                return pe.matmul(ps, w[1], r[0], start=False, stop=stop, skip_group_check=skip)

            def flip(src, banks, k):
                for t in range(T):
                    mm = pe.transpose(banks[:, t * P:(t + 1) * P], src[:, t, k * P:(k + 1) * P], ident[:])
                return mm

            def prep_small():
                pe.wait_ge(s["consts_ready"], 3)
                pe.wait_ge(s["rows_loaded"], 16 * 4)
                pe.transpose(bank["p0"][:, 0:5], vec_rows, ident[0:5, 0:5]).then_inc(s["vec_t"], 1)
                pe.wait_ge(s["qk_raw_loaded"], 32)
                for k in range(KD):
                    mm = pe.transpose(bank["p1"][:, k * P:(k + 1) * P], qk_raw[:, k * P:(k + 1) * P], ident[:])
                mm.then_inc(s["qkT_done"], 1)
                pe.wait_ge(s["v_raw_loaded"], 32)
                for k in range(KD):
                    for e in range(KD):
                        mm = pe.transpose(bank["y0"][:, k * D + e * P:k * D + (e + 1) * P],
                                          wo_raw[:, e, k * P:(k + 1) * P], ident[:])
                mm.then_inc(s["woT_done"], 1)

            def prep_late_vec():
                pe.wait_ge(s["late_rows_loaded"], 16 * 4)
                pe.transpose(bank["f0"][:, 0:26], late_rows, ident[0:26, 0:26]).then_inc(s["late_vec_t"], 1)

            def prep_vo():
                pe.wait_ge(s["woT_ready"], 1)
                for c in range(KD):
                    for k in range(KD):
                        mm = pe.matmul(bank["y1"][:, c * D:(c + 1) * D], wv_raw[:, k, c * P:(c + 1) * P],
                                       woT[:, k, :], start=(k == 0), stop=(k == KD - 1))
                mm.then_inc(s["wvo_done"], 1)
                pe.wait_ge(s["vb_wide_ready"], KD)
                pe.wait_ge(s["vec_ready"], 1)
                for k in range(KD):
                    mm = pe.matmul(bank["p0"][:, 0:D], vb_wide[:, k, :], woT[:, k, :],
                                   start=(k == 0), stop=(k == KD - 1))
                mm.then_inc(s["bvo_done"], 1)

            def prep_f1(n):
                k, half = n // 2, n % 2
                b = bank[("f0", "f1")[half]]
                if n == 0:
                    pe.wait_ge(s["f1_raw_loaded"], 16)
                    pe.wait_ge(s["late_vec_ready"], 1)
                if n >= 2:
                    pe.wait_ge(s["wf1_ready"], n - 1)
                for m in range(4):
                    mm = pe.transpose(b[:, m * P:(m + 1) * P], f1_raw[:, 4 * half + m, k * P:(k + 1) * P], ident[:])
                mm.then_inc(s["f1T_done"], 1)

            def prep_f2(n):
                b = bank[("y0", "y1")[n % 2]]
                if n == 0:
                    pe.wait_ge(s["f2_raw_loaded"], 16)
                    pe.wait_ge(s["woT_ready"], 1)
                if n == 1:
                    pe.wait_ge(s["wvo_ready"], 1)
                if n >= 2:
                    pe.wait_ge(s["wf2_ready"], n - 1)
                for q in range(4):
                    k, e = 2 * n + q // 2, q % 2
                    mm = pe.transpose(b[:, q * P:(q + 1) * P], f2_raw[:, e, k * P:(k + 1) * P], ident[:])
                mm.then_inc(s["f2T_done"], 1)

            def prep_theta():
                pe.wait_ge(s["abs_summed"], 8)
                pe.wait_ge(s["z2_lo"], 2)
                pe.matmul(bank["p1"][:, 0:8], mean_w[:], abs_sum[:], start=True, stop=True).then_inc(s["abs_tot_done"], 1)

            def prep_fc(n):
                k, half = n // 2, n % 2
                b = bank[("p0", "p1")[half]]
                if n == 0:
                    pe.wait_ge(s["fc_tern"], 1)
                    pe.wait_ge(s["xa_ready"], 4)
                if n == 1:
                    pe.wait_ge(s["theta_ready"], 1)
                if n >= 2:
                    pe.wait_ge(s["wfc_ready"], n - 1)
                for m in range(4):
                    mm = pe.transpose(b[:, m * P:(m + 1) * P], fc_raw[:, 4 * half + m, k * P:(k + 1) * P], ident[:])
                mm.then_inc(s["fcT_done"], 1)

            def prep_pj(n):
                b = bank[("p0", "p1")[n % 2]]
                if n == 0:
                    pe.wait_ge(s["pj_tern"], 1)
                if n < 2:
                    pe.wait_ge(s["wfc_ready"], n + 3)
                else:
                    pe.wait_ge(s["wpj_ready"], n - 1)
                for q in range(4):
                    k, e = 2 * n + q // 2, q % 2
                    mm = pe.transpose(b[:, q * P:(q + 1) * P], pj_raw[:, e, k * P:(k + 1) * P], ident[:])
                mm.then_inc(s["pjT_done"], 1)

            def prep_cpj(k):
                if k == 0:
                    pe.wait_ge(s["wpj_ready"], 4)
                    pe.wait_ge(s["late_vec_ready"], 1)
                pe.matmul(bank["p0"][0:2, 0:D], vec[:, 15 + k:24 + k:8], wpj[:, k, :].bitcast(F32),
                          start=(k == 0), stop=(k == KH - 1)).then_inc(s["cpj_done"], 1)

            def prep_spread():
                pe.wait_ge(s["rows_ready"], 1)
                pe.wait_ge(s["select_ready"], 2)
                for r in range(2):
                    mm = pe.matmul(bank["p0"][:, r * D:(r + 1) * D], row_select[:, r, :], pj_rows,
                                   start=True, stop=True)
                mm.then_inc(s["rows_spread"], 1)

            def tu(g, k, pj):
                if g is None:
                    return
                pe.wait_ge(s["u_ready"], 4 * g + 4)
                if k == 0 and later(g, 1):
                    pe.wait_ge(s["z2_lo"], 2 * (g - 1) + 1)
                if k == 1 and pj is not None:
                    pe.wait_ge(s["h3_gelu"], 8 * pj + 8)
                elif k == 1 and later(g, 1):
                    pe.wait_ge(s["a_lo_ready"], 4 * (g - 1) + 2)
                flip(u, bank[("x", "c")[k]], k).then_inc(s["tu_done"], 1)

            def qk_proj(g):
                if g is None:
                    return
                pe.wait_ge(s["u_lo"], 2 * g + 2)
                pe.wait_ge(s["u_hi"], 2 * g + 2)
                if isinstance(g, int) and g == 0:
                    pe.wait_ge(s["wqk_ready"], 1)
                for k in range(KD):
                    mm = split3(bank["x"][:], [w[:, k, :] for w in wqk], [r[:, k, :] for r in uT],
                                k == 0, k == KD - 1)
                mm.then_inc(s["qk_done"], 1)

            def v_proj(g, half, fc):
                if g is None:
                    return
                if half == 0 and isinstance(g, int) and g == 0:
                    pe.wait_ge(s["wvo_ready"], 1)
                if fc is not None:
                    pe.wait_ge(s["z3_lo"], 2 * fc + half + 1)
                elif half == 0:
                    pe.wait_ge(s["qk_minmax"], 2 * g + 2)
                b = bank[("x", "c")[half]]
                for j in range(2):
                    t = 2 * half + j
                    for k in range(KD):
                        mm = split3(b[:, j * D:(j + 1) * D], [r[:, k, t * P:(t + 1) * P] for r in uT],
                                    [w[:, k, :] for w in wvo], k == 0, k == KD - 1)
                mm.then_inc(s["v_done"], 1)

            def scores(g, half):
                if g is None:
                    return
                if half == 0:
                    pe.wait_ge(s["qk_lo_ready"], 2 * g + 2)
                    pe.wait_ge(s["qk_hi_ready"], 3 * g + 3)
                for j, b, c0, q0 in ((0, "x", 0, 0), (1, "c", 0, P), (2, "x", 0, 2 * P), (3, "x", 2 * P, 2 * P))[2 * half:2 * half + 2]:
                    if j < 2:
                        pe.wait_ge(s["v_ready"], 2 * g + j + 1)
                    if j == 2:
                        pe.wait_ge(s["a_lo_ready"], 4 * g + 1)
                    ps = bank[b][:, c0:c0 + N - q0]
                    pe.matmul(ps, k_stack[:, j * P:(j + 1) * P], q_stack[:, q0:], start=True, stop=False)
                    mm = pe.matmul(ps, k_lo[:, j * P:(j + 1) * P], q_stack[0:FQ, q0:], start=False, stop=True)
                    if j != 2:
                        mm.then_inc(s["s_done"], 1)

            def attend(g, t, pj):
                if g is None:
                    return
                if t == 0:
                    pe.wait_ge(s["v_lo_ready"], 2 * g + 2)
                    pe.wait_ge(s["v_hi_ready"], 2 * g + 2)
                    pe.wait_ge(s["a_hi_diag"], 4 * g + 4)
                    pe.wait_ge(s["a_hi_off"], 3 * g + 3)
                    pe.wait_ge(s["a_lo_ready"], 4 * g + 4)
                    pe.wait_ge(s["a_lo_masked"], g + 1)
                    if isinstance(g, int) and g == 0:
                        pe.wait_ge(s["v_ones_ready"], 3)
                if t < 2 and pj is not None:
                    pe.wait_ge(s["out_ready"], 4 * pj + 2 * t + 2)
                elif t < 2 and isinstance(g, int) and g == 0:
                    pe.wait_ge(s[("bvo_ready", "wqk_ready")[t]], 1)
                elif t < 2 and isinstance(g, int) and g == 1:
                    pe.wait_ge(s[("cpj_ready", "wpj_ready")[t]], (1, 4)[t])
                elif t == 0:
                    pe.wait_ge(s["xa_ready"], 4 * (g - 1) + 4)
                elif t == 1:
                    pe.wait_ge(s["z2_lo"], 2 * (g - 1) + 2)
                elif t == 3:
                    pe.wait_ge(s["xa_ready"], 4 * g + 1)
                b = bank[("p0", "p1", "x", "p0")[t]]
                for j in range(t + 1):
                    mm = split3(b[:, 0:VW], [w[:, j, (t - j) * P:(t - j + 1) * P] for w in a],
                                [r[:, j, :] for r in v], j == 0, j == t)
                mm.then_inc(s["av_done"], 1)

            def tz2(g, k):
                if g is None:
                    return
                pe.wait_ge(s["z2_ready"], 4 * g + 4)
                pe.wait_ge(s["xa_ready"], 4 * g + (3 if k == 0 else 2))
                flip(z, bank[("x", "p1")[k]], k).then_inc(s["tz2_done"], 1)

            def f1(g, m):
                if g is None:
                    return
                if m == 0:
                    pe.wait_ge(s["z2_lo"], 2 * g + 2)
                    pe.wait_ge(s["z2_hi"], 2 * g + 2)
                    if isinstance(g, int) and g == 0:
                        pe.wait_ge(s["wf1_ready"], 4)
                if later(g, 1) or m >= 2:
                    pe.wait_ge(s["h_gelu"], 8 * g + m - 1)
                for k in range(KD):
                    mm = split3(bank[("f0", "f1")[m % 2]][:], [w[:, k, m * P:(m + 1) * P] for w in wf1],
                                [r[:, k, :] for r in z2T], k == 0, k == KD - 1)
                mm.then_inc(s["f1_done"], 1)

            def f2(g, k):
                if g is None:
                    return
                if k == 0:
                    if later(g, 1):
                        pe.wait_ge(s["y_ready"], 2 * (g - 1) + 2)
                    if isinstance(g, int) and g == 0:
                        pe.wait_ge(s["wf2_ready"], 4)
                pe.wait_ge(s["h_lo_odd" if k % 2 else "h_lo_even"], 4 * g + k // 2 + 1)
                pe.wait_ge(s["h_hi_ready"], 8 * g + k + 1)
                for t in range(T):
                    ps = bank[("y0", "y1")[t // 2]][:, (t % 2) * D:(t % 2 + 1) * D]
                    mm = split3(ps, [r[:, k % 3, t * P:(t + 1) * P] for r in hr], [w[:, k, :] for w in wf2],
                                k == 0 and t % 2 == 0, k == KH - 1, skip=True)
                mm.then_inc(s["f2_step"], 1)

            def tz3(g, k, at, pj):
                if g is None:
                    return
                pe.wait_ge(s["z3_ready"], 4 * g + 4)
                if at is not None and k == 0:
                    pe.wait_ge(s["qk_minmax"], 2 * at + 2)
                elif at is not None:
                    pe.wait_ge(s["u_lo"], 2 * at + 2)
                elif k == 0 and later(g, G - 1):
                    pe.wait_ge(s["z3_lo"], 2 * (g - 1) + 1)
                elif k == 0:
                    pe.wait_ge(s["z2_lo"], 2 * (g + 1) + 1)
                else:
                    pe.wait_ge(s["h3_gelu"], 8 * pj + 8)
                flip(z, bank[("x", "c")[k]], k).then_inc(s["tz3_done"], 1)

            def fc_up(g, m, at, pj):
                if g is None:
                    return
                if m == 0:
                    pe.wait_ge(s["z3_lo"], 2 * g + 2)
                    pe.wait_ge(s["z3_hi"], 2 * g + 2)
                    if isinstance(g, int) and g == 0:
                        pe.wait_ge(s["wfc_ready"], 4)
                    if at is not None:
                        pe.wait_ge(s["a_lo_ready"], 4 * at + 2)
                if is_step(g, G - 1):
                    if m in (1, 2):
                        pe.wait_ge(s["h_gelu"], 8 * g + m + 6)
                    if m >= 3:
                        pe.wait_ge(s["h3_gelu"], 8 * g + m - 2)
                elif m >= 1:
                    pe.wait_ge(s["h3_gelu"], 8 * g + m)
                if m == 1 and pj is not None and not is_step(g, G - 1):
                    pe.wait_ge(s["var_ready"], pj + 1)
                b = fc_bank(g, m)
                for k in range(KD):
                    for part in range(2):
                        mm = pe.matmul(b[:], wfc[:, k, m * P:(m + 1) * P], z3T[part][:, k, :],
                                       start=(k == 0 and part == 0), stop=(k == KD - 1 and part == 1))
                mm.then_inc(s["fc_done"], 1)

            def proj(g, k, ml):
                if g is None:
                    return
                if k == 0:
                    if isinstance(g, int) and g == 0:
                        pe.wait_ge(s["wpj_ready"], 4)
                    if ml is not None:
                        pe.wait_ge(s["xa_ready"], 4 * ml + 4)
                        pe.wait_ge(s["z2_lo"], 2 * ml + 2)
                    else:
                        pe.wait_ge(s["out_ready"], 4 * (g - 1) + 4)
                pe.wait_ge(s["g_lo_ready"], 8 * g + k + 1)
                pe.wait_ge(s["g_hi_ready"], 8 * g + k + 1)
                for t in range(T):
                    ps = bank[("p0", "p1")[t // 2]][:, (t % 2) * D:(t % 2 + 1) * D]
                    for part in range(2):
                        mm = pe.matmul(ps, gr[part][:, k % 2, t * P:(t + 1) * P], wpj[:, k, :],
                                       start=(k == 0 and t % 2 == 0 and part == 0), stop=(k == KH - 1 and part == 1),
                                       skip_group_check=True)
                mm.then_inc(s["pj_step"], 1)

            def var(g, fc):
                if g is None:
                    return
                pe.wait_ge(s["sqsum_step"], 7 * g + 7)
                if is_step(g, G - 1):
                    pe.wait_ge(s["hsum_last"], 7)
                else:
                    pe.wait_ge(s["hsum_step"], 7 * g + 7)
                if is_step(g, G - 1):
                    pe.wait_ge(s["var_ready"], g)
                elif is_step(g, G - 2):
                    pe.wait_ge(s["z3_lo"], 2 * fc + 1)
                else:
                    pe.wait_ge(s["h3_gelu"], 8 * fc + 1)
                b = moment_bank(g)
                for n, src in enumerate((sqsum, hsum)):
                    for t in range(T):
                        mm = pe.matmul(b[:, n * T + t:n * T + t + 1], src[:, t * P:(t + 1) * P], mean_w[:, 0:1],
                                       start=True, stop=True)
                mm.then_inc(s["var_done"], 1)

            def body(i):
                at, ml, fc, pj = groups(i)
                if is_step(i, -1):
                    prep_small(); prep_late_vec(); tu(at, 0, pj); tu(at, 1, pj); prep_vo(); qk_proj(at)
                    prep_f1(0); prep_f1(1); prep_f2(0); prep_f2(1); v_proj(at, 0, fc); v_proj(at, 1, fc)
                    scores(at, 0); scores(at, 1); prep_f1(2); attend(at, 0, pj); attend(at, 1, pj)
                    attend(at, 2, pj); attend(at, 3, pj); prep_f2(2); prep_f1(3); prep_f2(3); tz2(at, 0)
                    tz2(at, 1)
                elif is_step(i, 0):
                    tu(at, 0, pj); tu(at, 1, pj); f1(ml, 0); f1(ml, 1); f1(ml, 2); f1(ml, 3); qk_proj(at)
                    f1(ml, 4); f2(ml, 0); prep_theta(); v_proj(at, 0, fc); v_proj(at, 1, fc); f2(ml, 1)
                    f1(ml, 5); prep_fc(0); prep_fc(1); f2(ml, 2); prep_fc(2); prep_fc(3); f1(ml, 6); prep_pj(0)
                    prep_pj(1); f2(ml, 3); prep_pj(2); prep_pj(3); scores(at, 0); prep_cpj(0); prep_cpj(1)
                    prep_cpj(2); prep_cpj(3); prep_cpj(4); prep_cpj(5); scores(at, 1); prep_cpj(6); prep_cpj(7)
                    prep_spread(); attend(at, 0, pj); attend(at, 1, pj); attend(at, 2, pj); attend(at, 3, pj)
                    f1(ml, 7); f2(ml, 4); f2(ml, 5); f2(ml, 6); tz2(at, 0); tz2(at, 1); f2(ml, 7)
                elif is_step(i, G - 1):
                    f1(ml, 0); proj(pj, 0, ml); f1(ml, 1); proj(pj, 1, ml); f1(ml, 2); f1(ml, 3)
                    tz3(fc, 0, at, pj); tz3(fc, 1, at, pj); f2(ml, 0); f1(ml, 4); proj(pj, 2, ml); f2(ml, 1)
                    fc_up(fc, 0, at, pj); f2(ml, 2); proj(pj, 3, ml); var(pj, fc); f1(ml, 5)
                    fc_up(fc, 1, at, pj); proj(pj, 4, ml); proj(pj, 5, ml); fc_up(fc, 2, at, pj); f1(ml, 6)
                    fc_up(fc, 3, at, pj); f2(ml, 3); fc_up(fc, 4, at, pj); proj(pj, 6, ml); fc_up(fc, 5, at, pj)
                    proj(pj, 7, ml); fc_up(fc, 6, at, pj); f1(ml, 7); fc_up(fc, 7, at, pj); f2(ml, 4); f2(ml, 5)
                    f2(ml, 6); f2(ml, 7)
                elif is_step(i, G):
                    proj(pj, 0, ml); proj(pj, 1, ml); proj(pj, 2, ml); proj(pj, 3, ml); tz3(fc, 0, at, pj)
                    tz3(fc, 1, at, pj); proj(pj, 4, ml); proj(pj, 5, ml); fc_up(fc, 0, at, pj)
                    fc_up(fc, 1, at, pj); var(pj, fc); fc_up(fc, 2, at, pj); proj(pj, 6, ml); proj(pj, 7, ml)
                    fc_up(fc, 3, at, pj); fc_up(fc, 4, at, pj); fc_up(fc, 5, at, pj); fc_up(fc, 6, at, pj)
                    proj(G - 1, 0, ml); proj(G - 1, 1, ml); fc_up(fc, 7, at, pj); proj(G - 1, 2, ml)
                    proj(G - 1, 3, ml); proj(G - 1, 4, ml); var(G - 1, fc); proj(G - 1, 5, ml)
                    proj(G - 1, 6, ml); proj(G - 1, 7, ml)
                else:
                    tu(at, 0, pj); f1(ml, 0); proj(pj, 0, ml); tu(at, 1, pj); proj(pj, 1, ml); f1(ml, 1)
                    f1(ml, 2); proj(pj, 2, ml); qk_proj(at); proj(pj, 3, ml); f1(ml, 3); tz3(fc, 0, at, pj)
                    tz3(fc, 1, at, pj); proj(pj, 4, ml); f2(ml, 0); v_proj(at, 0, fc); proj(pj, 5, ml)
                    f2(ml, 1); v_proj(at, 1, fc); f1(ml, 4); scores(at, 0); f2(ml, 2); f1(ml, 5)
                    fc_up(fc, 0, at, pj); proj(pj, 6, ml); scores(at, 1); var(pj, fc); proj(pj, 7, ml)
                    f1(ml, 6); fc_up(fc, 1, at, pj); f2(ml, 3); f1(ml, 7); fc_up(fc, 2, at, pj)
                    attend(at, 0, pj); attend(at, 1, pj); fc_up(fc, 3, at, pj); attend(at, 2, pj)
                    fc_up(fc, 4, at, pj); attend(at, 3, pj); fc_up(fc, 5, at, pj); f2(ml, 4)
                    fc_up(fc, 6, at, pj); f2(ml, 5); fc_up(fc, 7, at, pj); tz2(at, 0); tz2(at, 1); f2(ml, 6)
                    f2(ml, 7)

            steps(pe, body)

        @block.scalar
        def _(act):
            def prep_wo():
                act.wait_ge(s["woT_done"], 1)
                act.activation(woT[:].rearrange("p k d -> p (k d)"), bank["y0"][:], ACT.Copy).then_inc(s["woT_ready"], 1)

            def prep_wqk():
                act.wait_ge(s["qkT_done"], 1)
                act.wait_ge(s["vec_ready"], 1)
                for k in range(KD):
                    act.activation(wqk[0][:, k, :], bank["p1"][:, k * P:(k + 1) * P], ACT.Copy,
                                   scale=ln1w_c[:, k:k + 1]).then_inc(s["wqk_hi_ready"], 1)

            def prep_wvo():
                act.wait_ge(s["wvo_done"], 1)
                act.wait_ge(s["vec_ready"], 1)
                for k in range(KD):
                    act.activation(wvo[0][:, k, :], bank["y1"][:, k * D:(k + 1) * D], ACT.Copy,
                                   scale=ln1w_c[:, k:k + 1]).then_inc(s["wvo_hi_ready"], 1)

            def prep_bvo():
                act.wait_ge(s["bvo_done"], 1)
                act.activation(bvo_b[:], bank["p0"][:, 0:D], ACT.Copy).then_inc(s["bvo_ready"], 1)

            def prep_f1(n):
                k, half = n // 2, n % 2
                act.wait_ge(s["f1T_done"], n + 1)
                if n == 0:
                    act.wait_ge(s["late_vec_ready"], 1)
                act.activation(wf1[0][:, k, half * 512:(half + 1) * 512], bank[("f0", "f1")[half]][:], ACT.Copy,
                               scale=ln2w_c[:, k:k + 1]).then_inc(s["wf1_hi_ready"], 1)

            def prep_f2(n):
                act.wait_ge(s["f2T_done"], n + 1)
                act.activation(wf2[0][:, 2 * n:2 * n + 2, :].rearrange("p k d -> p (k d)"),
                               bank[("y0", "y1")[n % 2]][:], ACT.Copy).then_inc(s["wf2_hi_ready"], 1)

            def prep_abs(n):
                if n == 0:
                    act.wait_ge(s["fc_raw_loaded"], 16)
                if n == 4:
                    act.wait_ge(s["pj_raw_loaded"], 16)
                if n:
                    act.wait_ge(s["abs_summed"], n)
                act.activation(abs_out[:], h3[:, n, :], ACT.Abs,
                               accum_out=abs_sum[:, n:n + 1]).then_inc(s["abs_summed"], 1)

            def prep_fc(n):
                k, half = n // 2, n % 2
                act.wait_ge(s["fcT_done"], n + 1)
                act.activation(wfc[:, k, half * 512:(half + 1) * 512], bank[("p0", "p1")[half]][:],
                               ACT.Copy).then_inc(s["wfc_ready"], 1)

            def prep_pj(n):
                act.wait_ge(s["pjT_done"], n + 1)
                act.activation(wpj[:, 2 * n:2 * n + 2, :].rearrange("p k d -> p (k d)"),
                               bank[("p0", "p1")[n % 2]][:], ACT.Copy).then_inc(s["wpj_ready"], 1)

            def prep_rows():
                act.wait_ge(s["cpj_done"], KH)
                act.wait_ge(s["abs_tot_done"], 1)
                act.activation(pj_rows, bank["p0"][0:2, 0:D], ACT.Copy).then_inc(s["rows_ready"], 1)

            def prep_cpj():
                act.wait_ge(s["rows_spread"], 1)
                act.activation(pj_rows_b[:].rearrange("p r d -> p (r d)"), bank["p0"][:], ACT.Copy).then_inc(s["cpj_ready"], 1)

            def u_hi(g, k):
                if g is None:
                    return
                if k == 0 and later(g, 1):
                    act.wait_ge(s["v_done"], 2 * (g - 1) + 2)
                act.wait_ge(s["tu_done"], 2 * g + k + 1)
                act.activation(uT[0][:, k, :], bank[("x", "c")[k]][:], ACT.Copy).then_inc(s["u_hi"], 1)

            def qk_e(g):
                if g is None:
                    return
                act.wait_ge(s["qk_minmax"], 2 * g + 2)
                act.activation(qk_exp, qk_exp, ACT.Exp).then_inc(s["qk_exp_ready"], 1)

            def qk_h(g):
                if g is None:
                    return
                act.wait_ge(s["qk_ready"], g + 1)
                if later(g, 1):
                    act.wait_ge(s["s_done"], 3 * (g - 1) + 3)
                act.activation(q_stack[0:FQ, :], qk[0:FQ, :], ACT.Copy).then_inc(s["qk_hi_ready"], 1)
                act.activation(k_stack[FQ:P, :], qk[FQ:P, :], ACT.Copy).then_inc(s["qk_hi_ready"], 1)
                act.activation(k_stack[0:FQ, :], qk[FQ:P, :], ACT.Copy).then_inc(s["qk_hi_ready"], 1)

            def v_h(g, half):
                if g is None:
                    return
                act.wait_ge(s["v_ready"], 2 * g + half + 1)
                if half == 0 and later(g, 1):
                    act.wait_ge(s["av_done"], 4 * (g - 1) + 4)
                act.activation(v[0][:, 2 * half:2 * half + 2, 0:D], v32[:], ACT.Copy).then_inc(s["v_hi_ready"], 1)

            def a_off(g, j):
                if g is None:
                    return
                if j == 0 and later(g, 1):
                    act.wait_ge(s["av_done"], 4 * (g - 1) + 4)
                w = N - (j + 1) * P
                act.wait_ge(s["a_hi_diag"], 4 * g + (j + 1 if j < 2 else 4))
                act.wait_ge(s["s_done"], 3 * g + j + 1)
                act.activation(a[0][:, j, P:P + w], bank[("x", "c", "x")[j]][:, P:P + w],
                               ACT.Copy).then_inc(s["a_hi_off"], 1)

            def z2_hi(g, k):
                if g is None:
                    return
                if k == 0 and later(g, 1):
                    act.wait_ge(s["f1_done"], 8 * (g - 1) + 8)
                act.wait_ge(s["tz2_done"], 2 * g + k + 1)
                act.activation(z2T[0][:, k, :], bank[("x", "p1")[k]][:], ACT.Copy).then_inc(s["z2_hi"], 1)

            def gelu(g, m):
                if g is None:
                    return
                act.wait_ge(s["f1_done"], 8 * g + m + 1)
                if m >= 3:
                    act.wait_ge(s["h_lo_odd" if (m - 3) % 2 else "h_lo_even"], 4 * g + (m - 3) // 2 + 1)
                elif later(g, 1):
                    act.wait_ge(s["h_lo_odd"], 4 * g)
                    act.wait_ge(s["h_lo_even"], 4 * g)
                if m == 0 and isinstance(g, int) and g == 0:
                    act.wait_ge(s["bias_done"], 3)
                act.activation(hring[:, m % 3, :], bank[("f0", "f1")[m % 2]][:], ACT.Gelu,
                               bias=f1_bias[:, m:m + 1]).then_inc(s["h_gelu"], 1)

            def h_hi(g, m):
                if g is None:
                    return
                act.wait_ge(s["h_gelu"], 8 * g + m + 1)
                if later(g, 1) or m >= 3:
                    act.wait_ge(s["f2_step"], 8 * g + (m - 2 if m >= 3 else 0))
                act.activation(hr[0][:, m % 3, :], hring[:, m % 3, :], ACT.Copy).then_inc(s["h_hi_ready"], 1)

            def z3_hi(g, k):
                if g is None:
                    return
                if k == 0 and later(g, 1):
                    act.wait_ge(s["fc_done"], 8 * (g - 1) + 8)
                act.wait_ge(s["tz3_done"], 2 * g + k + 1)
                act.activation(z3T[0][:, k, :], bank[("x", "c")[k]][:], ACT.Copy).then_inc(s["z3_hi"], 1)

            def gelu3(g, m):
                if g is None:
                    return
                act.wait_ge(s["fc_done"], 8 * g + m + 1)
                if later(g, 1):
                    act.wait_ge(s["g_lo_ready"], 8 * (g - 1) + m + 1)
                    act.wait_ge(s["g_hi_ready"], 8 * (g - 1) + m + 1)
                    act.wait_ge(s["sq_ready"], 8 * (g - 1) + m + 1)
                    act.wait_ge(s["hsum_step"], 7 * (g - 1) + max(m, 1))
                act.activation(h3[:, m, :], fc_bank(g, m)[:], ACT.Gelu).then_inc(s["h3_gelu"], 1)

            def g_hi(g, m):
                if g is None:
                    return
                act.wait_ge(s["h3_gelu"], 8 * g + m + 1)
                if later(g, 1) or m >= 2:
                    act.wait_ge(s["pj_step"], 8 * g + (m - 1 if m >= 2 else 0))
                act.activation(gr[0][:, m % 2, :], h3[:, m, :], ACT.Copy,
                               scale=ln3w_c[:, m:m + 1]).then_inc(s["g_hi_ready"], 1)

            def square(g, m):
                if g is None:
                    return
                act.wait_ge(s["h3_gelu"], 8 * g + m + 1)
                if later(g, 1) or m >= 2:
                    act.wait_ge(s["sqsum_step"], 7 * g + (max(m - 2, 1) if m >= 2 else 0))
                act.activation(sq[:, m % 2, :], h3[:, m, :], ACT.Square).then_inc(s["sq_ready"], 1)

            def body(i):
                at, ml, fc, pj = groups(i)
                if is_step(i, -1):
                    prep_wqk(); prep_wo(); u_hi(at, 0); u_hi(at, 1); prep_wvo(); prep_f1(0); qk_e(at)
                    prep_f1(1); prep_bvo(); qk_h(at); v_h(at, 0); a_off(at, 0); a_off(at, 1); v_h(at, 1)
                    a_off(at, 2); prep_f1(2); prep_f2(0); prep_f2(1); prep_f1(3); prep_f2(2); prep_f2(3)
                    z2_hi(at, 0); z2_hi(at, 1)
                elif is_step(i, 0):
                    prep_abs(0); prep_abs(1); gelu(ml, 0); u_hi(at, 0); prep_abs(2); gelu(ml, 1); u_hi(at, 1)
                    prep_abs(3); h_hi(ml, 0); gelu(ml, 2); prep_abs(4); prep_abs(5); prep_abs(6); prep_abs(7)
                    h_hi(ml, 1); h_hi(ml, 2); gelu(ml, 3); h_hi(ml, 3); qk_e(at); gelu(ml, 4); prep_fc(0)
                    prep_fc(1); gelu(ml, 5); v_h(at, 0); prep_fc(2); prep_fc(3); qk_h(at); prep_pj(0)
                    prep_pj(1); prep_pj(2); prep_pj(3); v_h(at, 1); h_hi(ml, 4); a_off(at, 0); a_off(at, 1)
                    gelu(ml, 6); h_hi(ml, 5); a_off(at, 2); prep_rows(); prep_cpj(); h_hi(ml, 6); gelu(ml, 7)
                    h_hi(ml, 7); z2_hi(at, 0); z2_hi(at, 1)
                elif is_step(i, G - 1):
                    g_hi(pj, 0); g_hi(pj, 1); square(pj, 0); square(pj, 1); gelu(ml, 0); square(pj, 2)
                    gelu(ml, 1); h_hi(ml, 0); g_hi(pj, 2); h_hi(ml, 1); g_hi(pj, 3); square(pj, 3)
                    square(pj, 4); gelu(ml, 2); h_hi(ml, 2); z3_hi(fc, 0); z3_hi(fc, 1); square(pj, 5)
                    square(pj, 6); gelu(ml, 3); square(pj, 7); gelu3(fc, 0); g_hi(pj, 4); h_hi(ml, 3)
                    gelu(ml, 4); h_hi(ml, 4); g_hi(pj, 5); gelu3(fc, 1); gelu(ml, 5); g_hi(pj, 6); g_hi(pj, 7)
                    gelu3(fc, 2); gelu(ml, 6); gelu3(fc, 3); h_hi(ml, 5); gelu3(fc, 4); h_hi(ml, 6)
                    gelu3(fc, 5); gelu3(fc, 6); gelu3(fc, 7); gelu(ml, 7); h_hi(ml, 7)
                elif is_step(i, G):
                    g_hi(pj, 0); square(pj, 0); square(pj, 1); g_hi(pj, 1); square(pj, 2); g_hi(pj, 2)
                    square(pj, 3); g_hi(pj, 3); square(pj, 4); g_hi(pj, 4); square(pj, 5); g_hi(pj, 5)
                    square(pj, 6); z3_hi(fc, 0); z3_hi(fc, 1); square(pj, 7); g_hi(pj, 6); g_hi(pj, 7)
                    gelu3(fc, 0); gelu3(fc, 1); square(G - 1, 0); square(G - 1, 1); gelu3(fc, 2); g_hi(G - 1, 0)
                    square(G - 1, 2); gelu3(fc, 3); g_hi(G - 1, 1); square(G - 1, 3); gelu3(fc, 4); gelu3(fc, 5)
                    square(G - 1, 4); gelu3(fc, 6); g_hi(G - 1, 2); square(G - 1, 5); g_hi(G - 1, 3)
                    square(G - 1, 6); gelu3(fc, 7); g_hi(G - 1, 4); square(G - 1, 7); g_hi(G - 1, 5)
                    g_hi(G - 1, 6); g_hi(G - 1, 7)
                else:
                    g_hi(pj, 0); square(pj, 0); square(pj, 1); u_hi(at, 0); g_hi(pj, 1); gelu(ml, 0)
                    g_hi(pj, 2); h_hi(ml, 0); g_hi(pj, 3); square(pj, 2); u_hi(at, 1); square(pj, 3)
                    gelu(ml, 1); square(pj, 4); g_hi(pj, 4); gelu(ml, 2); h_hi(ml, 1); qk_e(at); z3_hi(fc, 0)
                    z3_hi(fc, 1); g_hi(pj, 5); square(pj, 5); g_hi(pj, 6); qk_h(at); h_hi(ml, 2); v_h(at, 0)
                    gelu(ml, 3); square(pj, 6); g_hi(pj, 7); v_h(at, 1); a_off(at, 0); a_off(at, 1); gelu(ml, 4)
                    h_hi(ml, 3); square(pj, 7); h_hi(ml, 4); gelu3(fc, 0); gelu(ml, 5); a_off(at, 2)
                    gelu(ml, 6); gelu3(fc, 1); h_hi(ml, 5); gelu3(fc, 2); gelu3(fc, 3); h_hi(ml, 6)
                    gelu3(fc, 4); gelu(ml, 7); gelu3(fc, 5); gelu3(fc, 6); h_hi(ml, 7); gelu3(fc, 7)
                    z2_hi(at, 0); z2_hi(at, 1)

            steps(act, body)

        @block.vector
        def _(dve):
            def consts():
                dve.memset(mean_w[:], 1.0 / H).then_inc(s["consts_ready"], 1)
                dve.memset(neg_half[:], -0.5)
                dve.memset(v[0][:, :, D:D + 1].bitcast(F32), 1.0).then_inc(s["v_ones_ready"], 1)
                dve.memset(v[0][:, :, D + 1:VW].bitcast(F32), 0.0).then_inc(s["v_ones_ready"], 1)
                dve.memset(v[1][:, :, D:VW].bitcast(F32), 0.0).then_inc(s["v_ones_ready"], 1)

            def prep_vec():
                dve.wait_ge(s["vec_t"], 1)
                dve.tensor_copy(vec[:, 0:5], bank["p0"][:, 0:5]).then_inc(s["vec_ready"], 1)

            def prep_late_vec():
                dve.wait_ge(s["late_vec_t"], 1)
                dve.tensor_copy(vec[:, 5:31], bank["f0"][:, 0:26]).then_inc(s["late_vec_ready"], 1)

            def prep_dots():
                dve.wait_ge(s["vec_ready"], 1)
                dve.wait_ge(s["ln1b_loaded"], 16)
                for n, (src, col) in enumerate(((qk_raw, 10), (wv_raw[:, 0, :], 8), (wv_raw[:, 1, :], 9))):
                    if n:
                        dve.wait_ge(s["dots_done"], n)
                    dve.wait_ge(s["v_raw_loaded" if n else "qk_raw_loaded"], 32)
                    dve.tensor_tensor_reduce(dot_out, src, ln1b_b, 1.0, 0.0, ALU.mult, ALU.add,
                                             dots[:, col:col + 1]).then_inc(s["dots_done"], 1)
                dve.wait_ge(s["dots_done"], 3)
                dve.tensor_tensor(vb_full[:], dots[:, 8:10], vb_c, ALU.add).then_inc(s["bias_done"], 1)
                dve.tensor_tensor(qk_bias[:], dots[:, 10:11], qkb_c, ALU.add).then_inc(s["bias_done"], 1)
                dve.wait_ge(s["bias_done"], 2)
                for k in range(KD):
                    dve.tensor_scalar(vb_wide[:, k, :], mean_w[:], 0.0, vb_full[:, k:k + 1],
                                      ALU.mult, ALU.add).then_inc(s["vb_wide_ready"], 1)

            def prep_wqk():
                dve.wait_ge(s["wqk_hi_ready"], 2)
                for k in range(KD):
                    mm = dve.scalar_tensor_tensor(wqk[1][:, k, :], bank["p1"][:, k * P:(k + 1) * P],
                                                  ln1w_c[:, k:k + 1], wqk[0][:, k, :].bitcast(F32),
                                                  ALU.mult, ALU.subtract)
                mm.then_inc(s["wqk_ready"], 1)

            def prep_wvo():
                dve.wait_ge(s["wvo_hi_ready"], 2)
                for k in range(KD):
                    mm = dve.scalar_tensor_tensor(wvo[1][:, k, :], bank["y1"][:, k * D:(k + 1) * D],
                                                  ln1w_c[:, k:k + 1], wvo[0][:, k, :].bitcast(F32),
                                                  ALU.mult, ALU.subtract)
                mm.then_inc(s["wvo_ready"], 1)

            def prep_f1(n):
                k, half = n // 2, n % 2
                dve.wait_ge(s["wf1_hi_ready"], n + 1)
                dve.scalar_tensor_tensor(wf1[1][:, k, half * 512:(half + 1) * 512],
                                         bank[("f0", "f1")[half]][:], ln2w_c[:, k:k + 1],
                                         wf1[0][:, k, half * 512:(half + 1) * 512].bitcast(F32),
                                         ALU.mult, ALU.subtract).then_inc(s["wf1_ready"], 1)

            def prep_f1_bias():
                dve.wait_ge(s["f1_raw_loaded"], 16)
                dve.wait_ge(s["ln2b_loaded"], 16)
                for m in range(KH):
                    dve.wait_ge(s["dots_done"], 3 + m)
                    dve.tensor_tensor_reduce(dot_out, f1_raw[:, m, :], ln2b_b, 1.0, 0.0, ALU.mult, ALU.add,
                                             dots[:, m:m + 1]).then_inc(s["dots_done"], 1)
                dve.wait_ge(s["dots_done"], 3 + KH)
                dve.wait_ge(s["late_vec_ready"], 1)
                dve.tensor_tensor(f1_bias[:], dots[:, 0:KH], f1b_c, ALU.add).then_inc(s["bias_done"], 1)

            def prep_f2(n):
                dve.wait_ge(s["wf2_hi_ready"], n + 1)
                dve.tensor_tensor(wf2[1][:, 2 * n:2 * n + 2, :].rearrange("p k d -> p (k d)"),
                                  bank[("y0", "y1")[n % 2]][:],
                                  wf2[0][:, 2 * n:2 * n + 2, :].rearrange("p k d -> p (k d)").bitcast(F32),
                                  ALU.subtract).then_inc(s["wf2_ready"], 1)

            def prep_theta():
                dve.wait_ge(s["abs_tot_done"], 1)
                dve.tensor_reduce(abs_tot[:], bank["p1"][:, 0:8].rearrange("p (w n) -> p w n", w=2),
                                  AXX, ALU.add).then_inc(s["theta_ready"], 1)
                dve.wait_ge(s["theta_ready"], 1)
                dve.tensor_scalar(theta[:, 0:2], abs_tot[:], 0.5 * H / (H * D), 0.5 * ABSMEAN_EPS,
                                  ALU.mult, ALU.add).then_inc(s["theta_ready"], 1)
                dve.wait_ge(s["theta_ready"], 2)
                dve.tensor_scalar(theta[:, 2:4], theta[:, 0:2], -1.0, None, ALU.mult).then_inc(s["theta_ready"], 1)

            def prep_tern(w):
                low, tern = (("fc_low", "fc_tern"), ("pj_low", "pj_tern"))[w]
                raw = h3[:, 4 * w:4 * w + 4, :].rearrange("p a n -> p (a n)")
                if w == 0:
                    dve.wait_ge(s["theta_ready"], 3)
                    dve.wait_ge(s["f1T_done"], 4)
                else:
                    dve.wait_ge(s["fc_tern"], 1)
                dve.tensor_scalar(tern_low, raw, theta[:, 2 + w:3 + w], None, ALU.is_lt).then_inc(s[low], 1)
                dve.wait_ge(s[low], 1)
                dve.scalar_tensor_tensor(raw, raw, theta[:, w:w + 1], tern_low,
                                         ALU.is_gt, ALU.subtract).then_inc(s[tern], 1)

            def prep_select():
                dve.wait_ge(s["consts_ready"], 3)
                dve.wait_ge(s["abs_summed"], 8)
                for r in range(2):
                    dve.tensor_scalar(row_select[:, r, :], mean_w[0:2, :], float(H), ident[0:2, r:r + 1],
                                      ALU.mult, ALU.mult).then_inc(s["select_ready"], 1)

            def stats(n, src, t, ready):
                dve.bn_stats(bn[n][:, t, :], src[:, t, :]).then_inc(s[f"ln{n + 1}_bn"], 1)

            def aggregate(n, g):
                if later(g, 1):
                    dve.wait_ge(s[f"ln{n + 1}_rs"], (g - 1) + 1)
                dve.wait_ge(s[f"ln{n + 1}_bn"], 4 * g + 4)
                dve.tensor_scalar(fence[:], mean_w[:, 0:1], 1.0, None, ALU.mult)
                for t in range(T):
                    dve.bn_aggr(mv[n][:, t, :], bn[n][:, t, :]).then_inc(s[f"ln{n + 1}_mv"], 1)
                dve.wait_ge(s[f"ln{n + 1}_mv"], 4 * g + 4)
                dve.tensor_scalar(ve[n][:, 0, :], mv[n][:, :, 1], 1.0, LN_EPS, ALU.mult, ALU.add).then_inc(s[f"ln{n + 1}_ve"], 1)
                if n == 0:
                    dve.tensor_scalar(ve[n][:, 1, :], mv[n][:, :, 1], 1.0 + LN_EPS, LN_EPS * LN_EPS,
                                      ALU.mult, ALU.add).then_inc(s["ln1_ve"], 1)

            def normalise(dst, src, n, t, row, ready):
                dve.tensor_scalar(dst[:, t, :], src[:, t, :], mv[n][:, t, 0:1], rs[n][:, row, t:t + 1],
                                  ALU.subtract, ALU.mult).then_inc(s[ready], 1)

            def ln1_stats(g):
                if g is None:
                    return
                dve.wait_ge(s["x_loaded"], 16 * g + 16)
                for t in range(T):
                    stats(0, x_sb, t, None)
                if later(g, 1):
                    dve.wait_ge(s["n1_ready"], 4 * (g - 1) + 4)
                aggregate(0, g)

            def ln1_u(g):
                if g is None:
                    return
                dve.wait_ge(s["ln1_rs"], g + 1)
                if later(g, 1):
                    dve.wait_ge(s["tu_done"], 2 * (g - 1) + 2)
                for t in range(T):
                    normalise(u, x_sb, 0, t, 1, "u_ready")

            def n1(g):
                if g is None:
                    return
                if later(g, 1):
                    dve.wait_ge(s["xs_ready"], (g - 1) + 1)
                dve.wait_ge(s["ln1_rs"], g + 1)
                for t in range(T):
                    normalise(xa, x_sb, 0, t, 0, "n1_ready")

            def lo_part(dst, b, hi, ready):
                dve.tensor_tensor(dst, b, hi.bitcast(F32), ALU.subtract).then_inc(s[ready], 1)

            def u_lo(g, k):
                if g is None:
                    return
                dve.wait_ge(s["u_hi"], 2 * g + k + 1)
                lo_part(uT[1][:, k, :], bank[("x", "c")[k]][:], uT[0][:, k, :], "u_lo")

            def qk_mm(g, pj):
                if g is None:
                    return
                dve.wait_ge(s["qk_done"], g + 1)
                if pj is not None and later(pj, 1):
                    dve.wait_ge(s["out_stored"], 16 * pj)
                if later(g, 1):
                    dve.wait_ge(s["qk_lo_ready"], 2 * (g - 1) + 2)
                    dve.wait_ge(s["qk_hi_ready"], 3 * (g - 1) + 3)
                dve.tensor_scalar(qk_exp, bank["x"][:], qk_bias[:], 0.0, ALU.add, ALU.min).then_inc(s["qk_minmax"], 1)
                dve.tensor_scalar(qk, bank["x"][:], qk_bias[:], 0.0, ALU.add, ALU.max).then_inc(s["qk_minmax"], 1)

            def qk_l(g):
                if g is None:
                    return
                dve.wait_ge(s["qk_hi_ready"], 3 * g + 3)
                dve.tensor_tensor(q_stack[FQ:P, :], qk[0:FQ, :], q_stack[0:FQ, :].bitcast(F32),
                                  ALU.subtract).then_inc(s["qk_lo_ready"], 1)
                dve.tensor_tensor(k_lo[:], qk[FQ:P, :], k_stack[FQ:P, :].bitcast(F32),
                                  ALU.subtract).then_inc(s["qk_lo_ready"], 1)

            def v_sum(g, half):
                if g is None:
                    return
                dve.wait_ge(s["v_done"], 2 * g + half + 1)
                if half == 0 and isinstance(g, int) and g == 0:
                    dve.wait_ge(s["bvo_ready"], 1)
                    dve.wait_ge(s["bvo_done"], 1)
                if half or later(g, 1):
                    dve.wait_ge(s["v_hi_ready"], 2 * g + half)
                    dve.wait_ge(s["v_lo_ready"], 2 * g + half)
                for j in range(2):
                    mm = dve.tensor_tensor(v32[:, j, :], bank[("x", "c")[half]][:, j * D:(j + 1) * D], bvo_b[:], ALU.add)
                mm.then_inc(s["v_ready"], 1)

            def a_split(g, half):
                if g is None:
                    return
                tiles = ((0, "x", 0, 1), (1, "c", 0, 2), (2, "x", 0, 3), (3, "x", 3 * P, 3))[2 * half:2 * half + 2]
                for j, b, c0, n in tiles:
                    dve.wait_ge(s["s_done"], 3 * g + n)
                    if j == 0 and later(g, 1):
                        dve.wait_ge(s["av_done"], 4 * (g - 1) + 4)
                    dve.tensor_tensor(a[0][:, j, 0:P], bank[b][:, c0:c0 + P], mask[:],
                                      ALU.mult).then_inc(s["a_hi_diag"], 1)
                for j, b, c0, n in tiles:
                    w = N - j * P
                    dve.wait_ge(s["a_hi_diag"], 4 * g + j + 1)
                    if j < 3:
                        dve.wait_ge(s["a_hi_off"], 3 * g + j + 1)
                    lo_part(a[1][:, j, 0:w], bank[b][:, c0:c0 + w], a[0][:, j, 0:w], "a_lo_ready")

            def attn_out(g, t):
                if g is None:
                    return
                b = ("p0", "p1", "x", "p0")[t]
                dve.wait_ge(s["av_done"], 4 * g + t + 1)
                dve.tensor_scalar(den[:, t:t + 1], bank[b][:, D:D + 1], ATTN_EPS, None, ALU.add).then_inc(s["den_ready"], 1)
                dve.wait_ge(s["den_ready"], 4 * g + t + 1)
                dve.reciprocal(rden[:, t:t + 1], den[:, t:t + 1]).then_inc(s["rden_ready"], 1)
                dve.wait_ge(s["rden_ready"], 4 * g + t + 1)
                if t == 0:
                    dve.wait_ge(s["n1o_ready"], g + 1)
                dve.scalar_tensor_tensor(xa[:, t, :], bank[b][:, 0:D], rden[:, t:t + 1], xa[:, t, :],
                                         ALU.mult, ALU.add).then_inc(s["xa_ready"], 1)

            def ln2_part(g, t):
                if g is None:
                    return
                dve.wait_ge(s["xa_ready"], 4 * g + t + 1)
                stats(1, xa, t, None)

            def ln2_end(g):
                if g is None:
                    return
                if later(g, 1):
                    dve.wait_ge(s["z2_ready"], 4 * (g - 1) + 4)
                aggregate(1, g)

            def z2(g, fc):
                if g is None:
                    return
                dve.wait_ge(s["ln2_rs"], g + 1)
                if fc is not None:
                    dve.wait_ge(s["tz3_done"], 2 * fc + 2)
                elif later(g, 1):
                    dve.wait_ge(s["tz2_done"], 2 * (g - 1) + 2)
                for t in range(T):
                    normalise(z, xa, 1, t, 0, "z2_ready")

            def z2_lo(g, k):
                if g is None:
                    return
                dve.wait_ge(s["z2_hi"], 2 * g + k + 1)
                lo_part(z2T[1][:, k, :], bank[("x", "p1")[k]][:], z2T[0][:, k, :], "z2_lo")

            def h_lo(g, m):
                if g is None:
                    return
                dve.wait_ge(s["h_hi_ready"], 8 * g + m + 1)
                if later(g, 1) or m >= 3:
                    dve.wait_ge(s["f2_step"], 8 * g + (m - 2 if m >= 3 else 0))
                dve.tensor_tensor(hr[1][:, m % 3, :], hring[:, m % 3, :], hr[0][:, m % 3, :].bitcast(F32),
                                  ALU.subtract).then_inc(s["h_lo_odd"], 1)

            def y_sum(g, h):
                if g is None:
                    return
                if h == 0:
                    dve.wait_ge(s["f2_step"], 8 * g + 8)
                    dve.wait_ge(s["xs_ready"], g + 1)
                    if later(g, 1):
                        dve.wait_ge(s["yc_ready"], (g - 1) + 1)
                dve.tensor_tensor(y[:, 2 * h:2 * h + 2, :].rearrange("p t d -> p (t d)"), bank[("y0", "y1")[h]][:],
                                  xs[:, 2 * h:2 * h + 2, :].rearrange("p t d -> p (t d)"), ALU.add).then_inc(s["y_ready"], 1)

            def ln3_part(g, h):
                if g is None:
                    return
                dve.wait_ge(s["y_ready"], 2 * g + h + 1)
                for t in (2 * h, 2 * h + 1):
                    stats(2, y, t, None)

            def ln3_end(g):
                if g is None:
                    return
                if later(g, 1):
                    dve.wait_ge(s["z3_ready"], 4 * (g - 1) + 4)
                aggregate(2, g)

            def z3(g):
                if g is None:
                    return
                dve.wait_ge(s["ln3_rs"], g + 1)
                dve.wait_ge(s["tz2_done"], 2 * min(g + 1, G - 1) + 2 if isinstance(g, int) else 2 * (g + 1) + 2)
                if isinstance(g, int) and g == G - 1:
                    dve.wait_ge(s["tz3_done"], 2 * (g - 1) + 2)
                for t in range(T):
                    normalise(z, y, 2, t, 0, "z3_ready")

            def z3_lo(g, k):
                if g is None:
                    return
                dve.wait_ge(s["z3_hi"], 2 * g + k + 1)
                lo_part(z3T[1][:, k, :], bank[("x", "c")[k]][:], z3T[0][:, k, :], "z3_lo")

            def g_lo(g, m):
                if g is None:
                    return
                dve.wait_ge(s["g_hi_ready"], 8 * g + m + 1)
                if later(g, 1) or m >= 2:
                    dve.wait_ge(s["pj_step"], 8 * g + (m - 1 if m >= 2 else 0))
                dve.wait_ge(s["h3_gelu"], 8 * g + m + 1)
                dve.scalar_tensor_tensor(gr[1][:, m % 2, :], h3[:, m, :], ln3w_c[:, m:m + 1],
                                         gr[0][:, m % 2, :].bitcast(F32), ALU.mult, ALU.subtract).then_inc(s["g_lo_ready"], 1)

            def hsum_last(g, m):
                dve.wait_ge(s["h3_gelu"], 8 * g + m + 1)
                if m == 1:
                    dve.wait_ge(s["var_done"], (g - 1) + 1)
                    dve.tensor_tensor(hsum, h3[:, 0, :], h3[:, 1, :], ALU.add).then_inc(s["hsum_last"], 1)
                else:
                    dve.wait_ge(s["hsum_last"], m - 1)
                    dve.tensor_tensor(hsum, hsum, h3[:, m, :], ALU.add).then_inc(s["hsum_last"], 1)

            def var_eps(g):
                if g is None:
                    return
                b = moment_bank(g)
                dve.wait_ge(s["var_done"], g + 1)
                if later(g, 1):
                    dve.wait_ge(s["rs3_ready"], (g - 1) + 1)
                dve.tensor_scalar(neg_mu[:], b[:, T:2 * T], -1.0, None, ALU.mult).then_inc(s["moments"], 1)
                dve.wait_ge(s["moments"], 3 * g + 1)
                dve.tensor_tensor(mu_sq[:], neg_mu[:], neg_mu[:], ALU.mult).then_inc(s["moments"], 1)
                dve.wait_ge(s["moments"], 3 * g + 2)
                dve.tensor_tensor(var_raw[:], b[:, 0:T], mu_sq[:], ALU.subtract).then_inc(s["moments"], 1)
                dve.wait_ge(s["moments"], 3 * g + 3)
                dve.tensor_scalar(ve[3][:, 0, :], var_raw[:], 0.0, LN_EPS, ALU.max, ALU.add).then_inc(s["var_ready"], 1)

            def correct(g):
                if g is None:
                    return
                dve.wait_ge(s["rs3_ready"], g + 1)
                dve.tensor_tensor(neg_mu_rs[:], neg_mu[:], rs[3][:, 0, :], ALU.mult).then_inc(s["scale_ready"], 1)
                dve.wait_ge(s["scale_ready"], g + 1)
                dve.wait_ge(s["yc_ready"], g + 1)
                for t in range(T):
                    dve.scalar_tensor_tensor(yc[:, t, :], csum_b, neg_mu_rs[:, t:t + 1], yc[:, t, :],
                                             ALU.mult, ALU.add).then_inc(s["corrected"], 1)

            def output(g, at):
                if g is None:
                    return
                dve.wait_ge(s["pj_step"], 8 * g + 8)
                dve.wait_ge(s["corrected"], 4 * g + 4)
                if at is not None:
                    dve.wait_ge(s["qk_lo_ready"], 2 * at + 2)
                elif later(g, 1):
                    dve.wait_ge(s["out_stored"], 16 * g)
                for t in range(T):
                    dve.scalar_tensor_tensor(out_sb[:, t, :], bank[("p0", "p1")[t // 2]][:, (t % 2) * D:(t % 2 + 1) * D],
                                             rs[3][:, 0, t:t + 1], yc[:, t, :], ALU.mult, ALU.add).then_inc(s["out_ready"], 1)

            def body(i):
                at, ml, fc, pj = groups(i)
                nx = following(i)
                if is_step(i, -1):
                    consts(); ln1_stats(at); prep_vec(); prep_wqk(); ln1_u(at); prep_late_vec(); prep_dots()
                    n1(at); u_lo(at, 0); u_lo(at, 1); prep_wvo(); qk_mm(at, pj); prep_f1_bias(); v_sum(at, 0)
                    prep_f1(0); qk_l(at); v_sum(at, 1); a_split(at, 0); a_split(at, 1); prep_f1(1)
                    ln1_stats(nx); attn_out(at, 0); prep_f2(0); attn_out(at, 1); ln2_part(at, 0)
                    ln2_part(at, 1); attn_out(at, 2); ln2_part(at, 2); attn_out(at, 3); ln2_part(at, 3)
                    ln2_end(at); prep_f2(1); prep_f1(2); z2(at, fc); prep_f1(3); ln1_u(nx); z2_lo(at, 0)
                    z2_lo(at, 1); prep_f2(2); prep_f2(3)
                elif is_step(i, 0):
                    n1(at); u_lo(at, 0); u_lo(at, 1); qk_mm(at, pj); prep_theta(); h_lo(ml, 1); prep_tern(0)
                    v_sum(at, 0); prep_tern(1); h_lo(ml, 3); v_sum(at, 1); qk_l(at); ln1_stats(nx)
                    a_split(at, 0); prep_select(); a_split(at, 1); h_lo(ml, 5); attn_out(at, 0); attn_out(at, 1)
                    ln2_part(at, 0); attn_out(at, 2); ln2_part(at, 1); attn_out(at, 3); ln2_part(at, 2)
                    ln2_part(at, 3); ln2_end(at); ln1_u(nx); z2(at, fc); h_lo(ml, 7); z2_lo(at, 0); z2_lo(at, 1)
                elif is_step(i, G - 1):
                    g_lo(pj, 0); y_sum(fc, 0); y_sum(fc, 1); g_lo(pj, 1); ln3_part(fc, 0); ln3_part(fc, 1)
                    ln3_end(fc); z3(fc); h_lo(ml, 1); g_lo(pj, 2); z3_lo(fc, 0); z3_lo(fc, 1); g_lo(pj, 3)
                    var_eps(pj); g_lo(pj, 4); g_lo(pj, 5); g_lo(pj, 6); h_lo(ml, 3); correct(pj); g_lo(pj, 7)
                    h_lo(ml, 5); output(pj, at); h_lo(ml, 7)
                elif is_step(i, G):
                    g_lo(pj, 0); g_lo(pj, 1); y_sum(fc, 0); y_sum(fc, 1); ln3_part(fc, 0); ln3_part(fc, 1)
                    g_lo(pj, 2); ln3_end(fc); g_lo(pj, 3); z3(fc); g_lo(pj, 4); g_lo(pj, 5); z3_lo(fc, 0)
                    z3_lo(fc, 1); g_lo(pj, 6); g_lo(pj, 7); var_eps(pj); hsum_last(G - 1, 1)
                    hsum_last(G - 1, 2); correct(pj); g_lo(G - 1, 0); output(pj, at); g_lo(G - 1, 1)
                    hsum_last(G - 1, 3); hsum_last(G - 1, 4); g_lo(G - 1, 2); hsum_last(G - 1, 5)
                    g_lo(G - 1, 3); hsum_last(G - 1, 6); g_lo(G - 1, 4); hsum_last(G - 1, 7); g_lo(G - 1, 5)
                    var_eps(G - 1); g_lo(G - 1, 6); g_lo(G - 1, 7); correct(G - 1); output(G - 1, at)
                else:
                    g_lo(pj, 0); y_sum(fc, 0); y_sum(fc, 1); g_lo(pj, 1); ln3_part(fc, 0); ln3_part(fc, 1)
                    g_lo(pj, 2); ln3_end(fc); u_lo(at, 0); u_lo(at, 1); g_lo(pj, 3); z3(fc); qk_mm(at, pj)
                    g_lo(pj, 4); n1(at); z3_lo(fc, 0); g_lo(pj, 5); z3_lo(fc, 1); h_lo(ml, 1); v_sum(at, 0)
                    g_lo(pj, 6); qk_l(at); v_sum(at, 1); g_lo(pj, 7); a_split(at, 0); ln1_stats(nx); h_lo(ml, 3)
                    a_split(at, 1); var_eps(pj); correct(pj); output(pj, at); h_lo(ml, 5); attn_out(at, 0)
                    attn_out(at, 1); ln2_part(at, 0); ln2_part(at, 1); attn_out(at, 2); attn_out(at, 3)
                    ln2_part(at, 2); ln2_part(at, 3); ln2_end(at); ln1_u(nx); z2(at, fc); h_lo(ml, 7)
                    z2_lo(at, 0); z2_lo(at, 1)

            steps(dve, body)

        @block.gpsimd
        def _(pool):
            def consts():
                pool.memset(ident[:], 0.0).then_inc(s["consts_memset"], 1)
                pool.memset(mask[:], 1.0).then_inc(s["consts_memset"], 1)
                pool.wait_ge(s["consts_memset"], 2)
                pool.affine_select(out=ident[:], in_=ident[:], compare_op=ALU.not_equal, fill=1.0, base=0,
                                   pattern=[[-1, P]], channel_multiplier=1).then_inc(s["consts_ready"], 1)
                pool.affine_select(out=mask[:], in_=mask[:], compare_op=ALU.is_ge, fill=0.0, base=0,
                                   pattern=[[1, P]], channel_multiplier=-1).then_inc(s["consts_ready"], 1)

            def rstd(n, g, two):
                if g is None:
                    return
                ve_s, rs_s = s[f"ln{n + 1}_ve"], s[f"ln{n + 1}_rs"]
                c = 2 if two else 1
                if later(g, 1):
                    pool.wait_ge(s[("u_ready", "z2_ready", "z3_ready")[n]], 4 * (g - 1) + 4)
                    if two:
                        pool.wait_ge(s["n1_ready"], 4 * (g - 1) + 4)
                pool.wait_ge(ve_s, c * g + c)
                pool.tensor_tensor(rs[n][:, 0:c, :].rearrange("p c t -> p (c t)"),
                                   ve[n][:, 0:c, :].rearrange("p c t -> p (c t)"),
                                   neg_half[:, 0:c * T], ALU.pow).then_inc(rs_s, 1)

            def n1o(g):
                if g is None:
                    return
                pool.wait_ge(s["n1_ready"], 4 * g + 4)
                if isinstance(g, int) and g == 0:
                    pool.wait_ge(s["ob_loaded"], 32)
                pool.tensor_tensor(xa[:], xa[:], ob_b[:].unsqueeze(1).to_broadcast([P, T, D]),
                                   ALU.add).then_inc(s["n1o_ready"], 1)

            def xpb_(g):
                if g is None:
                    return
                if isinstance(g, int) and g == 0:
                    pool.wait_ge(s["x_loaded"], 16)
                    pool.wait_ge(s["ob_loaded"], 32)
                if later(g, 1):
                    pool.wait_ge(s["xs_ready"], (g - 1) + 1)
                pool.tensor_tensor(xpb[:], x_sb[:], f2b_b[:].unsqueeze(1).to_broadcast([P, T, D]),
                                   ALU.add).then_inc(s["xpb_ready"], 1)

            def xs_(g):
                if g is None:
                    return
                pool.wait_ge(s["xa_ready"], 4 * g + 4)
                pool.wait_ge(s["xpb_ready"], g + 1)
                if later(g, 1):
                    pool.wait_ge(s["y_ready"], 2 * (g - 1) + 2)
                else:
                    pool.wait_ge(s["bias_done"], 3)
                    pool.wait_ge(s["bvo_done"], 1)
                pool.tensor_tensor(xs[:], xpb[:], xa[:], ALU.add).then_inc(s["xs_ready"], 1)

            def qk_sum(g):
                if g is None:
                    return
                pool.wait_ge(s["qk_exp_ready"], g + 1)
                pool.wait_ge(s["qk_minmax"], 2 * g + 2)
                pool.tensor_tensor(qk, qk_exp, qk, ALU.add).then_inc(s["qk_ready"], 1)

            def v_lo(g, half):
                if g is None:
                    return
                pool.wait_ge(s["v_hi_ready"], 2 * g + half + 1)
                pool.wait_ge(s["v_ready"], 2 * g + half + 1)
                if half == 0 and later(g, 1):
                    pool.wait_ge(s["av_done"], 4 * (g - 1) + 4)
                pool.tensor_tensor(v[1][:, 2 * half:2 * half + 2, 0:D], v32[:],
                                   v[0][:, 2 * half:2 * half + 2, 0:D].bitcast(F32), ALU.subtract).then_inc(s["v_lo_ready"], 1)

            def a_mask(g):
                if g is None:
                    return
                pool.wait_ge(s["a_lo_ready"], 4 * g + 4)
                pool.tensor_tensor(a[1][:, :, 0:P], a[1][:, :, 0:P].bitcast(F32), mask[:].unsqueeze(1).to_broadcast([P, T, P]),
                                   ALU.mult).then_inc(s["a_lo_masked"], 1)

            def h_lo(g, m):
                if g is None:
                    return
                pool.wait_ge(s["h_hi_ready"], 8 * g + m + 1)
                if later(g, 1) or m >= 3:
                    pool.wait_ge(s["f2_step"], 8 * g + (m - 2 if m >= 3 else 0))
                pool.tensor_tensor(hr[1][:, m % 3, :], hring[:, m % 3, :], hr[0][:, m % 3, :].bitcast(F32),
                                   ALU.subtract).then_inc(s["h_lo_even"], 1)

            def hsum_step(g, m):
                if g is None:
                    return
                pool.wait_ge(s["h3_gelu"], 8 * g + m + 1)
                if m == 1:
                    if later(g, 1):
                        pool.wait_ge(s["var_done"], (g - 1) + 1)
                    pool.tensor_tensor(hsum, h3[:, 0, :], h3[:, 1, :], ALU.add).then_inc(s["hsum_step"], 1)
                else:
                    pool.wait_ge(s["hsum_step"], 7 * g + m - 1)
                    pool.tensor_tensor(hsum, hsum, h3[:, m, :], ALU.add).then_inc(s["hsum_step"], 1)

            def sqsum_step(g, m):
                if g is None:
                    return
                pool.wait_ge(s["sq_ready"], 8 * g + m + 1)
                if m == 1:
                    if later(g, 1):
                        pool.wait_ge(s["var_done"], (g - 1) + 1)
                    pool.tensor_tensor(sqsum, sq[:, 0, :], sq[:, 1, :], ALU.add).then_inc(s["sqsum_step"], 1)
                else:
                    pool.wait_ge(s["sqsum_step"], 7 * g + m - 1)
                    pool.tensor_tensor(sqsum, sqsum, sq[:, m % 2, :], ALU.add).then_inc(s["sqsum_step"], 1)

            def rstd3(g):
                if g is None:
                    return
                pool.wait_ge(s["var_ready"], g + 1)
                if later(g, 1):
                    pool.wait_ge(s["out_ready"], 4 * (g - 1) + 4)
                pool.tensor_tensor(rs[3][:, 0, :], ve[3][:, 0, :], neg_half[:, 0:T], ALU.pow).then_inc(s["rs3_ready"], 1)

            def yc_(g):
                if g is None:
                    return
                pool.wait_ge(s["y_ready"], 2 * g + 2)
                if later(g, 1):
                    pool.wait_ge(s["out_ready"], 4 * (g - 1) + 4)
                pool.tensor_tensor(yc, y, cpj_b.unsqueeze(1).to_broadcast([P, T, D]),
                                   ALU.add).then_inc(s["yc_ready"], 1)

            def body(i):
                at, ml, fc, pj = groups(i)
                nx = following(i)
                if is_step(i, -1):
                    consts(); rstd(0, at, True); xpb_(at); n1o(at); qk_sum(at); v_lo(at, 0); v_lo(at, 1)
                    a_mask(at); rstd(1, at, False); rstd(0, nx, True)
                elif is_step(i, 0):
                    xs_(ml); n1o(at); h_lo(ml, 0); h_lo(ml, 2); qk_sum(at); xpb_(at); v_lo(at, 0); v_lo(at, 1)
                    rstd(0, nx, True); h_lo(ml, 4); a_mask(at); h_lo(ml, 6); rstd(1, at, False)
                elif is_step(i, G - 1):
                    sqsum_step(pj, 1); sqsum_step(pj, 2); rstd(2, fc, False); h_lo(ml, 0); sqsum_step(pj, 3)
                    h_lo(ml, 2); sqsum_step(pj, 4); sqsum_step(pj, 5); sqsum_step(pj, 6); sqsum_step(pj, 7)
                    rstd3(pj); hsum_step(fc, 1); xs_(ml); h_lo(ml, 4); hsum_step(fc, 2); hsum_step(fc, 3)
                    hsum_step(fc, 4); hsum_step(fc, 5); hsum_step(fc, 6); h_lo(ml, 6); yc_(fc); hsum_step(fc, 7)
                elif is_step(i, G):
                    sqsum_step(pj, 1); sqsum_step(pj, 2); sqsum_step(pj, 3); rstd(2, fc, False)
                    sqsum_step(pj, 4); sqsum_step(pj, 5); sqsum_step(pj, 6); sqsum_step(pj, 7); rstd3(pj)
                    sqsum_step(G - 1, 1); sqsum_step(G - 1, 2); sqsum_step(G - 1, 3); sqsum_step(G - 1, 4)
                    sqsum_step(G - 1, 5); sqsum_step(G - 1, 6); sqsum_step(G - 1, 7); yc_(fc); rstd3(G - 1)
                else:
                    sqsum_step(pj, 1); xs_(ml); sqsum_step(pj, 2); rstd(2, fc, False); sqsum_step(pj, 3)
                    xpb_(at); h_lo(ml, 0); qk_sum(at); sqsum_step(pj, 4); sqsum_step(pj, 5); h_lo(ml, 2)
                    v_lo(at, 0); n1o(at); sqsum_step(pj, 6); v_lo(at, 1); sqsum_step(pj, 7); h_lo(ml, 4)
                    rstd3(pj); a_mask(at); hsum_step(fc, 1); rstd(0, nx, True); hsum_step(fc, 2)
                    hsum_step(fc, 3); h_lo(ml, 6); hsum_step(fc, 4); rstd(1, at, False); hsum_step(fc, 5)
                    yc_(fc); hsum_step(fc, 6); hsum_step(fc, 7)

            steps(pool, body)


_INS = ["L0_attn_x", "L0_attn_ln1_w", "L0_attn_ln1_b", "L0_attn_q_w", "L0_attn_q_b", "L0_attn_k_w", "L0_attn_k_b",
        "L0_attn_v_w", "L0_attn_v_b", "L0_attn_o_w", "L0_attn_o_b", "L0_attn_ln2_w", "L0_attn_ln2_b", "L0_attn_f1_w",
        "L0_attn_f1_b", "L0_attn_f2_w", "L0_attn_f2_b", "L0_ffn_W_fc", "L0_ffn_ln_w", "L0_ffn_ln_b", "L0_ffn_W_proj"]


def kernel(**inputs):
    import numpy as _np
    import concourse.bacc as _bacc
    from concourse import mybir as _mybir
    from concourse.bass_utils import run_bass_kernel_spmd as _run

    nc = _bacc.Bacc("TRN2", target_bir_lowering=False, num_devices=1)
    arrays, args = {}, []
    for name in _INS:
        a = _np.ascontiguousarray(inputs[name])
        arrays[f"in_{name}"] = a
        args.append(nc.dram_tensor(f"in_{name}", a.shape, _mybir.dt.from_np(a.dtype), kind="ExternalInput").ap())
    args.append(nc.dram_tensor("out", inputs["L0_attn_x"].shape, _mybir.dt.float32, kind="ExternalOutput").ap())
    build(nc, *args)
    r = _run(nc, [arrays], core_ids=[0])
    return r.results[0]["out"]
```

```python
from contextlib import ExitStack

import concourse.bass as bass
from concourse import mybir

F32 = mybir.dt.float32
F32R = mybir.dt.float32r
ALU = mybir.AluOpType
ACT = mybir.ActivationFunctionType
AXX = mybir.AxisListType.X

P = 128
LN_EPS = 1e-5
ATTN_EPS = 1e-6
ABSMEAN_EPS = 1e-6


def later(g, n):
    return not isinstance(g, int) or g >= n


def build(nc, x, ln1_w, ln1_b, q_w, q_b, k_w, k_b, v_w, v_b, o_w, o_b, ln2_w, ln2_b, f1_w, f1_b,
          f2_w, f2_b, fc_w, ln3_w, ln3_b, pj_w, out):
    G, N, D = x.shape
    FQ = q_w.shape[0]
    H = f1_w.shape[0]
    T = N // P
    KD = D // P
    KH = H // P
    VW = D + 2
    assert (T, KD, KH, 2 * FQ) == (4, 2, 8, P) and H == fc_w.shape[0]

    x_flat = x.rearrange("g n d -> (g n d)")
    out_flat = out.rearrange("g n d -> (g n d)")

    def group_rows(flat, offset):
        return flat[bass.ds(offset, N * D)].rearrange("(t p d) -> p t d", t=T, p=P)

    with ExitStack() as ctx:
        def sb(name, shape, dt=F32):
            return ctx.enter_context(nc.sbuf_tensor(name, shape, dt))

        def sem(name):
            return ctx.enter_context(nc.semaphore(name))

        bank = {n: ctx.enter_context(nc.psum_tensor("bank_" + n, [P, 512], F32))
                for n in ("f0", "f1", "y0", "y1", "p0", "p1", "x", "c")}

        wqk = [sb("wqk_hi", [P, KD, P], F32R), sb("wqk_lo", [P, KD, P], F32R)]
        wvo = [sb("wvo_hi", [P, KD, D], F32R), sb("wvo_lo", [P, KD, D], F32R)]
        wf1 = [sb("wf1_hi", [P, KD, H], F32R), sb("wf1_lo", [P, KD, H], F32R)]
        wf2 = [sb("wf2_hi", [P, KH, D], F32R), sb("wf2_lo", [P, KH, D], F32R)]
        wfc = sb("wfc_t", [P, KD, H], F32R)
        wpj = sb("wpj_t", [P, KH, D], F32R)

        ident = sb("ident", [P, P])
        mean_w = sb("mean_w", [P, P])
        mask = sb("mask", [P, P])
        neg_half = sb("neg_half", [P, 8])
        vec = sb("vec", [P, 31])
        ln1w_c, vb_c, qkb_c = vec[:, 0:2], vec[:, 2:4], vec[:, 4:5]
        ln2w_c, f1b_c, ln3w_c, ln3b_c = vec[:, 5:7], vec[:, 7:15], vec[:, 15:23], vec[:, 23:31]
        ln3_split = sb("ln3_split", [P, KH, 4], F32R)
        dots = sb("dots", [P, 11])
        f1_bias = sb("f1_bias", [P, KH])
        vb_full = sb("vb_full", [P, KD])
        qk_bias = sb("qk_bias", [P, 1])
        abs_sum = sb("abs_sum", [P, 8])
        abs_tot = sb("abs_tot", [P, 2])
        theta = sb("theta", [P, 4])
        bvo_b = sb("bvo_b", [P, D])
        ob_b = sb("ob_b", [P, D])
        f2b_b = sb("f2b_b", [P, D])
        pj_rows_b = sb("pj_rows_b", [P, 2, D])
        csum_b, cpj_b = pj_rows_b[:, 0, :], pj_rows_b[:, 1, :]

        x_sb = sb("x_sb", [P, T, D])
        u = sb("u", [P, T, D])
        xa = sb("xa", [P, T, D])
        xpb = sb("xpb", [P, T, D])
        xs = sb("xs", [P, T, D])
        z = sb("z", [P, T, D])
        y_yc = sb("y_yc", [P, 2, T, D])
        y, yc = y_yc[:, 0], y_yc[:, 1]
        uT = [sb("uT_hi", [P, KD, N], F32R), sb("uT_lo", [P, KD, N], F32R)]
        z2T = [sb("z2T_hi", [P, KD, N], F32R), sb("z2T_lo", [P, KD, N], F32R)]
        z3T = [sb("z3T_hi", [P, KD, N], F32R), sb("z3T_lo", [P, KD, N], F32R)]
        qk_out = sb("qk_out", [P, 2, N])
        qk_exp, qk = qk_out[:, 0, :], qk_out[:, 1, :]
        out_sb = qk_out[:].rearrange("p a n -> p (a n)").rearrange("p (t d) -> p t d", t=T)
        q_stack = sb("q_stack", [P, N], F32R)
        k_stack = sb("k_stack", [P, N], F32R)
        k_lo = sb("k_lo", [FQ, N], F32R)
        v32 = sb("v32", [P, 2, D])
        v = [sb("v_hi", [P, T, VW], F32R), sb("v_lo", [P, T, VW], F32R)]
        a = [sb("a_hi", [P, T, N], F32R), sb("a_lo", [P, T, N], F32R)]
        hring = sb("hring", [P, 3, N])
        hr = [sb("h_hi", [P, 3, N], F32R), sb("h_lo", [P, 3, N], F32R)]
        h3 = sb("h3", [P, KH, N])
        sums = sb("sums", [P, 5, N])
        sq, hsum, sqsum = sums[:, 0:2], sums[:, 2], sums[:, 3]
        gr = [sb("g_hi", [P, 2, N], F32R), sb("g_lo", [P, 2, N], F32R)]
        bn = [sb(f"bn{n}", [P, T, 6]) for n in range(3)]
        mv = [sb(f"mv{n}", [P, T, 2]) for n in range(3)]
        ve = [sb(f"ve{n}", [P, 2, T]) for n in range(4)]
        rs = [sb(f"rs{n}", [P, 2, T]) for n in range(4)]
        fence = sb("fence", [P, 1])
        den = sb("den", [P, T])
        rden = sb("rden", [P, T])
        neg_mu, mu_sq, var_raw, neg_mu_rs = [sb(n, [P, T]) for n in ("neg_mu", "mu_sq", "var_raw", "neg_mu_rs")]

        qk_raw = hring[:, 0, 0:D]
        wv_raw = hring[:, 1, :].rearrange("p (k d) -> p k d", k=KD)
        wo_raw = hring[:, 2, :].rearrange("p (k d) -> p k d", k=KD)
        woT = v32
        vec_rows, late_rows = z[0:5, 0, 0:P], z[0:26, 1, 0:P]
        f1_raw = y_yc[:, :].rearrange("p a t d -> p (a t) d")
        f2_raw = sums[:, 0:4].rearrange("p a n -> p (a n)").rearrange("p (k h) -> p k h", k=KD)
        fc_raw = h3[:, 0:4, :].rearrange("p a n -> p (a n)").rearrange("p (m d) -> p m d", m=KH)
        pj_raw = h3[:, 4:8, :].rearrange("p a n -> p (a n)").rearrange("p (k h) -> p k h", k=KD)
        tern_low = y_yc[:].rearrange("p a t d -> p (a t d)")
        ln1b_b, ln2b_b, dot_out = xs[:, 0, :], xs[:, 1, :], xs[:, 2, :]
        vb_wide = xs[:, 3, :].rearrange("p (k m) -> p k m", k=KD)
        abs_out = sums[:, 4, :]
        pj_rows = sums[0:4, 4, 0:D]
        row_select = sums[0:4, 4, D:D + 2 * P].rearrange("p (r m) -> p r m", r=2)

        names = """x_loaded rows_loaded late_rows_loaded ln1b_loaded ln2b_loaded ob_loaded qk_raw_loaded
            v_raw_loaded f1_raw_loaded f2_raw_loaded fc_raw_loaded pj_raw_loaded consts_memset consts_ready
            vec_t vec_ready late_vec_t late_vec_ready dots_done bias_done vb_wide_ready qkT_done
            wqk_hi_ready wqk_ready woT_done woT_ready wvo_done wvo_hi_ready wvo_ready bvo_done bvo_ready
            f1T_done wf1_hi_ready f2T_done wf2_hi_ready abs_summed abs_tot_done theta_ready fc_low fc_tern
            pj_low pj_tern fcT_done wfc_ready pjT_done wpj_ready ln3_hi_ready ln3_lo_ready f1_scaled
            f1_summed wf1_staged wf2_staged w_lo_ready cpj_done rows_ready select_ready rows_spread
            cpj_ready v_ones_ready ln1_bn ln1_mv ln1_ve ln1_rs u_ready tu_done u_hi u_lo qk_done qk_minmax
            qk_exp_ready qk_ready qk_hi_ready qk_lo_ready v_done v_ready v_hi_ready v_lo_ready s_done
            a_hi_diag a_hi_off a_lo_ready a_lo_masked av_done den_ready rden_ready n1_ready n1o_ready
            xa_ready ln2_bn ln2_mv ln2_ve ln2_rs z2_ready tz2_done z2_hi z2_lo xpb_ready xs_ready f1_done
            h_gelu h_hi_ready h_lo_even h_lo_odd f2_step y_ready ln3_bn ln3_mv ln3_ve ln3_rs z3_ready
            tz3_done z3_hi z3_lo fc_done h3_gelu hsum_step hsum_last sq_ready sqsum_step g_hi_ready
            g_lo_ready pj_step var_done moments var_ready scale_ready corrected rs3_ready yc_ready out_ready
            out_stored""".split()
        s = {n: sem(n) for n in names}

        block = ctx.enter_context(nc.Block())

        def steps(engine, first, step, last):
            first()
            step(1)
            step(2)
            with engine.Fori(3, G - 2) as i:
                step(i)
            step(G - 2)
            last()

        def groups(i):
            g = [i + 1, i, i - 1, i - 2]
            if not isinstance(i, int):
                return g
            return [n if 0 <= n < G else None for n in g]

        def is_step(i, n):
            return isinstance(i, int) and i == n

        def fc_bank(g, m):
            return bank[("c", "f0", "f1")[m % 3] if is_step(g, G - 1) else "c"]

        def moment_bank(g):
            return bank["x" if is_step(g, G - 1) or is_step(g, G - 2) else "c"]

        def following(i):
            return i + 2 if not isinstance(i, int) or i + 2 < G else None

        @block.sync
        def _(sp):
            def load_rows(rows, column, done):
                for src, c in rows:
                    n = src.shape[0] // P
                    sp.dma_start(column[c:c + n, :], src.rearrange("(r p) -> r p", p=P)).then_inc(s[done], 16)

            def load_wide(dst, src, done):
                sp.dma_start(dst, src.rearrange("(r d) -> r d", r=1).to_broadcast([P, D])).then_inc(s[done], 16)

            sp.dma_start(x_sb[:], group_rows(x_flat, 0)).then_inc(s["x_loaded"], 16)
            load_rows([(ln1_w, 0), (v_b, 2)], vec_rows, "rows_loaded")
            sp.dma_start(vec_rows[4:5, 0:FQ], q_b.rearrange("(r p) -> r p", r=1)).then_inc(s["rows_loaded"], 16)
            sp.dma_start(vec_rows[4:5, FQ:P], k_b.rearrange("(r p) -> r p", r=1)).then_inc(s["rows_loaded"], 16)
            sp.dma_start(qk_raw[0:FQ, :], q_w).then_inc(s["qk_raw_loaded"], 16)
            sp.dma_start(qk_raw[FQ:P, :], k_w).then_inc(s["qk_raw_loaded"], 16)
            load_wide(ln1b_b, ln1_b, "ln1b_loaded")
            sp.dma_start(wo_raw, o_w.rearrange("(k p) d -> p k d", p=P)).then_inc(s["v_raw_loaded"], 16)
            sp.dma_start(wv_raw, v_w.rearrange("(k p) d -> p k d", p=P)).then_inc(s["v_raw_loaded"], 16)
            load_rows([(ln2_w, 0), (f1_b, 2), (ln3_w, 10), (ln3_b, 18)], late_rows, "late_rows_loaded")
            sp.dma_start(f1_raw, f1_w.rearrange("(m p) d -> p m d", p=P)).then_inc(s["f1_raw_loaded"], 16)
            load_wide(ob_b[:], o_b, "ob_loaded")
            load_wide(f2b_b[:], f2_b, "ob_loaded")
            load_wide(ln2b_b, ln2_b, "ln2b_loaded")
            sp.dma_start(f2_raw, f2_w.rearrange("(k p) h -> p k h", p=P)).then_inc(s["f2_raw_loaded"], 16)
            sp.dma_start(fc_raw, fc_w.rearrange("(m p) d -> p m d", p=P)).then_inc(s["fc_raw_loaded"], 16)
            sp.dma_start(pj_raw, pj_w.rearrange("(k p) h -> p k h", p=P)).then_inc(s["pj_raw_loaded"], 16)

            def load_x(g):
                offset = sp.snap(g * (N * D)) if not isinstance(g, int) else g * N * D
                if not isinstance(g, int):
                    n1_count, xpb_count = sp.snap(4 * g), sp.snap(g + 0)
                sp.wait_ge(s["n1_ready"], 4 * g if isinstance(g, int) else n1_count)
                sp.wait_ge(s["xpb_ready"], g if isinstance(g, int) else xpb_count)
                sp.dma_start(x_sb[:], group_rows(x_flat, offset)).then_inc(s["x_loaded"], 16)

            def store(g):
                offset = sp.snap(g * (N * D)) if not isinstance(g, int) else g * N * D
                sp.wait_ge(s["out_ready"], 4 * g + 4)
                sp.dma_start(group_rows(out_flat, offset), out_sb).then_inc(s["out_stored"], 16)

            def first():
                load_x(1)
                load_x(2)

            def step(i):
                if following(i) is not None:
                    load_x(i + 2)
                if later(i, 2):
                    store(i - 2)

            def last():
                store(G - 3)
                store(G - 2)
                for h in range(2):
                    sp.wait_ge(s["out_ready"], 4 * (G - 1) + 2 * h + 2)
                    sp.dma_start(group_rows(out_flat, (G - 1) * N * D)[:, 2 * h:2 * h + 2, :],
                                 out_sb[:, 2 * h:2 * h + 2, :]).then_inc(s["out_stored"], 16)

            steps(sp, first, step, last)
            sp.wait_ge(s["out_stored"], 16 * (G + 1))

        @block.tensor
        def _(pe):
            def split3(ps, w, r, start, stop, skip=False):
                pe.matmul(ps, w[0], r[0], start=start, stop=False, skip_group_check=skip)
                pe.matmul(ps, w[0], r[1], start=False, stop=False, skip_group_check=skip)
                return pe.matmul(ps, w[1], r[0], start=False, stop=stop, skip_group_check=skip)

            def flip(src, banks, k):
                for t in range(T):
                    mm = pe.transpose(banks[:, t * P:(t + 1) * P], src[:, t, k * P:(k + 1) * P], ident[:])
                return mm

            def prep_small():
                pe.wait_ge(s["consts_ready"], 3)
                pe.wait_ge(s["rows_loaded"], 16 * 4)
                pe.transpose(bank["p0"][:, 0:5], vec_rows, ident[0:5, 0:5]).then_inc(s["vec_t"], 1)
                pe.wait_ge(s["qk_raw_loaded"], 32)
                for k in range(KD):
                    mm = pe.transpose(bank["p1"][:, k * P:(k + 1) * P], qk_raw[:, k * P:(k + 1) * P], ident[:])
                mm.then_inc(s["qkT_done"], 1)
                pe.wait_ge(s["v_raw_loaded"], 32)
                for k in range(KD):
                    for e in range(KD):
                        mm = pe.transpose(bank["y0"][:, k * D + e * P:k * D + (e + 1) * P],
                                          wo_raw[:, e, k * P:(k + 1) * P], ident[:])
                mm.then_inc(s["woT_done"], 1)

            def prep_late_vec():
                pe.wait_ge(s["late_rows_loaded"], 16 * 4)
                pe.transpose(bank["f0"][:, 0:26], late_rows, ident[0:26, 0:26]).then_inc(s["late_vec_t"], 1)

            def prep_vo():
                pe.wait_ge(s["woT_ready"], 1)
                for c in range(KD):
                    for k in range(KD):
                        mm = pe.matmul(bank["y1"][:, c * D:(c + 1) * D], wv_raw[:, k, c * P:(c + 1) * P],
                                       woT[:, k, :], start=(k == 0), stop=(k == KD - 1))
                mm.then_inc(s["wvo_done"], 1)
                pe.wait_ge(s["vb_wide_ready"], KD)
                pe.wait_ge(s["vec_ready"], 1)
                for k in range(KD):
                    mm = pe.matmul(bank["p0"][:, 0:D], vb_wide[:, k, :], woT[:, k, :],
                                   start=(k == 0), stop=(k == KD - 1))
                mm.then_inc(s["bvo_done"], 1)

            def prep_f1(n):
                k, half = n // 2, n % 2
                b = bank[("f0", "f1")[half]]
                if n == 0:
                    pe.wait_ge(s["f1_raw_loaded"], 16)
                    pe.wait_ge(s["late_vec_ready"], 1)
                if n >= 2:
                    pe.wait_ge(s["wf1_staged"], n - 1)
                for m in range(4):
                    mm = pe.transpose(b[:, m * P:(m + 1) * P], f1_raw[:, 4 * half + m, k * P:(k + 1) * P], ident[:])
                mm.then_inc(s["f1T_done"], 1)

            def prep_f2(n):
                b = bank[("y0", "y1")[n % 2]]
                if n == 0:
                    pe.wait_ge(s["f2_raw_loaded"], 16)
                    pe.wait_ge(s["woT_ready"], 1)
                if n == 1:
                    pe.wait_ge(s["wvo_ready"], 1)
                if n >= 2:
                    pe.wait_ge(s["wf2_staged"], n - 1)
                for q in range(4):
                    k, e = 2 * n + q // 2, q % 2
                    mm = pe.transpose(b[:, q * P:(q + 1) * P], f2_raw[:, e, k * P:(k + 1) * P], ident[:])
                mm.then_inc(s["f2T_done"], 1)

            def prep_theta():
                pe.wait_ge(s["abs_summed"], 8)
                pe.wait_ge(s["z2_lo"], 2)
                pe.matmul(bank["p1"][:, 0:8], mean_w[:], abs_sum[:], start=True, stop=True).then_inc(s["abs_tot_done"], 1)

            def prep_fc(n):
                k, half = n // 2, n % 2
                b = bank[("p0", "p1")[half]]
                if n == 0:
                    pe.wait_ge(s["fc_tern"], 1)
                    pe.wait_ge(s["xa_ready"], 4)
                if n == 1:
                    pe.wait_ge(s["theta_ready"], 1)
                if n >= 2:
                    pe.wait_ge(s["wfc_ready"], n - 1)
                for m in range(4):
                    mm = pe.transpose(b[:, m * P:(m + 1) * P], fc_raw[:, 4 * half + m, k * P:(k + 1) * P], ident[:])
                mm.then_inc(s["fcT_done"], 1)

            def prep_pj(n):
                b = bank[("p0", "p1")[n % 2]]
                if n == 0:
                    pe.wait_ge(s["pj_tern"], 1)
                if n < 2:
                    pe.wait_ge(s["wfc_ready"], n + 3)
                else:
                    pe.wait_ge(s["wpj_ready"], n - 1)
                for q in range(4):
                    k, e = 2 * n + q // 2, q % 2
                    mm = pe.transpose(b[:, q * P:(q + 1) * P], pj_raw[:, e, k * P:(k + 1) * P], ident[:])
                mm.then_inc(s["pjT_done"], 1)

            def prep_cpj(k):
                if k == 0:
                    pe.wait_ge(s["wpj_ready"], 4)
                    pe.wait_ge(s["ln3_hi_ready"], 2)
                    pe.wait_ge(s["ln3_lo_ready"], 2)
                    pe.wait_ge(s["xa_ready"], 4)
                pe.matmul(bank["p0"][0:4, 0:D], ln3_split[:, k, :], wpj[:, k, :],
                          start=(k == 0), stop=(k == KH - 1)).then_inc(s["cpj_done"], 1)

            def prep_spread():
                pe.wait_ge(s["rows_ready"], 1)
                pe.wait_ge(s["select_ready"], 3)
                for r in range(2):
                    mm = pe.matmul(bank["p0"][:, r * D:(r + 1) * D], row_select[:, r, :], pj_rows,
                                   start=True, stop=True)
                mm.then_inc(s["rows_spread"], 1)

            def tu(g, k, pj):
                if g is None:
                    return
                pe.wait_ge(s["u_ready"], 4 * g + 4)
                if k == 0 and later(g, 1):
                    pe.wait_ge(s["z2_lo"], 2 * (g - 1) + 1)
                if k == 1 and pj is not None:
                    pe.wait_ge(s["h3_gelu"], 8 * pj + 8)
                elif k == 1 and later(g, 1):
                    pe.wait_ge(s["a_lo_ready"], 4 * (g - 1) + 2)
                flip(u, bank[("x", "c")[k]], k).then_inc(s["tu_done"], 1)

            def qk_proj(g):
                if g is None:
                    return
                pe.wait_ge(s["u_lo"], 2 * g + 2)
                pe.wait_ge(s["u_hi"], 2 * g + 2)
                if isinstance(g, int) and g == 0:
                    pe.wait_ge(s["wqk_ready"], 1)
                for k in range(KD):
                    mm = split3(bank["x"][:], [w[:, k, :] for w in wqk], [r[:, k, :] for r in uT],
                                k == 0, k == KD - 1)
                mm.then_inc(s["qk_done"], 1)

            def v_proj(g, half, fc):
                if g is None:
                    return
                if half == 0 and isinstance(g, int) and g == 0:
                    pe.wait_ge(s["wvo_ready"], 1)
                if fc is not None:
                    pe.wait_ge(s["z3_lo"], 2 * fc + half + 1)
                elif half == 0:
                    pe.wait_ge(s["qk_minmax"], 2 * g + 2)
                b = bank[("x", "c")[half]]
                for j in range(2):
                    t = 2 * half + j
                    for k in range(KD):
                        mm = split3(b[:, j * D:(j + 1) * D], [r[:, k, t * P:(t + 1) * P] for r in uT],
                                    [w[:, k, :] for w in wvo], k == 0, k == KD - 1)
                mm.then_inc(s["v_done"], 1)

            def scores(g, half):
                if g is None:
                    return
                if half == 0:
                    pe.wait_ge(s["qk_lo_ready"], 2 * g + 2)
                    pe.wait_ge(s["qk_hi_ready"], 3 * g + 3)
                for j, b, c0, q0 in ((0, "x", 0, 0), (1, "c", 0, P), (2, "x", 0, 2 * P), (3, "x", 2 * P, 2 * P))[2 * half:2 * half + 2]:
                    if j < 2:
                        pe.wait_ge(s["v_ready"], 2 * g + j + 1)
                    if j == 2:
                        pe.wait_ge(s["a_lo_ready"], 4 * g + 1)
                    ps = bank[b][:, c0:c0 + N - q0]
                    pe.matmul(ps, k_stack[:, j * P:(j + 1) * P], q_stack[:, q0:], start=True, stop=False)
                    mm = pe.matmul(ps, k_lo[:, j * P:(j + 1) * P], q_stack[0:FQ, q0:], start=False, stop=True)
                    if j != 2:
                        mm.then_inc(s["s_done"], 1)

            def attend(g, t, pj):
                if g is None:
                    return
                if t == 0:
                    pe.wait_ge(s["v_lo_ready"], 2 * g + 2)
                    pe.wait_ge(s["v_hi_ready"], 2 * g + 2)
                    pe.wait_ge(s["a_hi_diag"], 4 * g + 4)
                    pe.wait_ge(s["a_hi_off"], 3 * g + 3)
                    pe.wait_ge(s["a_lo_ready"], 4 * g + 4)
                    pe.wait_ge(s["a_lo_masked"], g + 1)
                    if isinstance(g, int) and g == 0:
                        pe.wait_ge(s["v_ones_ready"], 3)
                if t < 2 and pj is not None:
                    pe.wait_ge(s["out_ready"], 4 * pj + 2 * t + 2)
                elif t < 2 and isinstance(g, int) and g == 0:
                    pe.wait_ge(s[("bvo_ready", "wqk_ready")[t]], 1)
                elif t < 2 and isinstance(g, int) and g == 1:
                    pe.wait_ge(s[("cpj_ready", "wpj_ready")[t]], (1, 4)[t])
                elif t == 0:
                    pe.wait_ge(s["xa_ready"], 4 * (g - 1) + 4)
                elif t == 1:
                    pe.wait_ge(s["z2_lo"], 2 * (g - 1) + 2)
                elif t == 3:
                    pe.wait_ge(s["xa_ready"], 4 * g + 1)
                b = bank[("p0", "p1", "x", "p0")[t]]
                for j in range(t + 1):
                    mm = split3(b[:, 0:VW], [w[:, j, (t - j) * P:(t - j + 1) * P] for w in a],
                                [r[:, j, :] for r in v], j == 0, j == t)
                mm.then_inc(s["av_done"], 1)

            def tz2(g, k):
                if g is None:
                    return
                pe.wait_ge(s["z2_ready"], 4 * g + 4)
                pe.wait_ge(s["xa_ready"], 4 * g + (3 if k == 0 else 2))
                flip(z, bank[("x", "p1")[k]], k).then_inc(s["tz2_done"], 1)

            def f1(g, m):
                if g is None:
                    return
                if m == 0:
                    pe.wait_ge(s["z2_lo"], 2 * g + 2)
                    pe.wait_ge(s["z2_hi"], 2 * g + 2)
                    if isinstance(g, int) and g == 0:
                        pe.wait_ge(s["wf1_staged"], 4)
                        pe.wait_ge(s["w_lo_ready"], 4)
                if later(g, 1) or m >= 2:
                    pe.wait_ge(s["h_gelu"], 8 * g + m - 1)
                for k in range(KD):
                    mm = split3(bank[("f0", "f1")[m % 2]][:], [w[:, k, m * P:(m + 1) * P] for w in wf1],
                                [r[:, k, :] for r in z2T], k == 0, k == KD - 1)
                mm.then_inc(s["f1_done"], 1)

            def f2(g, k):
                if g is None:
                    return
                if k == 0:
                    if later(g, 1):
                        pe.wait_ge(s["y_ready"], 2 * (g - 1) + 2)
                    if isinstance(g, int) and g == 0:
                        pe.wait_ge(s["wf2_staged"], 4)
                        pe.wait_ge(s["w_lo_ready"], 8)
                pe.wait_ge(s["h_lo_odd" if k % 2 else "h_lo_even"], 4 * g + k // 2 + 1)
                pe.wait_ge(s["h_hi_ready"], 8 * g + k + 1)
                for t in range(T):
                    ps = bank[("y0", "y1")[t // 2]][:, (t % 2) * D:(t % 2 + 1) * D]
                    mm = split3(ps, [r[:, k % 3, t * P:(t + 1) * P] for r in hr], [w[:, k, :] for w in wf2],
                                k == 0 and t % 2 == 0, k == KH - 1, skip=True)
                mm.then_inc(s["f2_step"], 1)

            def tz3(g, k, at, pj):
                if g is None:
                    return
                pe.wait_ge(s["z3_ready"], 4 * g + 4)
                if at is not None and k == 0:
                    pe.wait_ge(s["qk_minmax"], 2 * at + 2)
                elif at is not None:
                    pe.wait_ge(s["u_lo"], 2 * at + 2)
                elif k == 0 and later(g, G - 1):
                    pe.wait_ge(s["z3_lo"], 2 * (g - 1) + 1)
                elif k == 0:
                    pe.wait_ge(s["z2_lo"], 2 * (g + 1) + 1)
                else:
                    pe.wait_ge(s["h3_gelu"], 8 * pj + 8)
                flip(z, bank[("x", "c")[k]], k).then_inc(s["tz3_done"], 1)

            def fc_up(g, m, at, pj):
                if g is None:
                    return
                if m == 0:
                    pe.wait_ge(s["z3_lo"], 2 * g + 2)
                    pe.wait_ge(s["z3_hi"], 2 * g + 2)
                    if isinstance(g, int) and g == 0:
                        pe.wait_ge(s["wfc_ready"], 4)
                    if at is not None:
                        pe.wait_ge(s["a_lo_ready"], 4 * at + 2)
                if is_step(g, G - 1):
                    if m in (1, 2):
                        pe.wait_ge(s["h_gelu"], 8 * g + m + 6)
                    if m >= 3:
                        pe.wait_ge(s["h3_gelu"], 8 * g + m - 2)
                elif m >= 1:
                    pe.wait_ge(s["h3_gelu"], 8 * g + m)
                if m == 1 and pj is not None and not is_step(g, G - 1):
                    pe.wait_ge(s["var_ready"], pj + 1)
                b = fc_bank(g, m)
                for k in range(KD):
                    for part in range(2):
                        mm = pe.matmul(b[:], wfc[:, k, m * P:(m + 1) * P], z3T[part][:, k, :],
                                       start=(k == 0 and part == 0), stop=(k == KD - 1 and part == 1))
                mm.then_inc(s["fc_done"], 1)

            def proj(g, k, ml):
                if g is None:
                    return
                if k == 0:
                    if isinstance(g, int) and g == 0:
                        pe.wait_ge(s["wpj_ready"], 4)
                    if ml is not None:
                        pe.wait_ge(s["xa_ready"], 4 * ml + 4)
                        pe.wait_ge(s["z2_lo"], 2 * ml + 2)
                    else:
                        pe.wait_ge(s["out_ready"], 4 * (g - 1) + 4)
                pe.wait_ge(s["g_lo_ready"], 8 * g + k + 1)
                pe.wait_ge(s["g_hi_ready"], 8 * g + k + 1)
                for t in range(T):
                    ps = bank[("p0", "p1")[t // 2]][:, (t % 2) * D:(t % 2 + 1) * D]
                    for part in range(2):
                        mm = pe.matmul(ps, gr[part][:, k % 2, t * P:(t + 1) * P], wpj[:, k, :],
                                       start=(k == 0 and t % 2 == 0 and part == 0), stop=(k == KH - 1 and part == 1),
                                       skip_group_check=True)
                mm.then_inc(s["pj_step"], 1)

            def moment(g, n, fc):
                if g is None:
                    return
                if n == 0:
                    if is_step(g, G - 1):
                        pe.wait_ge(s["hsum_last"], 7)
                        pe.wait_ge(s["var_ready"], g)
                    elif is_step(g, G - 2):
                        pe.wait_ge(s["hsum_step"], 7 * g + 7)
                        pe.wait_ge(s["z3_lo"], 2 * fc + 1)
                    else:
                        pe.wait_ge(s["hsum_step"], 7 * g + 7)
                        pe.wait_ge(s["h3_gelu"], 8 * fc + 1)
                if n == T:
                    pe.wait_ge(s["sqsum_step"], 7 * g + 7)
                src, t, column = (hsum, n, T + n) if n < T else (sqsum, n - T, n - T)
                pe.matmul(moment_bank(g)[:, column:column + 1], src[:, t * P:(t + 1) * P], mean_w[:, 0:1],
                          start=True, stop=True).then_inc(s["var_done"], 1)

            def first():
                prep_small(); prep_late_vec(); tu(0, 0, None); tu(0, 1, None); prep_vo(); qk_proj(0); prep_f1(0)
                v_proj(0, 0, None); prep_f2(0); prep_f1(1); v_proj(0, 1, None); prep_f2(1); scores(0, 0)
                prep_f1(2); prep_f1(3); scores(0, 1); attend(0, 0, None); attend(0, 1, None); attend(0, 2, None)
                attend(0, 3, None); prep_f2(2); tz2(0, 0); tz2(0, 1); prep_f2(3); tu(1, 0, None); prep_theta()
                tu(1, 1, None); f1(0, 0); qk_proj(1); f1(0, 1); f1(0, 2); prep_fc(0); v_proj(1, 0, None)
                prep_fc(1); v_proj(1, 1, None); f1(0, 3); prep_fc(2); f2(0, 0); prep_fc(3); f1(0, 4); prep_pj(0)
                prep_pj(1); scores(1, 0); prep_pj(2); prep_pj(3); f2(0, 1); prep_cpj(0); prep_cpj(1)
                prep_cpj(2); prep_cpj(3); prep_cpj(4); f1(0, 5); prep_cpj(5); prep_cpj(6); prep_cpj(7); f1(0, 6)
                scores(1, 1); prep_spread(); f2(0, 2); f2(0, 3); attend(1, 0, None); attend(1, 1, None)
                attend(1, 2, None); attend(1, 3, None); f2(0, 4); f1(0, 7); f2(0, 5); f2(0, 6); tz2(1, 0)
                tz2(1, 1); f2(0, 7)

            def step(i):
                at, ml, fc, pj = groups(i)
                tu(at, 0, pj); tu(at, 1, pj); f1(ml, 0); proj(pj, 0, ml); f1(ml, 1); qk_proj(at); f1(ml, 2)
                f1(ml, 3); proj(pj, 1, ml); f2(ml, 0); tz3(fc, 0, at, pj); tz3(fc, 1, at, pj); f2(ml, 1)
                proj(pj, 2, ml); v_proj(at, 0, fc); proj(pj, 3, ml); f1(ml, 4); v_proj(at, 1, fc); f1(ml, 5)
                scores(at, 0); f1(ml, 6); f2(ml, 2); fc_up(fc, 0, at, pj); proj(pj, 4, ml); moment(pj, 0, fc)
                proj(pj, 5, ml); moment(pj, 1, fc); moment(pj, 2, fc); scores(at, 1); moment(pj, 3, fc)
                moment(pj, 4, fc); moment(pj, 5, fc); proj(pj, 6, ml); moment(pj, 6, fc); proj(pj, 7, ml)
                moment(pj, 7, fc); f2(ml, 3); f1(ml, 7); fc_up(fc, 1, at, pj); f2(ml, 4); fc_up(fc, 2, at, pj)
                attend(at, 0, pj); attend(at, 1, pj); fc_up(fc, 3, at, pj); attend(at, 2, pj)
                fc_up(fc, 4, at, pj); attend(at, 3, pj); fc_up(fc, 5, at, pj); f2(ml, 5); fc_up(fc, 6, at, pj)
                f2(ml, 6); fc_up(fc, 7, at, pj); tz2(at, 0); tz2(at, 1); f2(ml, 7)

            def last():
                f1(G - 1, 0); f1(G - 1, 1); f1(G - 1, 2); proj(G - 3, 0, G - 1); f1(G - 1, 3)
                proj(G - 3, 1, G - 1); tz3(G - 2, 0, None, G - 3); tz3(G - 2, 1, None, G - 3); f1(G - 1, 4)
                proj(G - 3, 2, G - 1); fc_up(G - 2, 0, None, G - 3); f1(G - 1, 5); f2(G - 1, 0)
                moment(G - 3, 0, G - 2); moment(G - 3, 1, G - 2); moment(G - 3, 2, G - 2); proj(G - 3, 3, G - 1)
                proj(G - 3, 4, G - 1); moment(G - 3, 3, G - 2); f1(G - 1, 6); moment(G - 3, 4, G - 2)
                proj(G - 3, 5, G - 1); moment(G - 3, 5, G - 2); moment(G - 3, 6, G - 2); f2(G - 1, 1)
                moment(G - 3, 7, G - 2); f2(G - 1, 2); fc_up(G - 2, 1, None, G - 3); proj(G - 3, 6, G - 1)
                fc_up(G - 2, 2, None, G - 3); f2(G - 1, 3); fc_up(G - 2, 3, None, G - 3); proj(G - 3, 7, G - 1)
                f1(G - 1, 7); f2(G - 1, 4); f2(G - 1, 5); f2(G - 1, 6); fc_up(G - 2, 4, None, G - 3)
                f2(G - 1, 7); fc_up(G - 2, 5, None, G - 3); proj(G - 2, 0, None); fc_up(G - 2, 6, None, G - 3)
                proj(G - 2, 1, None); fc_up(G - 2, 7, None, G - 3); proj(G - 2, 2, None); proj(G - 2, 3, None)
                tz3(G - 1, 0, None, G - 2); tz3(G - 1, 1, None, G - 2); proj(G - 2, 4, None)
                proj(G - 2, 5, None); moment(G - 2, 0, G - 1); fc_up(G - 1, 0, None, G - 2)
                moment(G - 2, 1, G - 1); moment(G - 2, 2, G - 1); moment(G - 2, 3, G - 1)
                fc_up(G - 1, 1, None, G - 2); moment(G - 2, 4, G - 1); moment(G - 2, 5, G - 1)
                moment(G - 2, 6, G - 1); moment(G - 2, 7, G - 1); fc_up(G - 1, 2, None, G - 2)
                proj(G - 2, 6, None); proj(G - 2, 7, None); fc_up(G - 1, 3, None, G - 2)
                fc_up(G - 1, 4, None, G - 2); fc_up(G - 1, 5, None, G - 2); fc_up(G - 1, 6, None, G - 2)
                proj(G - 1, 0, None); proj(G - 1, 1, None); fc_up(G - 1, 7, None, G - 2); proj(G - 1, 2, None)
                proj(G - 1, 3, None); moment(G - 1, 0, G - 1); moment(G - 1, 1, G - 1); moment(G - 1, 2, G - 1)
                moment(G - 1, 3, G - 1); proj(G - 1, 4, None); moment(G - 1, 4, G - 1); moment(G - 1, 5, G - 1)
                moment(G - 1, 6, G - 1); moment(G - 1, 7, G - 1); proj(G - 1, 5, None); proj(G - 1, 6, None)
                proj(G - 1, 7, None)

            steps(pe, first, step, last)

        @block.scalar
        def _(act):
            def prep_wo():
                act.wait_ge(s["woT_done"], 1)
                act.activation(woT[:].rearrange("p k d -> p (k d)"), bank["y0"][:], ACT.Copy).then_inc(s["woT_ready"], 1)

            def prep_wqk():
                act.wait_ge(s["qkT_done"], 1)
                act.wait_ge(s["vec_ready"], 1)
                for k in range(KD):
                    act.activation(wqk[0][:, k, :], bank["p1"][:, k * P:(k + 1) * P], ACT.Copy,
                                   scale=ln1w_c[:, k:k + 1]).then_inc(s["wqk_hi_ready"], 1)

            def prep_wvo():
                act.wait_ge(s["wvo_done"], 1)
                act.wait_ge(s["vec_ready"], 1)
                for k in range(KD):
                    act.activation(wvo[0][:, k, :], bank["y1"][:, k * D:(k + 1) * D], ACT.Copy,
                                   scale=ln1w_c[:, k:k + 1]).then_inc(s["wvo_hi_ready"], 1)

            def prep_bvo():
                act.wait_ge(s["bvo_done"], 1)
                act.activation(bvo_b[:], bank["p0"][:, 0:D], ACT.Copy).then_inc(s["bvo_ready"], 1)

            def stage(b, n, scale, staged):
                if n < 3:
                    act.wait_ge(s["wvo_done"], 1)
                    act.wait_ge(s["dots_done"], 3)
                else:
                    act.wait_ge(s["w_lo_ready"], n - 2)
                act.activation(hring[:, n % 3, :], b[:], ACT.Copy, scale=scale).then_inc(s[staged], 1)

            def prep_f1(n):
                k, half = n // 2, n % 2
                act.wait_ge(s["f1T_done"], n + 1)
                if n == 0:
                    act.wait_ge(s["late_vec_ready"], 1)
                act.activation(wf1[0][:, k, half * 512:(half + 1) * 512], bank[("f0", "f1")[half]][:], ACT.Copy,
                               scale=ln2w_c[:, k:k + 1]).then_inc(s["wf1_hi_ready"], 1)
                stage(bank[("f0", "f1")[half]], n, ln2w_c[:, k:k + 1], "wf1_staged")

            def prep_f2(n):
                act.wait_ge(s["f2T_done"], n + 1)
                act.activation(wf2[0][:, 2 * n:2 * n + 2, :].rearrange("p k d -> p (k d)"),
                               bank[("y0", "y1")[n % 2]][:], ACT.Copy).then_inc(s["wf2_hi_ready"], 1)
                stage(bank[("y0", "y1")[n % 2]], 4 + n, 1.0, "wf2_staged")

            def prep_f1_bias():
                act.wait_ge(s["f1_scaled"], 1)
                for m in range(KH):
                    act.activation(f1_raw[:, m, :], f1_raw[:, m, :], ACT.Copy,
                                   accum_out=dots[:, m:m + 1]).then_inc(s["f1_summed"], 1)

            def prep_abs(n):
                if n == 0:
                    act.wait_ge(s["fc_raw_loaded"], 16)
                if n == 4:
                    act.wait_ge(s["pj_raw_loaded"], 16)
                if n:
                    act.wait_ge(s["abs_summed"], n)
                act.activation(abs_out[:], h3[:, n, :], ACT.Abs,
                               accum_out=abs_sum[:, n:n + 1]).then_inc(s["abs_summed"], 1)

            def prep_fc(n):
                k, half = n // 2, n % 2
                act.wait_ge(s["fcT_done"], n + 1)
                act.activation(wfc[:, k, half * 512:(half + 1) * 512], bank[("p0", "p1")[half]][:],
                               ACT.Copy).then_inc(s["wfc_ready"], 1)

            def prep_pj(n):
                act.wait_ge(s["pjT_done"], n + 1)
                act.activation(wpj[:, 2 * n:2 * n + 2, :].rearrange("p k d -> p (k d)"),
                               bank[("p0", "p1")[n % 2]][:], ACT.Copy).then_inc(s["wpj_ready"], 1)

            def prep_ln3():
                act.wait_ge(s["late_vec_ready"], 1)
                act.activation(ln3_split[:, :, 0], ln3w_c, ACT.Copy).then_inc(s["ln3_hi_ready"], 1)
                act.activation(ln3_split[:, :, 1], ln3b_c, ACT.Copy).then_inc(s["ln3_hi_ready"], 1)

            def prep_rows():
                act.wait_ge(s["cpj_done"], KH)
                act.wait_ge(s["abs_tot_done"], 1)
                act.activation(pj_rows, bank["p0"][0:4, 0:D], ACT.Copy).then_inc(s["rows_ready"], 1)

            def prep_cpj():
                act.wait_ge(s["rows_spread"], 1)
                act.activation(pj_rows_b[:].rearrange("p r d -> p (r d)"), bank["p0"][:], ACT.Copy).then_inc(s["cpj_ready"], 1)

            def u_hi(g, k):
                if g is None:
                    return
                if k == 0 and later(g, 1):
                    act.wait_ge(s["v_done"], 2 * (g - 1) + 2)
                act.wait_ge(s["tu_done"], 2 * g + k + 1)
                act.activation(uT[0][:, k, :], bank[("x", "c")[k]][:], ACT.Copy).then_inc(s["u_hi"], 1)

            def qk_e(g):
                if g is None:
                    return
                act.wait_ge(s["qk_minmax"], 2 * g + 2)
                act.activation(qk_exp, qk_exp, ACT.Exp).then_inc(s["qk_exp_ready"], 1)

            def qk_h(g):
                if g is None:
                    return
                act.wait_ge(s["qk_ready"], g + 1)
                if later(g, 1):
                    act.wait_ge(s["s_done"], 3 * (g - 1) + 3)
                act.activation(q_stack[0:FQ, :], qk[0:FQ, :], ACT.Copy).then_inc(s["qk_hi_ready"], 1)
                act.activation(k_stack[FQ:P, :], qk[FQ:P, :], ACT.Copy).then_inc(s["qk_hi_ready"], 1)
                act.activation(k_stack[0:FQ, :], qk[FQ:P, :], ACT.Copy).then_inc(s["qk_hi_ready"], 1)

            def v_h(g, half):
                if g is None:
                    return
                act.wait_ge(s["v_ready"], 2 * g + half + 1)
                if half == 0 and later(g, 1):
                    act.wait_ge(s["av_done"], 4 * (g - 1) + 4)
                act.activation(v[0][:, 2 * half:2 * half + 2, 0:D], v32[:], ACT.Copy).then_inc(s["v_hi_ready"], 1)

            def a_off(g, j):
                if g is None:
                    return
                if j == 0 and later(g, 1):
                    act.wait_ge(s["av_done"], 4 * (g - 1) + 4)
                w = N - (j + 1) * P
                act.wait_ge(s["a_hi_diag"], 4 * g + (j + 1 if j < 2 else 4))
                act.wait_ge(s["s_done"], 3 * g + j + 1)
                act.activation(a[0][:, j, P:P + w], bank[("x", "c", "x")[j]][:, P:P + w],
                               ACT.Copy).then_inc(s["a_hi_off"], 1)

            def z2_hi(g, k):
                if g is None:
                    return
                if k == 0 and later(g, 1):
                    act.wait_ge(s["f1_done"], 8 * (g - 1) + 8)
                act.wait_ge(s["tz2_done"], 2 * g + k + 1)
                act.activation(z2T[0][:, k, :], bank[("x", "p1")[k]][:], ACT.Copy).then_inc(s["z2_hi"], 1)

            def gelu(g, m):
                if g is None:
                    return
                act.wait_ge(s["f1_done"], 8 * g + m + 1)
                if m >= 3:
                    act.wait_ge(s["h_lo_odd" if (m - 3) % 2 else "h_lo_even"], 4 * g + (m - 3) // 2 + 1)
                elif later(g, 1):
                    act.wait_ge(s["h_lo_odd"], 4 * g)
                    act.wait_ge(s["h_lo_even"], 4 * g)
                if m == 0 and isinstance(g, int) and g == 0:
                    act.wait_ge(s["bias_done"], 3)
                if m < 3 and isinstance(g, int) and g == 0:
                    act.wait_ge(s["w_lo_ready"], 8)
                act.activation(hring[:, m % 3, :], bank[("f0", "f1")[m % 2]][:], ACT.Gelu,
                               bias=f1_bias[:, m:m + 1]).then_inc(s["h_gelu"], 1)

            def h_hi(g, m):
                if g is None:
                    return
                act.wait_ge(s["h_gelu"], 8 * g + m + 1)
                if later(g, 1) or m >= 3:
                    act.wait_ge(s["f2_step"], 8 * g + (m - 2 if m >= 3 else 0))
                act.activation(hr[0][:, m % 3, :], hring[:, m % 3, :], ACT.Copy).then_inc(s["h_hi_ready"], 1)

            def z3_hi(g, k):
                if g is None:
                    return
                if k == 0 and later(g, 1):
                    act.wait_ge(s["fc_done"], 8 * (g - 1) + 8)
                act.wait_ge(s["tz3_done"], 2 * g + k + 1)
                act.activation(z3T[0][:, k, :], bank[("x", "c")[k]][:], ACT.Copy).then_inc(s["z3_hi"], 1)

            def gelu3(g, m):
                if g is None:
                    return
                act.wait_ge(s["fc_done"], 8 * g + m + 1)
                if later(g, 1):
                    act.wait_ge(s["g_lo_ready"], 8 * (g - 1) + m + 1)
                    act.wait_ge(s["g_hi_ready"], 8 * (g - 1) + m + 1)
                    act.wait_ge(s["sq_ready"], 8 * (g - 1) + m + 1)
                    act.wait_ge(s["hsum_step"], 7 * (g - 1) + max(m, 1))
                act.activation(h3[:, m, :], fc_bank(g, m)[:], ACT.Gelu).then_inc(s["h3_gelu"], 1)

            def g_hi(g, m):
                if g is None:
                    return
                act.wait_ge(s["h3_gelu"], 8 * g + m + 1)
                if later(g, 1) or m >= 2:
                    act.wait_ge(s["pj_step"], 8 * g + (m - 1 if m >= 2 else 0))
                act.activation(gr[0][:, m % 2, :], h3[:, m, :], ACT.Copy,
                               scale=ln3w_c[:, m:m + 1]).then_inc(s["g_hi_ready"], 1)

            def square(g, m):
                if g is None:
                    return
                act.wait_ge(s["h3_gelu"], 8 * g + m + 1)
                if later(g, 1) or m >= 2:
                    act.wait_ge(s["sqsum_step"], 7 * g + (max(m - 2, 1) if m >= 2 else 0))
                act.activation(sq[:, m % 2, :], h3[:, m, :], ACT.Square).then_inc(s["sq_ready"], 1)

            def first():
                prep_wqk(); prep_wo(); u_hi(0, 0); u_hi(0, 1); prep_wvo(); qk_e(0); prep_f1(0); prep_bvo()
                qk_h(0); v_h(0, 0); prep_abs(0); prep_f1(1); prep_abs(1); a_off(0, 0); a_off(0, 1); v_h(0, 1)
                a_off(0, 2); prep_abs(2); prep_f1(2); prep_abs(3); prep_abs(4); prep_abs(5); prep_abs(6)
                prep_f1(3); prep_f2(0); prep_f1_bias(); prep_abs(7); prep_f2(1); prep_f2(2); z2_hi(0, 0)
                z2_hi(0, 1); u_hi(1, 0); u_hi(1, 1); prep_f2(3); gelu(0, 0); gelu(0, 1); h_hi(0, 0); qk_e(1)
                prep_fc(0); gelu(0, 2); h_hi(0, 1); prep_fc(1); qk_h(1); prep_ln3(); v_h(1, 0); prep_fc(2)
                prep_fc(3); gelu(0, 3); prep_pj(0); prep_pj(1); prep_pj(2); a_off(1, 0); a_off(1, 1); prep_pj(3)
                h_hi(0, 2); gelu(0, 4); h_hi(0, 3); prep_rows(); v_h(1, 1); a_off(1, 2); prep_cpj(); gelu(0, 5)
                h_hi(0, 4); h_hi(0, 5); gelu(0, 6); h_hi(0, 6); gelu(0, 7); h_hi(0, 7); z2_hi(1, 0); z2_hi(1, 1)

            def step(i):
                at, ml, fc, pj = groups(i)
                g_hi(pj, 0); square(pj, 0); g_hi(pj, 1); square(pj, 1); u_hi(at, 0); u_hi(at, 1); gelu(ml, 0)
                square(pj, 2); square(pj, 3); h_hi(ml, 0); g_hi(pj, 2); gelu(ml, 1); h_hi(ml, 1); qk_e(at)
                gelu(ml, 2); g_hi(pj, 3); z3_hi(fc, 0); z3_hi(fc, 1); qk_h(at); g_hi(pj, 4); square(pj, 4)
                square(pj, 5); gelu(ml, 3); h_hi(ml, 2); v_h(at, 0); gelu(ml, 4); square(pj, 6); g_hi(pj, 5)
                h_hi(ml, 3); h_hi(ml, 4); a_off(at, 0); v_h(at, 1); a_off(at, 1); gelu3(fc, 0); square(pj, 7)
                g_hi(pj, 6); gelu(ml, 5); g_hi(pj, 7); gelu(ml, 6); a_off(at, 2); h_hi(ml, 5); h_hi(ml, 6)
                gelu3(fc, 1); gelu(ml, 7); gelu3(fc, 2); gelu3(fc, 3); gelu3(fc, 4); h_hi(ml, 7); gelu3(fc, 5)
                gelu3(fc, 6); gelu3(fc, 7); z2_hi(at, 0); z2_hi(at, 1)

            def last():
                square(G - 3, 0); g_hi(G - 3, 0); square(G - 3, 1); gelu(G - 1, 0); h_hi(G - 1, 0)
                square(G - 3, 2); gelu(G - 1, 1); g_hi(G - 3, 1); square(G - 3, 3); gelu(G - 1, 2)
                square(G - 3, 4); g_hi(G - 3, 2); z3_hi(G - 2, 0); z3_hi(G - 2, 1); h_hi(G - 1, 1)
                gelu(G - 1, 3); h_hi(G - 1, 2); g_hi(G - 3, 3); gelu(G - 1, 4); gelu3(G - 2, 0)
                square(G - 3, 5); square(G - 3, 6); g_hi(G - 3, 4); square(G - 3, 7); g_hi(G - 3, 5)
                h_hi(G - 1, 3); g_hi(G - 3, 6); square(G - 2, 0); gelu(G - 1, 5); g_hi(G - 3, 7); h_hi(G - 1, 4)
                gelu3(G - 2, 1); h_hi(G - 1, 5); square(G - 2, 1); gelu3(G - 2, 2); gelu(G - 1, 6)
                square(G - 2, 2); h_hi(G - 1, 6); gelu3(G - 2, 3); g_hi(G - 2, 0); g_hi(G - 2, 1)
                gelu(G - 1, 7); h_hi(G - 1, 7); square(G - 2, 3); gelu3(G - 2, 4); square(G - 2, 4)
                gelu3(G - 2, 5); g_hi(G - 2, 2); gelu3(G - 2, 6); square(G - 2, 5); g_hi(G - 2, 3)
                square(G - 2, 6); g_hi(G - 2, 4); gelu3(G - 2, 7); g_hi(G - 2, 5); z3_hi(G - 1, 0)
                z3_hi(G - 1, 1); square(G - 2, 7); g_hi(G - 2, 6); g_hi(G - 2, 7); gelu3(G - 1, 0)
                gelu3(G - 1, 1); square(G - 1, 0); square(G - 1, 1); gelu3(G - 1, 2); g_hi(G - 1, 0)
                square(G - 1, 2); gelu3(G - 1, 3); gelu3(G - 1, 4); g_hi(G - 1, 1); gelu3(G - 1, 5)
                square(G - 1, 3); square(G - 1, 4); gelu3(G - 1, 6); g_hi(G - 1, 2); square(G - 1, 5)
                g_hi(G - 1, 3); gelu3(G - 1, 7); square(G - 1, 6); g_hi(G - 1, 4); square(G - 1, 7)
                g_hi(G - 1, 5); g_hi(G - 1, 6); g_hi(G - 1, 7)

            steps(act, first, step, last)

        @block.vector
        def _(dve):
            def consts():
                dve.memset(mean_w[:], 1.0 / H).then_inc(s["consts_ready"], 1)
                dve.memset(neg_half[:], -0.5)
                dve.memset(v[0][:, :, D:D + 1].bitcast(F32), 1.0).then_inc(s["v_ones_ready"], 1)
                dve.memset(v[0][:, :, D + 1:VW].bitcast(F32), 0.0).then_inc(s["v_ones_ready"], 1)
                dve.memset(v[1][:, :, D:VW].bitcast(F32), 0.0).then_inc(s["v_ones_ready"], 1)

            def prep_vec():
                dve.wait_ge(s["vec_t"], 1)
                dve.tensor_copy(vec[:, 0:5], bank["p0"][:, 0:5]).then_inc(s["vec_ready"], 1)

            def prep_late_vec():
                dve.wait_ge(s["late_vec_t"], 1)
                dve.tensor_copy(vec[:, 5:31], bank["f0"][:, 0:26]).then_inc(s["late_vec_ready"], 1)

            def prep_dots():
                dve.wait_ge(s["vec_ready"], 1)
                dve.wait_ge(s["ln1b_loaded"], 16)
                for n, (src, col) in enumerate(((qk_raw, 10), (wv_raw[:, 0, :], 8), (wv_raw[:, 1, :], 9))):
                    if n:
                        dve.wait_ge(s["dots_done"], n)
                    dve.wait_ge(s["v_raw_loaded" if n else "qk_raw_loaded"], 32)
                    dve.tensor_tensor_reduce(dot_out, src, ln1b_b, 1.0, 0.0, ALU.mult, ALU.add,
                                             dots[:, col:col + 1]).then_inc(s["dots_done"], 1)
                dve.wait_ge(s["dots_done"], 3)
                dve.tensor_tensor(vb_full[:], dots[:, 8:10], vb_c, ALU.add).then_inc(s["bias_done"], 1)
                dve.tensor_tensor(qk_bias[:], dots[:, 10:11], qkb_c, ALU.add).then_inc(s["bias_done"], 1)
                dve.wait_ge(s["bias_done"], 2)
                for k in range(KD):
                    dve.tensor_scalar(vb_wide[:, k, :], mean_w[:], 0.0, vb_full[:, k:k + 1],
                                      ALU.mult, ALU.add).then_inc(s["vb_wide_ready"], 1)

            def prep_wqk():
                dve.wait_ge(s["wqk_hi_ready"], 2)
                for k in range(KD):
                    mm = dve.scalar_tensor_tensor(wqk[1][:, k, :], bank["p1"][:, k * P:(k + 1) * P],
                                                  ln1w_c[:, k:k + 1], wqk[0][:, k, :].bitcast(F32),
                                                  ALU.mult, ALU.subtract)
                mm.then_inc(s["wqk_ready"], 1)

            def prep_wvo():
                dve.wait_ge(s["wvo_hi_ready"], 2)
                for k in range(KD):
                    mm = dve.scalar_tensor_tensor(wvo[1][:, k, :], bank["y1"][:, k * D:(k + 1) * D],
                                                  ln1w_c[:, k:k + 1], wvo[0][:, k, :].bitcast(F32),
                                                  ALU.mult, ALU.subtract)
                mm.then_inc(s["wvo_ready"], 1)

            def prep_f1_bias():
                dve.wait_ge(s["f1_summed"], KH)
                dve.wait_ge(s["late_vec_ready"], 1)
                dve.tensor_tensor(f1_bias[:], dots[:, 0:KH], f1b_c, ALU.add).then_inc(s["bias_done"], 1)

            def prep_theta():
                dve.wait_ge(s["abs_tot_done"], 1)
                dve.tensor_reduce(abs_tot[:], bank["p1"][:, 0:8].rearrange("p (w n) -> p w n", w=2),
                                  AXX, ALU.add).then_inc(s["theta_ready"], 1)
                dve.wait_ge(s["theta_ready"], 1)
                dve.tensor_scalar(theta[:, 0:2], abs_tot[:], 0.5 * H / (H * D), 0.5 * ABSMEAN_EPS,
                                  ALU.mult, ALU.add).then_inc(s["theta_ready"], 1)
                dve.wait_ge(s["theta_ready"], 2)
                dve.tensor_scalar(theta[:, 2:4], theta[:, 0:2], -1.0, None, ALU.mult).then_inc(s["theta_ready"], 1)

            def prep_tern(w):
                low, tern = (("fc_low", "fc_tern"), ("pj_low", "pj_tern"))[w]
                raw = h3[:, 4 * w:4 * w + 4, :].rearrange("p a n -> p (a n)")
                if w == 0:
                    dve.wait_ge(s["theta_ready"], 3)
                    dve.wait_ge(s["f1_summed"], KH)
                else:
                    dve.wait_ge(s["fc_tern"], 1)
                dve.tensor_scalar(tern_low, raw, theta[:, 2 + w:3 + w], None, ALU.is_lt).then_inc(s[low], 1)
                dve.wait_ge(s[low], 1)
                dve.scalar_tensor_tensor(raw, raw, theta[:, w:w + 1], tern_low,
                                         ALU.is_gt, ALU.subtract).then_inc(s[tern], 1)

            def prep_select():
                dve.wait_ge(s["consts_ready"], 3)
                dve.wait_ge(s["abs_summed"], 8)
                dve.tensor_tensor(dots[0:4, 8:10], ident[0:4, 0:2], ident[0:4, 2:4], ALU.add).then_inc(s["select_ready"], 1)
                dve.wait_ge(s["select_ready"], 1)
                for r in range(2):
                    dve.tensor_scalar(row_select[:, r, :], mean_w[0:4, :], float(H), dots[0:4, 8 + r:9 + r],
                                      ALU.mult, ALU.mult).then_inc(s["select_ready"], 1)

            def prep_ln3():
                dve.wait_ge(s["ln3_hi_ready"], 2)
                for c, src in enumerate((ln3w_c, ln3b_c)):
                    dve.tensor_tensor(ln3_split[:, :, 2 + c], src, ln3_split[:, :, c].bitcast(F32),
                                      ALU.subtract).then_inc(s["ln3_lo_ready"], 1)

            def stats(n, src, t, ready):
                dve.bn_stats(bn[n][:, t, :], src[:, t, :]).then_inc(s[f"ln{n + 1}_bn"], 1)

            def aggregate(n, g):
                if later(g, 1):
                    dve.wait_ge(s[f"ln{n + 1}_rs"], (g - 1) + 1)
                dve.wait_ge(s[f"ln{n + 1}_bn"], 4 * g + 4)
                dve.tensor_scalar(fence[:], mean_w[:, 0:1], 1.0, None, ALU.mult)
                for t in range(T):
                    dve.bn_aggr(mv[n][:, t, :], bn[n][:, t, :]).then_inc(s[f"ln{n + 1}_mv"], 1)
                dve.wait_ge(s[f"ln{n + 1}_mv"], 4 * g + 4)
                dve.tensor_scalar(ve[n][:, 0, :], mv[n][:, :, 1], 1.0, LN_EPS, ALU.mult, ALU.add).then_inc(s[f"ln{n + 1}_ve"], 1)
                if n == 0:
                    dve.tensor_scalar(ve[n][:, 1, :], mv[n][:, :, 1], 1.0 + LN_EPS, LN_EPS * LN_EPS,
                                      ALU.mult, ALU.add).then_inc(s["ln1_ve"], 1)

            def normalise(dst, src, n, t, row, ready):
                dve.tensor_scalar(dst[:, t, :], src[:, t, :], mv[n][:, t, 0:1], rs[n][:, row, t:t + 1],
                                  ALU.subtract, ALU.mult).then_inc(s[ready], 1)

            def ln1_stats(g):
                if g is None:
                    return
                dve.wait_ge(s["x_loaded"], 16 * g + 16)
                for t in range(T):
                    stats(0, x_sb, t, None)
                if later(g, 1):
                    dve.wait_ge(s["n1_ready"], 4 * (g - 1) + 4)
                aggregate(0, g)

            def ln1_u(g):
                if g is None:
                    return
                dve.wait_ge(s["ln1_rs"], g + 1)
                if later(g, 1):
                    dve.wait_ge(s["tu_done"], 2 * (g - 1) + 2)
                for t in range(T):
                    normalise(u, x_sb, 0, t, 1, "u_ready")

            def n1(g):
                if g is None:
                    return
                if later(g, 1):
                    dve.wait_ge(s["xs_ready"], (g - 1) + 1)
                dve.wait_ge(s["ln1_rs"], g + 1)
                for t in range(T):
                    normalise(xa, x_sb, 0, t, 0, "n1_ready")

            def lo_part(dst, b, hi, ready):
                dve.tensor_tensor(dst, b, hi.bitcast(F32), ALU.subtract).then_inc(s[ready], 1)

            def u_lo(g, k):
                if g is None:
                    return
                dve.wait_ge(s["u_hi"], 2 * g + k + 1)
                lo_part(uT[1][:, k, :], bank[("x", "c")[k]][:], uT[0][:, k, :], "u_lo")

            def qk_mm(g, pj):
                if g is None:
                    return
                dve.wait_ge(s["qk_done"], g + 1)
                if pj is not None and later(pj, 1):
                    dve.wait_ge(s["out_stored"], 16 * pj)
                if later(g, 1):
                    dve.wait_ge(s["qk_lo_ready"], 2 * (g - 1) + 2)
                    dve.wait_ge(s["qk_hi_ready"], 3 * (g - 1) + 3)
                dve.tensor_scalar(qk_exp, bank["x"][:], qk_bias[:], 0.0, ALU.add, ALU.min).then_inc(s["qk_minmax"], 1)
                dve.tensor_scalar(qk, bank["x"][:], qk_bias[:], 0.0, ALU.add, ALU.max).then_inc(s["qk_minmax"], 1)

            def qk_l(g):
                if g is None:
                    return
                dve.wait_ge(s["qk_hi_ready"], 3 * g + 3)
                dve.tensor_tensor(q_stack[FQ:P, :], qk[0:FQ, :], q_stack[0:FQ, :].bitcast(F32),
                                  ALU.subtract).then_inc(s["qk_lo_ready"], 1)
                dve.tensor_tensor(k_lo[:], qk[FQ:P, :], k_stack[FQ:P, :].bitcast(F32),
                                  ALU.subtract).then_inc(s["qk_lo_ready"], 1)

            def v_sum(g, half):
                if g is None:
                    return
                dve.wait_ge(s["v_done"], 2 * g + half + 1)
                if half == 0 and isinstance(g, int) and g == 0:
                    dve.wait_ge(s["bvo_ready"], 1)
                    dve.wait_ge(s["bvo_done"], 1)
                if half or later(g, 1):
                    dve.wait_ge(s["v_hi_ready"], 2 * g + half)
                    dve.wait_ge(s["v_lo_ready"], 2 * g + half)
                for j in range(2):
                    mm = dve.tensor_tensor(v32[:, j, :], bank[("x", "c")[half]][:, j * D:(j + 1) * D], bvo_b[:], ALU.add)
                mm.then_inc(s["v_ready"], 1)

            def a_split(g, half):
                if g is None:
                    return
                tiles = ((0, "x", 0, 1), (1, "c", 0, 2), (2, "x", 0, 3), (3, "x", 3 * P, 3))[2 * half:2 * half + 2]
                for j, b, c0, n in tiles:
                    dve.wait_ge(s["s_done"], 3 * g + n)
                    if j == 0 and later(g, 1):
                        dve.wait_ge(s["av_done"], 4 * (g - 1) + 4)
                    dve.tensor_tensor(a[0][:, j, 0:P], bank[b][:, c0:c0 + P], mask[:],
                                      ALU.mult).then_inc(s["a_hi_diag"], 1)
                for j, b, c0, n in tiles:
                    w = N - j * P
                    dve.wait_ge(s["a_hi_diag"], 4 * g + j + 1)
                    if j < 3:
                        dve.wait_ge(s["a_hi_off"], 3 * g + j + 1)
                    lo_part(a[1][:, j, 0:w], bank[b][:, c0:c0 + w], a[0][:, j, 0:w], "a_lo_ready")

            def attn_out(g, t):
                if g is None:
                    return
                b = ("p0", "p1", "x", "p0")[t]
                dve.wait_ge(s["av_done"], 4 * g + t + 1)
                dve.tensor_scalar(den[:, t:t + 1], bank[b][:, D:D + 1], ATTN_EPS, None, ALU.add).then_inc(s["den_ready"], 1)
                dve.wait_ge(s["den_ready"], 4 * g + t + 1)
                dve.reciprocal(rden[:, t:t + 1], den[:, t:t + 1]).then_inc(s["rden_ready"], 1)
                dve.wait_ge(s["rden_ready"], 4 * g + t + 1)
                if t == 0:
                    dve.wait_ge(s["n1o_ready"], g + 1)
                dve.scalar_tensor_tensor(xa[:, t, :], bank[b][:, 0:D], rden[:, t:t + 1], xa[:, t, :],
                                         ALU.mult, ALU.add).then_inc(s["xa_ready"], 1)

            def ln2_part(g, t):
                if g is None:
                    return
                dve.wait_ge(s["xa_ready"], 4 * g + t + 1)
                stats(1, xa, t, None)

            def ln2_end(g):
                if g is None:
                    return
                if later(g, 1):
                    dve.wait_ge(s["z2_ready"], 4 * (g - 1) + 4)
                aggregate(1, g)

            def z2(g, fc):
                if g is None:
                    return
                dve.wait_ge(s["ln2_rs"], g + 1)
                if fc is not None:
                    dve.wait_ge(s["tz3_done"], 2 * fc + 2)
                elif later(g, 1):
                    dve.wait_ge(s["tz2_done"], 2 * (g - 1) + 2)
                for t in range(T):
                    normalise(z, xa, 1, t, 0, "z2_ready")

            def z2_lo(g, k):
                if g is None:
                    return
                dve.wait_ge(s["z2_hi"], 2 * g + k + 1)
                lo_part(z2T[1][:, k, :], bank[("x", "p1")[k]][:], z2T[0][:, k, :], "z2_lo")

            def h_lo(g, m):
                if g is None:
                    return
                dve.wait_ge(s["h_hi_ready"], 8 * g + m + 1)
                if later(g, 1) or m >= 3:
                    dve.wait_ge(s["f2_step"], 8 * g + (m - 2 if m >= 3 else 0))
                dve.tensor_tensor(hr[1][:, m % 3, :], hring[:, m % 3, :], hr[0][:, m % 3, :].bitcast(F32),
                                  ALU.subtract).then_inc(s["h_lo_odd"], 1)

            def y_sum(g, h):
                if g is None:
                    return
                if h == 0:
                    dve.wait_ge(s["f2_step"], 8 * g + 8)
                    dve.wait_ge(s["xs_ready"], g + 1)
                    if later(g, 1):
                        dve.wait_ge(s["yc_ready"], (g - 1) + 1)
                dve.tensor_tensor(y[:, 2 * h:2 * h + 2, :].rearrange("p t d -> p (t d)"), bank[("y0", "y1")[h]][:],
                                  xs[:, 2 * h:2 * h + 2, :].rearrange("p t d -> p (t d)"), ALU.add).then_inc(s["y_ready"], 1)

            def ln3_part(g, h):
                if g is None:
                    return
                dve.wait_ge(s["y_ready"], 2 * g + h + 1)
                for t in (2 * h, 2 * h + 1):
                    stats(2, y, t, None)

            def ln3_end(g):
                if g is None:
                    return
                if later(g, 1):
                    dve.wait_ge(s["z3_ready"], 4 * (g - 1) + 4)
                aggregate(2, g)

            def z3(g):
                if g is None:
                    return
                dve.wait_ge(s["ln3_rs"], g + 1)
                dve.wait_ge(s["tz2_done"], 2 * min(g + 1, G - 1) + 2 if isinstance(g, int) else 2 * (g + 1) + 2)
                if isinstance(g, int) and g == G - 1:
                    dve.wait_ge(s["tz3_done"], 2 * (g - 1) + 2)
                for t in range(T):
                    normalise(z, y, 2, t, 0, "z3_ready")

            def z3_lo(g, k):
                if g is None:
                    return
                dve.wait_ge(s["z3_hi"], 2 * g + k + 1)
                lo_part(z3T[1][:, k, :], bank[("x", "c")[k]][:], z3T[0][:, k, :], "z3_lo")

            def g_lo(g, m):
                if g is None:
                    return
                dve.wait_ge(s["g_hi_ready"], 8 * g + m + 1)
                if later(g, 1) or m >= 2:
                    dve.wait_ge(s["pj_step"], 8 * g + (m - 1 if m >= 2 else 0))
                dve.wait_ge(s["h3_gelu"], 8 * g + m + 1)
                dve.scalar_tensor_tensor(gr[1][:, m % 2, :], h3[:, m, :], ln3w_c[:, m:m + 1],
                                         gr[0][:, m % 2, :].bitcast(F32), ALU.mult, ALU.subtract).then_inc(s["g_lo_ready"], 1)

            def hsum_last(g, m):
                dve.wait_ge(s["h3_gelu"], 8 * g + m + 1)
                if m == 1:
                    dve.wait_ge(s["var_done"], 8 * (g - 1) + 8)
                    dve.tensor_tensor(hsum, h3[:, 0, :], h3[:, 1, :], ALU.add).then_inc(s["hsum_last"], 1)
                else:
                    dve.wait_ge(s["hsum_last"], m - 1)
                    dve.tensor_tensor(hsum, hsum, h3[:, m, :], ALU.add).then_inc(s["hsum_last"], 1)

            def var_eps(g):
                if g is None:
                    return
                b = moment_bank(g)
                dve.wait_ge(s["var_done"], 8 * g + 8)
                if later(g, 1):
                    dve.wait_ge(s["rs3_ready"], (g - 1) + 1)
                dve.tensor_scalar(neg_mu[:], b[:, T:2 * T], -1.0, None, ALU.mult).then_inc(s["moments"], 1)
                dve.wait_ge(s["moments"], 3 * g + 1)
                dve.tensor_tensor(mu_sq[:], neg_mu[:], neg_mu[:], ALU.mult).then_inc(s["moments"], 1)
                dve.wait_ge(s["moments"], 3 * g + 2)
                dve.tensor_tensor(var_raw[:], b[:, 0:T], mu_sq[:], ALU.subtract).then_inc(s["moments"], 1)
                dve.wait_ge(s["moments"], 3 * g + 3)
                dve.tensor_scalar(ve[3][:, 0, :], var_raw[:], 0.0, LN_EPS, ALU.max, ALU.add).then_inc(s["var_ready"], 1)

            def correct(g):
                if g is None:
                    return
                dve.wait_ge(s["rs3_ready"], g + 1)
                dve.tensor_tensor(neg_mu_rs[:], neg_mu[:], rs[3][:, 0, :], ALU.mult).then_inc(s["scale_ready"], 1)
                dve.wait_ge(s["scale_ready"], g + 1)
                dve.wait_ge(s["yc_ready"], g + 1)
                for t in range(T):
                    dve.scalar_tensor_tensor(yc[:, t, :], csum_b, neg_mu_rs[:, t:t + 1], yc[:, t, :],
                                             ALU.mult, ALU.add).then_inc(s["corrected"], 1)

            def output(g, at):
                if g is None:
                    return
                dve.wait_ge(s["pj_step"], 8 * g + 8)
                dve.wait_ge(s["corrected"], 4 * g + 4)
                if at is not None:
                    dve.wait_ge(s["qk_lo_ready"], 2 * at + 2)
                elif later(g, 1):
                    dve.wait_ge(s["out_stored"], 16 * g)
                for t in range(T):
                    dve.scalar_tensor_tensor(out_sb[:, t, :], bank[("p0", "p1")[t // 2]][:, (t % 2) * D:(t % 2 + 1) * D],
                                             rs[3][:, 0, t:t + 1], yc[:, t, :], ALU.mult, ALU.add).then_inc(s["out_ready"], 1)

            def first():
                consts(); ln1_stats(0); prep_vec(); ln1_u(0); prep_dots(); prep_late_vec(); n1(0); u_lo(0, 0)
                u_lo(0, 1); prep_wqk(); prep_wvo(); qk_mm(0, None); v_sum(0, 0); qk_l(0); v_sum(0, 1)
                a_split(0, 0); a_split(0, 1); ln1_stats(1); attn_out(0, 0); attn_out(0, 1); ln2_part(0, 0)
                attn_out(0, 2); attn_out(0, 3); ln2_part(0, 1); ln2_part(0, 2); ln2_part(0, 3); ln2_end(0)
                z2(0, None); ln1_u(1); z2_lo(0, 0); z2_lo(0, 1); prep_f1_bias(); u_lo(1, 0); u_lo(1, 1)
                prep_theta(); prep_tern(0); qk_mm(1, None); n1(1); prep_tern(1); v_sum(1, 0); qk_l(1)
                prep_select(); prep_ln3(); v_sum(1, 1); h_lo(0, 1); a_split(1, 0); ln1_stats(2); h_lo(0, 3)
                a_split(1, 1); h_lo(0, 5); attn_out(1, 0); attn_out(1, 1); ln2_part(1, 0); attn_out(1, 2)
                ln2_part(1, 1); attn_out(1, 3); ln2_part(1, 2); ln2_part(1, 3); ln2_end(1); ln1_u(2)
                z2(1, None); h_lo(0, 7); z2_lo(1, 0); z2_lo(1, 1)

            def step(i):
                at, ml, fc, pj = groups(i)
                nx = following(i)
                y_sum(fc, 0); g_lo(pj, 0); g_lo(pj, 1); u_lo(at, 0); u_lo(at, 1); y_sum(fc, 1); ln3_part(fc, 0)
                ln3_part(fc, 1); ln3_end(fc); qk_mm(at, pj); g_lo(pj, 2); z3(fc); h_lo(ml, 1); z3_lo(fc, 0)
                g_lo(pj, 3); z3_lo(fc, 1); v_sum(at, 0); n1(at); g_lo(pj, 4); qk_l(at); v_sum(at, 1)
                a_split(at, 0); g_lo(pj, 5); h_lo(ml, 3); ln1_stats(nx); g_lo(pj, 6); g_lo(pj, 7)
                a_split(at, 1); var_eps(pj); correct(pj); output(pj, at); h_lo(ml, 5); attn_out(at, 0)
                ln2_part(at, 0); ln1_u(nx); attn_out(at, 1); ln2_part(at, 1); attn_out(at, 2); attn_out(at, 3)
                ln2_part(at, 2); ln2_part(at, 3); ln2_end(at); h_lo(ml, 7); z2(at, fc); z2_lo(at, 0)
                z2_lo(at, 1)

            def last():
                y_sum(G - 2, 0); ln3_part(G - 2, 0); g_lo(G - 3, 0); y_sum(G - 2, 1); ln3_part(G - 2, 1)
                ln3_end(G - 2); g_lo(G - 3, 1); z3(G - 2); g_lo(G - 3, 2); z3_lo(G - 2, 0); z3_lo(G - 2, 1)
                h_lo(G - 1, 1); g_lo(G - 3, 3); g_lo(G - 3, 4); g_lo(G - 3, 5); h_lo(G - 1, 3); g_lo(G - 3, 6)
                var_eps(G - 3); g_lo(G - 3, 7); correct(G - 3); h_lo(G - 1, 5); output(G - 3, None)
                g_lo(G - 2, 0); h_lo(G - 1, 7); g_lo(G - 2, 1); y_sum(G - 1, 0); y_sum(G - 1, 1)
                ln3_part(G - 1, 0); ln3_part(G - 1, 1); ln3_end(G - 1); g_lo(G - 2, 2); g_lo(G - 2, 3)
                z3(G - 1); g_lo(G - 2, 4); g_lo(G - 2, 5); z3_lo(G - 1, 0); z3_lo(G - 1, 1); g_lo(G - 2, 6)
                g_lo(G - 2, 7); var_eps(G - 2); hsum_last(G - 1, 1); hsum_last(G - 1, 2); correct(G - 2)
                g_lo(G - 1, 0); output(G - 2, None); g_lo(G - 1, 1); hsum_last(G - 1, 3); hsum_last(G - 1, 4)
                g_lo(G - 1, 2); hsum_last(G - 1, 5); g_lo(G - 1, 3); hsum_last(G - 1, 6); hsum_last(G - 1, 7)
                g_lo(G - 1, 4); g_lo(G - 1, 5); var_eps(G - 1); g_lo(G - 1, 6); g_lo(G - 1, 7); correct(G - 1)
                output(G - 1, None)

            steps(dve, first, step, last)

        @block.gpsimd
        def _(pool):
            def consts():
                pool.memset(ident[:], 0.0).then_inc(s["consts_memset"], 1)
                pool.memset(mask[:], 1.0).then_inc(s["consts_memset"], 1)
                pool.wait_ge(s["consts_memset"], 2)
                pool.affine_select(out=ident[:], in_=ident[:], compare_op=ALU.not_equal, fill=1.0, base=0,
                                   pattern=[[-1, P]], channel_multiplier=1).then_inc(s["consts_ready"], 1)
                pool.affine_select(out=mask[:], in_=mask[:], compare_op=ALU.is_ge, fill=0.0, base=0,
                                   pattern=[[1, P]], channel_multiplier=-1).then_inc(s["consts_ready"], 1)

            def prep_w(n):
                if n < 4:
                    k, half = n // 2, n % 2
                    hi, lo = [w[:, k, half * 512:(half + 1) * 512] for w in wf1]
                    pool.wait_ge(s["wf1_staged"], n + 1)
                else:
                    hi, lo = [w[:, 2 * n - 8:2 * n - 6, :].rearrange("p k d -> p (k d)") for w in wf2]
                    pool.wait_ge(s["wf2_staged"], n - 3)
                pool.tensor_tensor(lo, hring[:, n % 3, :], hi.bitcast(F32), ALU.subtract).then_inc(s["w_lo_ready"], 1)

            def prep_f1_bias():
                pool.wait_ge(s["f1T_done"], 4)
                pool.wait_ge(s["ln2b_loaded"], 16)
                pool.tensor_tensor(f1_raw, f1_raw, ln2b_b.unsqueeze(1).to_broadcast([P, KH, D]),
                                   ALU.mult).then_inc(s["f1_scaled"], 1)

            def rstd(n, g, two):
                if g is None:
                    return
                ve_s, rs_s = s[f"ln{n + 1}_ve"], s[f"ln{n + 1}_rs"]
                c = 2 if two else 1
                if later(g, 1):
                    pool.wait_ge(s[("u_ready", "z2_ready", "z3_ready")[n]], 4 * (g - 1) + 4)
                    if two:
                        pool.wait_ge(s["n1_ready"], 4 * (g - 1) + 4)
                pool.wait_ge(ve_s, c * g + c)
                pool.tensor_tensor(rs[n][:, 0:c, :].rearrange("p c t -> p (c t)"),
                                   ve[n][:, 0:c, :].rearrange("p c t -> p (c t)"),
                                   neg_half[:, 0:c * T], ALU.pow).then_inc(rs_s, 1)

            def n1o(g):
                if g is None:
                    return
                pool.wait_ge(s["n1_ready"], 4 * g + 4)
                if isinstance(g, int) and g == 0:
                    pool.wait_ge(s["ob_loaded"], 32)
                pool.tensor_tensor(xa[:], xa[:], ob_b[:].unsqueeze(1).to_broadcast([P, T, D]),
                                   ALU.add).then_inc(s["n1o_ready"], 1)

            def xpb_(g):
                if g is None:
                    return
                if isinstance(g, int) and g == 0:
                    pool.wait_ge(s["x_loaded"], 16)
                    pool.wait_ge(s["ob_loaded"], 32)
                if later(g, 1):
                    pool.wait_ge(s["xs_ready"], (g - 1) + 1)
                pool.tensor_tensor(xpb[:], x_sb[:], f2b_b[:].unsqueeze(1).to_broadcast([P, T, D]),
                                   ALU.add).then_inc(s["xpb_ready"], 1)

            def xs_(g):
                if g is None:
                    return
                pool.wait_ge(s["xa_ready"], 4 * g + 4)
                pool.wait_ge(s["xpb_ready"], g + 1)
                if later(g, 1):
                    pool.wait_ge(s["y_ready"], 2 * (g - 1) + 2)
                else:
                    pool.wait_ge(s["bias_done"], 3)
                    pool.wait_ge(s["bvo_done"], 1)
                pool.tensor_tensor(xs[:], xpb[:], xa[:], ALU.add).then_inc(s["xs_ready"], 1)

            def qk_sum(g):
                if g is None:
                    return
                pool.wait_ge(s["qk_exp_ready"], g + 1)
                pool.wait_ge(s["qk_minmax"], 2 * g + 2)
                pool.tensor_tensor(qk, qk_exp, qk, ALU.add).then_inc(s["qk_ready"], 1)

            def v_lo(g, half):
                if g is None:
                    return
                pool.wait_ge(s["v_hi_ready"], 2 * g + half + 1)
                pool.wait_ge(s["v_ready"], 2 * g + half + 1)
                if half == 0 and later(g, 1):
                    pool.wait_ge(s["av_done"], 4 * (g - 1) + 4)
                pool.tensor_tensor(v[1][:, 2 * half:2 * half + 2, 0:D], v32[:],
                                   v[0][:, 2 * half:2 * half + 2, 0:D].bitcast(F32), ALU.subtract).then_inc(s["v_lo_ready"], 1)

            def a_mask(g):
                if g is None:
                    return
                pool.wait_ge(s["a_lo_ready"], 4 * g + 4)
                pool.tensor_tensor(a[1][:, :, 0:P], a[1][:, :, 0:P].bitcast(F32), mask[:].unsqueeze(1).to_broadcast([P, T, P]),
                                   ALU.mult).then_inc(s["a_lo_masked"], 1)

            def h_lo(g, m):
                if g is None:
                    return
                pool.wait_ge(s["h_hi_ready"], 8 * g + m + 1)
                if later(g, 1) or m >= 3:
                    pool.wait_ge(s["f2_step"], 8 * g + (m - 2 if m >= 3 else 0))
                pool.tensor_tensor(hr[1][:, m % 3, :], hring[:, m % 3, :], hr[0][:, m % 3, :].bitcast(F32),
                                   ALU.subtract).then_inc(s["h_lo_even"], 1)

            def hsum_step(g, m):
                if g is None:
                    return
                pool.wait_ge(s["h3_gelu"], 8 * g + m + 1)
                if m == 1:
                    if later(g, 1):
                        pool.wait_ge(s["var_done"], 8 * (g - 1) + 8)
                    pool.tensor_tensor(hsum, h3[:, 0, :], h3[:, 1, :], ALU.add).then_inc(s["hsum_step"], 1)
                else:
                    pool.wait_ge(s["hsum_step"], 7 * g + m - 1)
                    pool.tensor_tensor(hsum, hsum, h3[:, m, :], ALU.add).then_inc(s["hsum_step"], 1)

            def sqsum_step(g, m):
                if g is None:
                    return
                pool.wait_ge(s["sq_ready"], 8 * g + m + 1)
                if m == 1:
                    if later(g, 1):
                        pool.wait_ge(s["var_done"], 8 * (g - 1) + 8)
                    pool.tensor_tensor(sqsum, sq[:, 0, :], sq[:, 1, :], ALU.add).then_inc(s["sqsum_step"], 1)
                else:
                    pool.wait_ge(s["sqsum_step"], 7 * g + m - 1)
                    pool.tensor_tensor(sqsum, sqsum, sq[:, m % 2, :], ALU.add).then_inc(s["sqsum_step"], 1)

            def rstd3(g):
                if g is None:
                    return
                pool.wait_ge(s["var_ready"], g + 1)
                if later(g, 1):
                    pool.wait_ge(s["out_ready"], 4 * (g - 1) + 4)
                pool.tensor_tensor(rs[3][:, 0, :], ve[3][:, 0, :], neg_half[:, 0:T], ALU.pow).then_inc(s["rs3_ready"], 1)

            def yc_(g):
                if g is None:
                    return
                pool.wait_ge(s["y_ready"], 2 * g + 2)
                if later(g, 1):
                    pool.wait_ge(s["out_ready"], 4 * (g - 1) + 4)
                pool.tensor_tensor(yc, y, cpj_b.unsqueeze(1).to_broadcast([P, T, D]),
                                   ALU.add).then_inc(s["yc_ready"], 1)

            def first():
                consts(); rstd(0, 0, True); xpb_(0); qk_sum(0); prep_w(0); v_lo(0, 0); n1o(0); prep_w(1)
                v_lo(0, 1); a_mask(0); prep_f1_bias(); prep_w(2); prep_w(3); prep_w(4); rstd(1, 0, False)
                rstd(0, 1, True); prep_w(5); prep_w(6); prep_w(7); xs_(0); xpb_(1); qk_sum(1); h_lo(0, 0)
                n1o(1); v_lo(1, 0); h_lo(0, 2); v_lo(1, 1); a_mask(1); h_lo(0, 4); rstd(0, 2, True); h_lo(0, 6)
                rstd(1, 1, False)

            def step(i):
                at, ml, fc, pj = groups(i)
                nx = following(i)
                sqsum_step(pj, 1); sqsum_step(pj, 2); h_lo(ml, 0); rstd(2, fc, False); xs_(ml)
                sqsum_step(pj, 3); qk_sum(at); xpb_(at); sqsum_step(pj, 4); v_lo(at, 0); h_lo(ml, 2)
                sqsum_step(pj, 5); v_lo(at, 1); sqsum_step(pj, 6); sqsum_step(pj, 7); n1o(at); h_lo(ml, 4)
                rstd3(pj); a_mask(at); rstd(0, nx, True); hsum_step(fc, 1); hsum_step(fc, 2); hsum_step(fc, 3)
                h_lo(ml, 6); yc_(fc); rstd(1, at, False); hsum_step(fc, 4); hsum_step(fc, 5); hsum_step(fc, 6)
                hsum_step(fc, 7)

            def last():
                sqsum_step(G - 3, 1); h_lo(G - 1, 0); rstd(2, G - 2, False); sqsum_step(G - 3, 2)
                sqsum_step(G - 3, 3); sqsum_step(G - 3, 4); xs_(G - 1); sqsum_step(G - 3, 5)
                sqsum_step(G - 3, 6); sqsum_step(G - 3, 7); h_lo(G - 1, 2); rstd3(G - 3); h_lo(G - 1, 4)
                hsum_step(G - 2, 1); sqsum_step(G - 2, 1); hsum_step(G - 2, 2); h_lo(G - 1, 6)
                sqsum_step(G - 2, 2); yc_(G - 2); hsum_step(G - 2, 3); sqsum_step(G - 2, 3)
                sqsum_step(G - 2, 4); hsum_step(G - 2, 4); hsum_step(G - 2, 5); rstd(2, G - 1, False)
                sqsum_step(G - 2, 5); hsum_step(G - 2, 6); hsum_step(G - 2, 7); sqsum_step(G - 2, 6)
                sqsum_step(G - 2, 7); rstd3(G - 2); sqsum_step(G - 1, 1); sqsum_step(G - 1, 2)
                sqsum_step(G - 1, 3); sqsum_step(G - 1, 4); sqsum_step(G - 1, 5); sqsum_step(G - 1, 6)
                sqsum_step(G - 1, 7); yc_(G - 1); rstd3(G - 1)

            steps(pool, first, step, last)


_INS = ["L0_attn_x", "L0_attn_ln1_w", "L0_attn_ln1_b", "L0_attn_q_w", "L0_attn_q_b", "L0_attn_k_w", "L0_attn_k_b",
        "L0_attn_v_w", "L0_attn_v_b", "L0_attn_o_w", "L0_attn_o_b", "L0_attn_ln2_w", "L0_attn_ln2_b", "L0_attn_f1_w",
        "L0_attn_f1_b", "L0_attn_f2_w", "L0_attn_f2_b", "L0_ffn_W_fc", "L0_ffn_ln_w", "L0_ffn_ln_b", "L0_ffn_W_proj"]


def kernel(**inputs):
    import numpy as _np
    import concourse.bacc as _bacc
    from concourse import mybir as _mybir
    from concourse.bass_utils import run_bass_kernel_spmd as _run

    nc = _bacc.Bacc("TRN2", target_bir_lowering=False, num_devices=1)
    arrays, args = {}, []
    for name in _INS:
        a = _np.ascontiguousarray(inputs[name])
        arrays[f"in_{name}"] = a
        args.append(nc.dram_tensor(f"in_{name}", a.shape, _mybir.dt.from_np(a.dtype), kind="ExternalInput").ap())
    args.append(nc.dram_tensor("out", inputs["L0_attn_x"].shape, _mybir.dt.float32, kind="ExternalOutput").ap())
    build(nc, *args)
    r = _run(nc, [arrays], core_ids=[0])
    return r.results[0]["out"]
```
